# Optimizing a Trainium2 kernel written in Bass

```python
import numpy as np
import jax
import jax.numpy as jnp

def _softmax(x, axis=-1):
    return jax.nn.softmax(x, axis=axis)

def _gelu(x):
    return jax.nn.gelu(x, approximate=True)

def _silu(x):
    return jax.nn.silu(x)

def _sigmoid(x):
    return jax.nn.sigmoid(x)

def _layernorm(x, axis=-1, eps=1e-05):
    m = jnp.mean(x, axis=axis, keepdims=True)
    v = jnp.var(x, axis=axis, keepdims=True)
    return (x - m) / jnp.sqrt(v + eps)

def _scatter_add(tgt, idx, src, axis=0):
    return tgt.at[idx].add(src)

def _segment_sum(src, seg, n):
    return jax.ops.segment_sum(src, seg, n)
kernel_name = 'mk_prb_d2_jaxref_r4_23fa80'

def setup_inputs(seed: int=0):
    np.random.seed(seed)
    _w = jnp.asarray

    def _L0_attn_setup():
        import math
        import jax, jax.numpy as jnp
        import numpy as np
        N_HEADS = 16
        THETA = 10000.0

        def _rope_cos_sin(S, head_dim):
            half = head_dim // 2
            inv_freq = 1.0 / THETA ** (jnp.arange(half, dtype=jnp.float32) / half)
            t = jnp.arange(S, dtype=jnp.float32)
            freqs = t[:, None] * inv_freq[None, :]
            return (jnp.cos(freqs), jnp.sin(freqs))

        def _apply_rope(x, cos, sin):
            half = x.shape[-1] // 2
            x1, x2 = (x[..., :half], x[..., half:])
            c = cos[None, None, :, :]
            s = sin[None, None, :, :]
            return jnp.concatenate([x1 * c - x2 * s, x1 * s + x2 * c], axis=-1)
        key = jax.random.key(seed)
        k1, k2, k3 = jax.random.split(key, 3)
        B, S, D = (4, 512, 256)
        x = jax.random.normal(k1, (B, S, D), dtype=jnp.float32)
        w_qkv = jax.random.normal(k2, (3 * D, D), dtype=jnp.float32) * (1.0 / math.sqrt(D))
        w_out = jax.random.normal(k3, (D, D), dtype=jnp.float32) * (1.0 / math.sqrt(D))
        return {'x': x, 'w_qkv': w_qkv, 'w_out': w_out}
    _L0_attn_in = _L0_attn_setup()

    def _L0_ffn_setup():
        import jax, jax.numpy as jnp
        import numpy as np
        D_MODEL = 256
        N_HEADS = 16
        HEAD_DIM = D_MODEL // N_HEADS
        KV_LATENT = 128
        N_EXPERTS = 4
        D_HIDDEN = 4 * D_MODEL
        B, T = (2, 256)

        def rmsnorm(x, w, eps=1e-06):
            return w * (x * jax.lax.rsqrt(jnp.mean(x * x, axis=-1, keepdims=True) + eps))

        def layernorm(x, g, b, eps=1e-05):
            mu = jnp.mean(x, axis=-1, keepdims=True)
            var = jnp.mean((x - mu) ** 2, axis=-1, keepdims=True)
            return (x - mu) * jax.lax.rsqrt(var + eps) * g + b

        def apply_rope(x):
            t, d = (x.shape[2], x.shape[3])
            half = d // 2
            pos = jnp.arange(t, dtype=x.dtype)[:, None]
            inv_freq = 1.0 / 10000.0 ** (jnp.arange(half, dtype=x.dtype) / half)
            ang = pos * inv_freq[None, :]
            sin, cos = (jnp.sin(ang), jnp.cos(ang))
            x1, x2 = (x[..., :half], x[..., half:])
            return jnp.concatenate([x1 * cos - x2 * sin, x1 * sin + x2 * cos], axis=-1)

        def mla_attention(x, Wq, Wdkv, Wuk, Wuv, Wo, ln_g, ln_b):
            b, t, _ = x.shape
            q = (x @ Wq.T).reshape(b, t, N_HEADS, HEAD_DIM).transpose(0, 2, 1, 3)
            latent = layernorm(x @ Wdkv.T, ln_g, ln_b)
            k = (latent @ Wuk.T).reshape(b, t, N_HEADS, HEAD_DIM).transpose(0, 2, 1, 3)
            v = (latent @ Wuv.T).reshape(b, t, N_HEADS, HEAD_DIM).transpose(0, 2, 1, 3)
            q = apply_rope(q)
            k = apply_rope(k)
            scores = jnp.einsum('bhqd,bhkd->bhqk', q, k) / np.sqrt(HEAD_DIM)
            causal = jnp.tril(jnp.ones((t, t), dtype=bool))
            scores = jnp.where(causal, scores, -jnp.inf)
            attn = jax.nn.softmax(scores, axis=-1)
            out = jnp.einsum('bhqk,bhkd->bhqd', attn, v).transpose(0, 2, 1, 3).reshape(b, t, D_MODEL)
            return out @ Wo.T

        def moe(x, gate_w, gate_b, W1, b1, W2, b2):
            logits = x @ gate_w.T + gate_b
            top = jnp.argmax(logits, axis=-1)
            onehot = jax.nn.one_hot(top, N_EXPERTS, dtype=x.dtype)
            h = jax.nn.relu(jnp.einsum('btd,ehd->bteh', x, W1) + b1)
            y = jnp.einsum('bteh,edh->bted', h, W2) + b2
            return jnp.einsum('bted,bte->btd', y, onehot)
        key = jax.random.key(seed)
        ks = jax.random.split(key, 16)
        s = lambda fan_in: 1.0 / np.sqrt(fan_in)
        return {'x': jax.random.normal(ks[0], (B, T, D_MODEL), jnp.float32), 'norm1_w': jnp.ones((D_MODEL,), jnp.float32), 'norm2_w': jnp.ones((D_MODEL,), jnp.float32), 'Wq': jax.random.normal(ks[1], (D_MODEL, D_MODEL), jnp.float32) * s(D_MODEL), 'Wdkv': jax.random.normal(ks[2], (KV_LATENT, D_MODEL), jnp.float32) * s(D_MODEL), 'Wuk': jax.random.normal(ks[3], (D_MODEL, KV_LATENT), jnp.float32) * s(KV_LATENT), 'Wuv': jax.random.normal(ks[4], (D_MODEL, KV_LATENT), jnp.float32) * s(KV_LATENT), 'Wo': jax.random.normal(ks[5], (D_MODEL, D_MODEL), jnp.float32) * s(D_MODEL), 'ln_g': jnp.ones((KV_LATENT,), jnp.float32), 'ln_b': jnp.zeros((KV_LATENT,), jnp.float32), 'gate_w': jax.random.normal(ks[6], (N_EXPERTS, D_MODEL), jnp.float32) * s(D_MODEL), 'gate_b': jnp.zeros((N_EXPERTS,), jnp.float32), 'W1': jax.random.normal(ks[7], (N_EXPERTS, D_HIDDEN, D_MODEL), jnp.float32) * s(D_MODEL), 'b1': jnp.zeros((N_EXPERTS, D_HIDDEN), jnp.float32), 'W2': jax.random.normal(ks[8], (N_EXPERTS, D_MODEL, D_HIDDEN), jnp.float32) * s(D_HIDDEN), 'b2': jnp.zeros((N_EXPERTS, D_MODEL), jnp.float32)}
    _L0_ffn_in = _L0_ffn_setup()

    def _L1_attn_setup():
        import jax, jax.numpy as jnp
        import numpy as np
        D_INNER = 256
        STATE = 16
        DT_RANK = 64

        def _combine(carry, nxt):
            a1, b1 = carry
            a2, b2 = nxt
            return (a1 * a2, a2 * b1 + b2)
        key = jax.random.key(seed)
        k_u, k_x, k_dt, k_b = jax.random.split(key, 4)
        u = jax.random.normal(k_u, (2, 512, D_INNER), dtype=jnp.float32)
        A_log = jnp.broadcast_to(jnp.log(jnp.arange(1, STATE + 1, dtype=jnp.float32))[None, :], (D_INNER, STATE))
        W_x = jax.random.normal(k_x, (DT_RANK + 2 * STATE, D_INNER), dtype=jnp.float32) * 0.02
        W_dt = jax.random.normal(k_dt, (D_INNER, DT_RANK), dtype=jnp.float32) * 0.02
        dt_init = jnp.exp(jax.random.uniform(k_b, (D_INNER,), dtype=jnp.float32) * (np.log(0.1) - np.log(0.001)) + np.log(0.001))
        b_dt = dt_init + jnp.log(-jnp.expm1(-dt_init))
        D_param = jnp.ones((D_INNER,), dtype=jnp.float32)
        return {'u': u, 'A_log': A_log, 'W_x': W_x, 'W_dt': W_dt, 'b_dt': b_dt, 'D_param': D_param}
    _L1_attn_in = _L1_attn_setup()

    def _L1_ffn_setup():
        import jax, jax.numpy as jnp
        import numpy as np
        NUM_EXPERTS = 8
        TOP_K = 2
        D = 256
        H = 4 * D
        B, S = (4, 512)
        key = jax.random.key(seed)
        ks = jax.random.split(key, 8)
        s = 0.02
        return {'x': jax.random.normal(ks[0], (B, S, D), dtype=jnp.float32), 'gate_w': jax.random.normal(ks[1], (NUM_EXPERTS, D), dtype=jnp.float32) * s, 'gate_b': jnp.zeros((NUM_EXPERTS,), dtype=jnp.float32), 'w1': jax.random.normal(ks[2], (NUM_EXPERTS, D, H), dtype=jnp.float32) * s, 'b1': jnp.zeros((NUM_EXPERTS, H), dtype=jnp.float32), 'w2': jax.random.normal(ks[3], (NUM_EXPERTS, H, D), dtype=jnp.float32) * s, 'b2': jnp.zeros((NUM_EXPERTS, D), dtype=jnp.float32)}
    _L1_ffn_in = _L1_ffn_setup()
    _d = {'L0_attn_x': _L0_attn_in['x'], 'L0_attn_w_qkv': _L0_attn_in['w_qkv'], 'L0_attn_w_out': _L0_attn_in['w_out'], 'L0_ffn_norm1_w': _L0_ffn_in['norm1_w'], 'L0_ffn_norm2_w': _L0_ffn_in['norm2_w'], 'L0_ffn_Wq': _L0_ffn_in['Wq'], 'L0_ffn_Wdkv': _L0_ffn_in['Wdkv'], 'L0_ffn_Wuk': _L0_ffn_in['Wuk'], 'L0_ffn_Wuv': _L0_ffn_in['Wuv'], 'L0_ffn_Wo': _L0_ffn_in['Wo'], 'L0_ffn_ln_g': _L0_ffn_in['ln_g'], 'L0_ffn_ln_b': _L0_ffn_in['ln_b'], 'L0_ffn_gate_w': _L0_ffn_in['gate_w'], 'L0_ffn_gate_b': _L0_ffn_in['gate_b'], 'L0_ffn_W1': _L0_ffn_in['W1'], 'L0_ffn_b1': _L0_ffn_in['b1'], 'L0_ffn_W2': _L0_ffn_in['W2'], 'L0_ffn_b2': _L0_ffn_in['b2'], 'L1_attn_A_log': _L1_attn_in['A_log'], 'L1_attn_W_x': _L1_attn_in['W_x'], 'L1_attn_W_dt': _L1_attn_in['W_dt'], 'L1_attn_b_dt': _L1_attn_in['b_dt'], 'L1_attn_D_param': _L1_attn_in['D_param'], 'L1_ffn_gate_w': _L1_ffn_in['gate_w'], 'L1_ffn_gate_b': _L1_ffn_in['gate_b'], 'L1_ffn_w1': _L1_ffn_in['w1'], 'L1_ffn_b1': _L1_ffn_in['b1'], 'L1_ffn_w2': _L1_ffn_in['w2'], 'L1_ffn_b2': _L1_ffn_in['b2']}
    _x0 = _d['L0_attn_x']
    _d['L0_attn_x'] = jax.random.normal(jax.random.fold_in(jax.random.key(seed), 1), (4, 1024, 256), dtype=_x0.dtype)
    del _x0
    return _d

def reference(L0_attn_x, L0_attn_w_qkv, L0_attn_w_out, L0_ffn_norm1_w, L0_ffn_norm2_w, L0_ffn_Wq, L0_ffn_Wdkv, L0_ffn_Wuk, L0_ffn_Wuv, L0_ffn_Wo, L0_ffn_ln_g, L0_ffn_ln_b, L0_ffn_gate_w, L0_ffn_gate_b, L0_ffn_W1, L0_ffn_b1, L0_ffn_W2, L0_ffn_b2, L1_attn_A_log, L1_attn_W_x, L1_attn_W_dt, L1_attn_b_dt, L1_attn_D_param, L1_ffn_gate_w, L1_ffn_gate_b, L1_ffn_w1, L1_ffn_b1, L1_ffn_w2, L1_ffn_b2):

    def _L0_attn_ref(x, w_qkv, w_out):
        import math
        import jax, jax.numpy as jnp
        import numpy as np
        N_HEADS = 16
        THETA = 10000.0

        def _rope_cos_sin(S, head_dim):
            half = head_dim // 2
            inv_freq = 1.0 / THETA ** (jnp.arange(half, dtype=jnp.float32) / half)
            t = jnp.arange(S, dtype=jnp.float32)
            freqs = t[:, None] * inv_freq[None, :]
            return (jnp.cos(freqs), jnp.sin(freqs))

        def _apply_rope(x, cos, sin):
            half = x.shape[-1] // 2
            x1, x2 = (x[..., :half], x[..., half:])
            c = cos[None, None, :, :]
            s = sin[None, None, :, :]
            return jnp.concatenate([x1 * c - x2 * s, x1 * s + x2 * c], axis=-1)
        B, S, D = x.shape
        H = N_HEADS
        hd = D // H
        qkv = x @ w_qkv.T
        q, k, v = jnp.split(qkv, 3, axis=-1)

        def reshape(t):
            return t.reshape(B, S, H, hd).transpose(0, 2, 1, 3)
        q, k, v = (reshape(q), reshape(k), reshape(v))
        cos, sin = _rope_cos_sin(S, hd)
        q = _apply_rope(q.astype(jnp.float32), cos, sin).astype(x.dtype)
        k = _apply_rope(k.astype(jnp.float32), cos, sin).astype(x.dtype)
        scale = math.sqrt(hd)
        scores = jnp.einsum('bhsd,bhtd->bhst', q, k) / scale
        causal = jnp.tril(jnp.ones((S, S), dtype=bool))
        scores = jnp.where(causal[None, None], scores, -jnp.inf)
        attn = jax.nn.softmax(scores.astype(jnp.float32), axis=-1).astype(x.dtype)
        out = jnp.einsum('bhst,bhtd->bhsd', attn, v)
        out = out.transpose(0, 2, 1, 3).reshape(B, S, D)
        return out @ w_out.T

    def _L0_ffn_ref(x, norm1_w, norm2_w, Wq, Wdkv, Wuk, Wuv, Wo, ln_g, ln_b, gate_w, gate_b, W1, b1, W2, b2):
        import jax, jax.numpy as jnp
        import numpy as np
        D_MODEL = 256
        N_HEADS = 16
        HEAD_DIM = D_MODEL // N_HEADS
        KV_LATENT = 128
        N_EXPERTS = 4
        D_HIDDEN = 4 * D_MODEL
        B, T = (2, 256)

        def rmsnorm(x, w, eps=1e-06):
            return w * (x * jax.lax.rsqrt(jnp.mean(x * x, axis=-1, keepdims=True) + eps))

        def layernorm(x, g, b, eps=1e-05):
            mu = jnp.mean(x, axis=-1, keepdims=True)
            var = jnp.mean((x - mu) ** 2, axis=-1, keepdims=True)
            return (x - mu) * jax.lax.rsqrt(var + eps) * g + b

        def apply_rope(x):
            t, d = (x.shape[2], x.shape[3])
            half = d // 2
            pos = jnp.arange(t, dtype=x.dtype)[:, None]
            inv_freq = 1.0 / 10000.0 ** (jnp.arange(half, dtype=x.dtype) / half)
            ang = pos * inv_freq[None, :]
            sin, cos = (jnp.sin(ang), jnp.cos(ang))
            x1, x2 = (x[..., :half], x[..., half:])
            return jnp.concatenate([x1 * cos - x2 * sin, x1 * sin + x2 * cos], axis=-1)

        def mla_attention(x, Wq, Wdkv, Wuk, Wuv, Wo, ln_g, ln_b):
            b, t, _ = x.shape
            q = (x @ Wq.T).reshape(b, t, N_HEADS, HEAD_DIM).transpose(0, 2, 1, 3)
            latent = layernorm(x @ Wdkv.T, ln_g, ln_b)
            k = (latent @ Wuk.T).reshape(b, t, N_HEADS, HEAD_DIM).transpose(0, 2, 1, 3)
            v = (latent @ Wuv.T).reshape(b, t, N_HEADS, HEAD_DIM).transpose(0, 2, 1, 3)
            q = apply_rope(q)
            k = apply_rope(k)
            scores = jnp.einsum('bhqd,bhkd->bhqk', q, k) / np.sqrt(HEAD_DIM)
            causal = jnp.tril(jnp.ones((t, t), dtype=bool))
            scores = jnp.where(causal, scores, -jnp.inf)
            attn = jax.nn.softmax(scores, axis=-1)
            out = jnp.einsum('bhqk,bhkd->bhqd', attn, v).transpose(0, 2, 1, 3).reshape(b, t, D_MODEL)
            return out @ Wo.T

        def moe(x, gate_w, gate_b, W1, b1, W2, b2):
            logits = x @ gate_w.T + gate_b
            top = jnp.argmax(logits, axis=-1)
            onehot = jax.nn.one_hot(top, N_EXPERTS, dtype=x.dtype)
            h = jax.nn.relu(jnp.einsum('btd,ehd->bteh', x, W1) + b1)
            y = jnp.einsum('bteh,edh->bted', h, W2) + b2
            return jnp.einsum('bted,bte->btd', y, onehot)
        x = x + mla_attention(rmsnorm(x, norm1_w), Wq, Wdkv, Wuk, Wuv, Wo, ln_g, ln_b)
        x = x + moe(rmsnorm(x, norm2_w), gate_w, gate_b, W1, b1, W2, b2)
        return x

    def _L1_attn_ref(u, A_log, W_x, W_dt, b_dt, D_param):
        import jax, jax.numpy as jnp
        import numpy as np
        D_INNER = 256
        STATE = 16
        DT_RANK = 64

        def _combine(carry, nxt):
            a1, b1 = carry
            a2, b2 = nxt
            return (a1 * a2, a2 * b1 + b2)
        N = A_log.shape[1]
        dt_rank = W_dt.shape[1]
        x_dbl = jnp.einsum('bld,ed->ble', u, W_x)
        dt_raw = x_dbl[..., :dt_rank]
        B_sel = x_dbl[..., dt_rank:dt_rank + N]
        C_sel = x_dbl[..., dt_rank + N:]
        dt = jax.nn.softplus(jnp.einsum('blr,dr->bld', dt_raw, W_dt) + b_dt)
        A = -jnp.exp(A_log)
        A_bar = jnp.exp(dt[..., None] * A)
        dB_u = (dt * u)[..., None] * B_sel[:, :, None, :]
        _, h = jax.lax.associative_scan(_combine, (A_bar, dB_u), axis=1)
        y = jnp.einsum('bldn,bln->bld', h, C_sel)
        return y + u * D_param

    def _L1_ffn_ref(x, gate_w, gate_b, w1, b1, w2, b2):
        import jax, jax.numpy as jnp
        import numpy as np
        NUM_EXPERTS = 8
        TOP_K = 2
        D = 256
        H = 4 * D
        B, S = (4, 512)
        orig_shape = x.shape
        xf = x.reshape(-1, orig_shape[-1])
        gates = xf @ gate_w.T + gate_b
        weights, indices = jax.lax.top_k(gates, TOP_K)
        weights = jax.nn.softmax(weights, axis=-1)
        out = jnp.zeros_like(xf)
        for e in range(NUM_EXPERTS):
            w_e = jnp.sum(weights * (indices == e), axis=-1, keepdims=True)
            h = jax.nn.gelu(xf @ w1[e] + b1[e], approximate=False)
            out = out + w_e * (h @ w2[e] + b2[e])
        return out.reshape(orig_shape)
    x = L0_attn_x
    xn = _layernorm(x, axis=-1)
    x = x + _L0_attn_ref(xn, L0_attn_w_qkv, L0_attn_w_out) + _L0_ffn_ref(xn, L0_ffn_norm1_w, L0_ffn_norm2_w, L0_ffn_Wq, L0_ffn_Wdkv, L0_ffn_Wuk, L0_ffn_Wuv, L0_ffn_Wo, L0_ffn_ln_g, L0_ffn_ln_b, L0_ffn_gate_w, L0_ffn_gate_b, L0_ffn_W1, L0_ffn_b1, L0_ffn_W2, L0_ffn_b2)
    xn = _layernorm(x, axis=-1)
    x = x + _L1_attn_ref(xn, L1_attn_A_log, L1_attn_W_x, L1_attn_W_dt, L1_attn_b_dt, L1_attn_D_param) + _L1_ffn_ref(xn, L1_ffn_gate_w, L1_ffn_gate_b, L1_ffn_w1, L1_ffn_b1, L1_ffn_w2, L1_ffn_b2)
    return x

_drawn_inputs = setup_inputs


def setup_inputs(seed=0):
    import zlib

    import numpy as np

    out = dict(_drawn_inputs(seed))
    spreads = {'L0_ffn_norm1_w': (1.0, 0.2),
     'L0_ffn_norm2_w': (1.0, 0.2),
     'L0_ffn_ln_g': (1.0, 0.2),
     'L0_ffn_ln_b': (0.0, 0.1),
     'L0_ffn_gate_b': (0.0, 0.1),
     'L0_ffn_b1': (0.0, 0.1),
     'L0_ffn_b2': (0.0, 0.1),
     'L1_attn_D_param': (1.0, 0.2),
     'L1_ffn_gate_b': (0.0, 0.514),
     'L1_ffn_b1': (0.0, 0.8),
     'L1_ffn_b2': (0.0, 0.357)}
    factors = {'L1_attn_A_log': 8.0, 'L1_attn_W_x': 8.0, 'L1_attn_W_dt': 8.0, 'L1_attn_b_dt': 8.0}
    for name, (base, spread) in spreads.items():
        noise = np.random.default_rng([zlib.crc32(name.encode()), seed]).standard_normal(out[name].shape)
        drawn = base * np.exp(spread * noise) if base else spread * noise
        out[name] = jnp.asarray(drawn.astype(out[name].dtype))
    for name, factor in factors.items():
        out[name] = (out[name] * factor).astype(out[name].dtype)
    return out
```

```python
import math
from contextlib import ExitStack

import numpy as np

import concourse.bass as bass
from concourse import mybir

F32 = mybir.dt.float32
BF16 = mybir.dt.bfloat16
I32 = mybir.dt.int32
U32 = mybir.dt.uint32
ALU = mybir.AluOpType
ACT = mybir.ActivationFunctionType
AX = mybir.AxisListType

P = 128
BATCH, SEQ, D = 4, 1024, 256
TOK = BATCH * SEQ
H, HD = 16, 16
KC = D // P
BLK = 512
SUB = BLK // P
HPG = 4
HG = H // HPG
GROUPS = 2 * BATCH * HG
NQT = SEQ // P
TILES = TOK // P
E0, K0 = 4, 1
E1, K1 = 8, 2
PARTS = 3
SPLIT = [(0, 0), (0, 1), (1, 0), (1, 1), (0, 2), (2, 0)]
SROWS = len(SPLIT) * HD
MROWS = 2
VW = 2 * HD
MASKED = -1.0e30
LN_EPS, RMS_EPS = 1e-5, 1e-6
HID = 4 * D
HC = HID // P
NB = HID + D
NS, RANK = 16, 64


def expert_tiles(experts, per_token):
    most = TILES * per_token + experts - 1
    return most + most % 2


class Semaphores:

    GPSIMD_DMAS = ("sent", "gathered")

    def __init__(self, nc, prefix):
        self.nc, self.prefix, self.held = nc, prefix, []

    def __call__(self, name):
        s = self.nc.alloc_semaphore(self.prefix + name)
        if not name.startswith(self.GPSIMD_DMAS):
            self.held.append(s)
        return s

    def __enter__(self):
        return self

    def __exit__(self, *_):
        self.nc.clear_and_free_semaphores(self.held)
        self.nc.all_engine_barrier()


class Steps:

    def __init__(self, eng, sem, turn=0, per_turn=0):
        self.eng, self.sem, self.turn, self.per_turn, self.n = eng, sem, turn, per_turn, 0

    def __call__(self, ins):
        ins.then_inc(self.sem, 1)
        self.n += 1
        self.eng.wait_ge(self.sem, self.turn * self.per_turn + self.n)

    def end(self):
        assert self.n == self.per_turn, (self.n, self.per_turn)


def project_phase(nc, T):
    with ExitStack() as ctx:
        sb = lambda n, s, d=F32: ctx.enter_context(nc.sbuf_tensor("pj_" + n, s, d))
        ps = lambda n, s, d=F32: ctx.enter_context(nc.psum_tensor("pj_" + n, s, d))
        sem = ctx.enter_context(Semaphores(nc, "pj_"))
        ident = sb("ident", [P, P])
        cos = sb("cos", [P, SEQ])
        sin = sb("sin", [P, SEQ])
        w_qk = sb("w_qk", [P, KC, 4, 2, P])
        w_v = sb("w_v", [P, KC, D])
        m_q = sb("m_q", [P, KC, 2, 2, P])
        m_dkv = sb("m_dkv", [P, KC, P])
        m_k = sb("m_k", [P, 2, 2, P])
        m_v = sb("m_v", [P, D])
        norm1 = sb("norm1", [P, KC])
        lng = sb("lng", [P, 2])
        x = sb("x", [P, 2, SUB, D])
        xn = sb("xn", [P, 2, SUB, D])
        xr = sb("xr", [P, 2, SUB, D])
        stats = sb("stats", [P, SUB, 6])
        spare = sb("spare", [P, 1])
        mv = sb("mv", [P, SUB, 2])
        rs = sb("rs", [P, 4, SUB])
        xnT = sb("xnT", [P, 2, KC, BLK])
        xrT = sb("xrT", [P, 2, KC, BLK])
        lat = sb("lat", [P, SUB, P])
        latn = sb("latn", [P, SUB, P])
        lstats = sb("lstats", [P, SUB, 6])
        lmv = sb("lmv", [P, SUB, 2])
        lrs = sb("lrs", [P, 2, SUB])
        latT = sb("latT", [P, BLK])
        tc = sb("tc", [P, 2, BLK])
        ts = sb("ts", [P, 2, BLK])
        rot = sb("rot", [P, 2, BLK])
        rest = sb("rest", [P, 2, BLK])
        parts = sb("parts", [P, 2, PARTS, BLK], BF16)
        val = sb("val", [P, 2, SUB, H * VW])
        pT = ps("pT", [P, 2, BLK])
        pQ = ps("pQ", [P, 2, 2, BLK])
        pV = ps("pV", [P, 2, BLK])

        consts = sem("consts")
        x_in, xn_stored = [sem("x_in0"), sem("x_in1")], [sem("xn_stored0"), sem("xn_stored1")]
        scaled, dve, normed, tps, tev = sem("scaled"), sem("dve"), sem("normed"), sem("tps"), sem("tev")
        pair_mm, pair_rot, rotd = sem("pair_mm"), sem("pair_rot"), sem("rotd")
        hi_done, rest_done, mid_done, lo_done = sem("hi"), sem("rest"), sem("mid"), sem("lo")
        stored = [sem("stored0"), sem("stored1")]
        dkv_mm, lat_ev, latn_ready, latT_ready = sem("dkv"), sem("lat_ev"), sem("latn"), sem("latT")
        v_mm, v_ev, ones = sem("v_mm"), sem("v_ev"), sem("ones")
        v_stored = [sem("v_stored0"), sem("v_stored1")]
        var_ready, root_ready, lvar_ready, lroot_ready = sem("var"), sem("root"), sem("lvar"), sem("lroot")
        block = ctx.enter_context(nc.Block())
        NCONST = 11
        PAIRS = 8

        @block.sync
        def _(sp):
            for dst, src in ((ident, "ident"), (cos, "cos"), (sin, "sin"), (w_qk, "w_qk"), (w_v, "w_v"),
                             (m_q, "m_q"), (m_dkv, "m_dkv"), (m_k, "m_k"), (m_v, "m_v"), (norm1, "norm1"),
                             (lng, "lng")):
                sp.dma_start(dst[:], T[src]).then_inc(consts, 16)
            for h in range(2):
                sp.dma_start(x[:, h], T["x"][0, :, SUB * h:SUB * h + SUB, :]).then_inc(x_in[h], 16)

            def turn(b, last):
                for h in range(2):
                    n = 2 * b + h
                    sp.wait_ge(normed, n + 1)
                    if not last:
                        sp.dma_start(x[:, h], T["x"][b + 1, :, SUB * h:SUB * h + SUB, :]).then_inc(x_in[h], 16)
                    sp.dma_start(T["xn"][b, :, SUB * h:SUB * h + SUB, :], xn[:, h]).then_inc(xn_stored[h], 16)
                    for s in range(PAIRS):
                        k, p = PAIRS * n + s, s % 2
                        at, qk, c = s // 4, s // 2 % 2, s % 2
                        sp.wait_ge(lo_done, k + 1)
                        for g2 in range(2):
                            sp.dma_start(
                                T["qk_parts"][at * BATCH + b, 2 * c + g2, qk].rearrange("a r t -> r a t")[
                                    :, :, BLK * h:BLK * h + BLK],
                                parts[64 * g2:64 * g2 + 64, p]).then_inc(stored[p], 16)
                        if s not in (3, 6):
                            continue
                        at = s // 6
                        sp.wait_ge(v_ev, 4 * n + 2 * at + 3)
                        for hg in range(HG):
                            sp.dma_start(
                                T["v_pad"][at * BATCH + b, hg, BLK * h:BLK * h + BLK, :].rearrange(
                                    "(j p) w -> p j w", p=P),
                                val[:, at, :, P * hg:P * hg + P]).then_inc(v_stored[at], 16)

            with sp.Fori(0, BATCH - 1) as b:
                turn(b, False)
            turn(BATCH - 1, True)
            for h in range(2):
                sp.wait_ge(xn_stored[h], 16 * (BATCH + 1))
            for at in range(2):
                sp.wait_ge(v_stored[at], 64 * (2 * BATCH + 1))
            for p in range(2):
                sp.wait_ge(stored[p], 32 * (4 * 2 * BATCH + 1))

        @block.vector
        def _(dve_e):
            v = nc.vector
            for credit, count in ((xn_stored[0], 16), (xn_stored[1], 16), (dkv_mm, 2), (latn_ready, 1), (latT_ready, 1), (v_ev, 1),
                                  (pair_rot, 2), (rotd, 2), (stored[0], 32), (stored[1], 32),
                                  (v_stored[0], 64), (v_stored[1], 64)):
                v.sem_inc(credit, count)
            v.memset(val[:], 1.0).then_inc(ones, 1)
            dve_e.wait_ge(consts, 16 * NCONST)
            for kc in range(KC):
                v.tensor_scalar(m_q[:, kc], m_q[:, kc], norm1[:, kc:kc + 1], None, ALU.mult).then_inc(scaled, 1)
                v.tensor_scalar(m_dkv[:, kc], m_dkv[:, kc], norm1[:, kc:kc + 1], None,
                                ALU.mult).then_inc(scaled, 1)
            with dve_e.Fori(0, BATCH) as b:
                step = Steps(dve_e, dve, b, 2 * 6)
                for h in range(2):
                    n = 2 * b + h
                    dve_e.wait_ge(x_in[h], 16 * (b + 1))
                    for j in range(SUB):
                        ins = v.bn_stats(stats[:, j], x[:, h, j])
                        if j == SUB - 1:
                            step(ins)
                    v.memset(spare[:], 0.0)
                    for j in range(SUB):
                        ins = v.bn_aggr(mv[:, j], stats[:, j])
                        if j == SUB - 1:
                            step(ins)
                    v.tensor_scalar(rs[:, 0], mv[:, :, 1], LN_EPS, None, ALU.add)
                    v.tensor_scalar(rs[:, 1], mv[:, :, 1], 1.0 + RMS_EPS, LN_EPS * RMS_EPS, ALU.mult,
                                    ALU.add).then_inc(var_ready, 1)
                    dve_e.wait_ge(root_ready, n + 1)
                    step(v.reciprocal(rs[:, 0:2], rs[:, 2:4]))
                    dve_e.wait_ge(xn_stored[h], 16 * (b + 1))
                    dve_e.wait_ge(dkv_mm, n + 1)
                    for j in range(SUB):
                        v.tensor_scalar(xn[:, h, j], x[:, h, j], mv[:, j, 0:1], rs[:, 0, j:j + 1],
                                        ALU.subtract, ALU.mult)
                    for j in range(SUB):
                        ins = v.tensor_scalar(xr[:, h, j], x[:, h, j], mv[:, j, 0:1], rs[:, 1, j:j + 1],
                                              ALU.subtract, ALU.mult)
                    ins.then_inc(normed, 1)

                    def pair(s):
                        k, p = PAIRS * n + s, s % 2
                        at = BLK * h
                        dve_e.wait_ge(pair_mm, k + 1)
                        dve_e.wait_ge(rotd, k + 1)
                        v.tensor_tensor(tc[:, p], pQ[:, p, 0], cos[:, at:at + BLK], ALU.mult)
                        v.tensor_tensor(ts[:, p], pQ[:, p, 1], sin[:, at:at + BLK],
                                        ALU.mult).then_inc(pair_rot, 1)

                    pair(0)
                    dve_e.wait_ge(lat_ev, n + 1)
                    for j in range(SUB):
                        ins = v.bn_stats(lstats[:, j], lat[:, j])
                        if j == SUB - 1:
                            step(ins)
                    v.memset(spare[:], 0.0)
                    for j in range(SUB):
                        ins = v.bn_aggr(lmv[:, j], lstats[:, j])
                        if j == SUB - 1:
                            step(ins)
                    v.tensor_scalar(lrs[:, 0], lmv[:, :, 1], LN_EPS, None, ALU.add).then_inc(lvar_ready, 1)
                    dve_e.wait_ge(lroot_ready, n + 1)
                    step(v.reciprocal(lrs[:, 0], lrs[:, 1]))
                    for j in range(SUB):
                        ins = v.tensor_scalar(latn[:, j], lat[:, j], lmv[:, j, 0:1], lrs[:, 0, j:j + 1],
                                              ALU.subtract, ALU.mult)
                    ins.then_inc(latn_ready, 1)
                    for s in range(1, PAIRS):
                        pair(s)
                step.end()

        @block.scalar
        def _(act):
            a = nc.scalar
            act.wait_ge(ones, 1)
            act.wait_ge(consts, 16 * NCONST)
            with act.Fori(0, BATCH) as b:
                for h in range(2):
                    n = 2 * b + h
                    act.wait_ge(var_ready, n + 1)
                    a.activation(rs[:, 2:4], rs[:, 0:2], ACT.Sqrt).then_inc(root_ready, 1)
                    for q, dst in enumerate((xnT[:, h, 0], xnT[:, h, 1], xrT[:, h, 0], xrT[:, h, 1])):
                        act.wait_ge(tps, 5 * n + q + 1)
                        a.activation(dst, pT[:, q % 2], ACT.Copy).then_inc(tev, 1)
                    act.wait_ge(dkv_mm, n + 3)
                    act.wait_ge(latn_ready, n + 1)
                    a.activation(lat[:], pV[:, 0].rearrange("p (j l) -> p j l", j=SUB),
                                 ACT.Copy).then_inc(lat_ev, 1)
                    act.wait_ge(lvar_ready, n + 1)
                    a.activation(lrs[:, 1], lrs[:, 0], ACT.Sqrt).then_inc(lroot_ready, 1)

                    def split(s):
                        k, p = PAIRS * n + s, s % 2
                        act.wait_ge(rotd, k + 3)
                        act.wait_ge(stored[p], 32 * (4 * n + s // 2 + 1))
                        a.activation(parts[:, p, 0], rot[:, p], ACT.Copy).then_inc(hi_done, 1)
                        act.wait_ge(rest_done, k + 1)
                        a.activation(parts[:, p, 1], rest[:, p], ACT.Copy).then_inc(mid_done, 1)

                    def values(at, half):
                        act.wait_ge(v_mm, 4 * n + 2 * at + half + 1)
                        if half == 0:
                            act.wait_ge(v_stored[at], 64 * (n + 1))
                        for j in range(2):
                            ins = a.activation(
                                val[:, at, 2 * half + j].rearrange("p (h w) -> p h w", w=VW)[:, :, 0:HD],
                                pV[:, half, D * j:D * j + D].rearrange("p (h w) -> p h w", w=HD), ACT.Copy)
                        ins.then_inc(v_ev, 1)

                    split(0)
                    act.wait_ge(tps, 5 * n + 5)
                    a.activation(latT[:], pT[:, 0], ACT.Identity, bias=lng[:, 1:2],
                                 scale=lng[:, 0:1]).then_inc(latT_ready, 1)
                    for s in range(1, PAIRS):
                        split(s)
                        if s in (2, 3):
                            values(0, s - 2)
                        if s in (5, 6):
                            values(1, s - 5)

        @block.gpsimd
        def _(pool):
            g = nc.gpsimd
            with pool.Fori(0, BATCH) as b:
                for h in range(2):
                    n = 2 * b + h
                    for s in range(PAIRS):
                        k, p = PAIRS * n + s, s % 2
                        pool.wait_ge(pair_rot, k + 3)
                        g.tensor_tensor(rot[:, p], tc[:, p], ts[:, p], ALU.add).then_inc(rotd, 1)
                        pool.wait_ge(hi_done, k + 1)
                        g.tensor_tensor(rest[:, p], rot[:, p], parts[:, p, 0], ALU.subtract).then_inc(rest_done, 1)
                        pool.wait_ge(mid_done, k + 1)
                        g.tensor_tensor(parts[:, p, 2], rest[:, p], parts[:, p, 1],
                                        ALU.subtract).then_inc(lo_done, 1)

        @block.tensor
        def _(pe):
            t = nc.tensor
            pe.wait_ge(consts, 16 * NCONST)
            pe.wait_ge(scaled, 2 * KC)
            with pe.Fori(0, BATCH) as b:
                for h in range(2):
                    n = 2 * b + h
                    pe.wait_ge(normed, n + 1)
                    for q in range(4):
                        if q < 2:
                            pe.wait_ge(latT_ready, n + 1)
                        else:
                            pe.wait_ge(tev, 4 * n + q - 1)
                        src = xn if q < 2 else xr
                        for j in range(SUB):
                            ins = t.transpose(pT[:, q % 2, P * j:P * j + P],
                                              src[:, h, j, P * (q % 2):P * (q % 2) + P], ident[:])
                        ins.then_inc(tps, 1)
                    pe.wait_ge(tev, 4 * n + 4)
                    pe.wait_ge(v_ev, 4 * n + 1)
                    for j in range(SUB):
                        for kc in range(KC):
                            ins = t.matmul(pV[:, 0, P * j:P * j + P], xrT[:, h, kc, P * j:P * j + P],
                                           m_dkv[:, kc], start=kc == 0, stop=kc == KC - 1)
                    ins.then_inc(dkv_mm, 1)

                    def pair(s):
                        k, p, c = PAIRS * n + s, s % 2, s % 4
                        pe.wait_ge(pair_rot, k + 1)
                        for turned in range(2):
                            if s < 4:
                                ops = [(w_qk[:, kc, c, turned], xnT[:, h, kc]) for kc in range(KC)]
                            elif s < 6:
                                ops = [(m_q[:, kc, c, turned], xrT[:, h, kc]) for kc in range(KC)]
                            else:
                                ops = [(m_k[:, c - 2, turned], latT[:])]
                            for m, (w, r) in enumerate(ops):
                                ins = t.matmul(pQ[:, p, turned], w, r, start=m == 0, stop=m == len(ops) - 1)
                        ins.then_inc(pair_mm, 1)

                    def values(at, half):
                        if half == 0 and at == 0:
                            pe.wait_ge(lat_ev, n + 1)
                        else:
                            pe.wait_ge(v_ev, 4 * n + 2 * at + half)
                        for j in range(2):
                            jj = 2 * half + j
                            if at == 0:
                                for kc in range(KC):
                                    ins = t.matmul(pV[:, half, D * j:D * j + D],
                                                   xnT[:, h, kc, P * jj:P * jj + P], w_v[:, kc],
                                                   start=kc == 0, stop=kc == KC - 1)
                            else:
                                ins = t.matmul(pV[:, half, D * j:D * j + D], latT[:, P * jj:P * jj + P],
                                               m_v[:], start=True, stop=True)
                        ins.then_inc(v_mm, 1)

                    pair(0)
                    pe.wait_ge(latn_ready, n + 2)
                    for j in range(SUB):
                        ins = t.transpose(pT[:, 0, P * j:P * j + P], latn[:, j], ident[:])
                    ins.then_inc(tps, 1)
                    for s in range(1, PAIRS):
                        pair(s)
                        if s in (1, 2):
                            values(0, s - 1)
                        if s in (4, 5):
                            values(1, s - 4)


def attention_phase(nc, T):
    with ExitStack() as ctx:
        sb = lambda n, s, d=F32: ctx.enter_context(nc.sbuf_tensor("at_" + n, s, d))
        ps = lambda n, s, d=F32: ctx.enter_context(nc.psum_tensor("at_" + n, s, d))
        sem = ctx.enter_context(Semaphores(nc, "at_"))
        NBUF = 4
        AHEAD = 2
        masks_in = sb("masks_in", [P, 3, P])
        masks = sb("masks", [P, 3, P], BF16)
        ident, mask_q, mask_k = masks[:, 0], masks[:, 1], masks[:, 2]
        qs = sb("qs", [SROWS + MROWS, NBUF, HPG, SEQ], BF16)
        ks = sb("ks", [SROWS + MROWS, NBUF, HPG, SEQ], BF16)
        vs = sb("vs", [P, NBUF, NQT, HPG * VW])
        mp = sb("mp", [P, 2, HPG * NQT])
        mx = sb("mx", [P, HPG * NQT])
        mm = sb("mm", [P, MROWS, HPG * NQT], BF16)
        mt = sb("mt", [MROWS * HPG * NQT, P], BF16)
        w = sb("w", [P, 2, HPG, SEQ])
        zero = sb("zero", [P, SUB * D])
        outg = sb("outg", [P, 2, SEQ])
        pS = ps("pS", [P, 2, BLK])
        pW = ps("pW", [P, 2, SEQ])
        pO = ps("pO", [P, SEQ])

        consts, ones = sem("consts"), sem("ones")
        loaded = [sem(f"loaded{u}") for u in range(NBUF)]
        m_in = [sem(f"m_in{u}") for u in range(NBUF)]
        s_mm, s_red, mm_ready, mt_ready, m_out = (sem(n) for n in (
            "s_mm", "s_red", "mm_ready", "mt_ready", "m_out"))
        w_mm, exp_done, pv_mm, dve, out_ready = (sem(n) for n in ("w_mm", "exp", "pv_mm", "dve", "out_ready"))
        zeroed, cleared = sem("zeroed"), sem("cleared")
        out_stored = [sem("out_stored0"), sem("out_stored1")]
        block = ctx.enter_context(nc.Block())

        PIECES = [(h, qt, c) for h in range(HPG) for qt in range(NQT) for c in range((qt + 4) // 4)]
        SPREAD = 1.15
        COLUMNS = HPG * (2 * P * NQT * (NQT + 1) // 2 + P * NQT)
        NP = len(PIECES) + 2
        NW = NQT * HPG
        LOADS = 2 * len(SPLIT) + 1
        TURNS = GROUPS // NBUF

        def groups(eng, body):
            with eng.Fori(0, TURNS - 1) as i:
                for u in range(NBUF):
                    body(NBUF * i + u, u, i, False)
            for u in range(NBUF):
                body(NBUF * (TURNS - 1) + u, u, TURNS - 1, True)

        @block.sync
        def _(sp):
            sp.dma_start(masks_in[:], T["masks"]).then_inc(consts, 16)
            parts = T["qk_parts"].rearrange("a g q p r t -> (a g) q p r t")
            vals = T["v_pad"].rearrange("a g t w -> (a g) t w")

            def load(g, u):
                for n, which in enumerate(SPLIT):
                    for side, dst in enumerate((qs, ks)):
                        sp.dma_start(dst[HD * n:HD * n + HD, u],
                                     parts[g, side, which[side]].rearrange("(h d) t -> d h t", d=HD)
                                     ).then_inc(loaded[u], 16)
                sp.dma_start(vs[:, u], vals[g].rearrange("(k p) w -> p k w", p=P)).then_inc(loaded[u], 16)

            def send_maxima(g, u):
                sp.wait_ge(mt_ready, g + 1)
                sp.dma_start(T["m_rows"][g].rearrange("m (a t) -> (m a) t", t=P), mt[:]).then_inc(m_out, 16)
                sp.wait_ge(m_out, 16 * (g + 2))
                sp.dma_start(qs[SROWS:SROWS + MROWS, u], T["m_rows"][g].rearrange("m (h t) -> m h t", h=HPG)
                             ).then_inc(m_in[u], 16)

            def send_out(g, u):
                sp.wait_ge(out_ready, g + 2)
                sp.dma_start(T["att"][g], outg[:, u % 2]).then_inc(out_stored[u % 2], 16)

            for u in range(NBUF - 1):
                load(u, u)
            sp.wait_ge(zeroed, 1)
            clears = 0
            for table in (T["a_sorted"], T["b_sorted"]):
                rows = table.rearrange("(n p j) d -> n p (j d)", p=P, j=SUB)
                for n in range(rows.shape[0]):
                    sp.dma_start(rows[n], zero[:]).then_inc(cleared, 16)
                    clears += 1
            for u in range(AHEAD):
                send_maxima(u, u)

            def body(g, u, i, last):
                if not last or u + NBUF - 1 < NBUF:
                    sp.wait_ge(pv_mm, NQT * g + 2)
                    load(g + NBUF - 1, (u + NBUF - 1) % NBUF)
                if not last or u + AHEAD < NBUF:
                    send_maxima(g + AHEAD, (u + AHEAD) % NBUF)
                send_out(g, u)

            groups(sp, body)
            for p in range(2):
                sp.wait_ge(out_stored[p], 16 * (GROUPS // 2 + 1))
            sp.wait_ge(cleared, 16 * clears)

        @block.vector
        def _(dve_e):
            v = nc.vector
            for credit, count in ((exp_done, 2), (pv_mm, 2), (out_stored[0], 16),
                                  (out_stored[1], 16), (s_red, 2), (out_ready, 1), (m_out, 16)):
                v.sem_inc(credit, count)
            v.memset(zero[:], 0.0).then_inc(zeroed, 1)
            v.memset(ks[SROWS:SROWS + MROWS], 1.0).then_inc(ones, 1)
            v.memset(mp[:], -3.0e38).then_inc(ones, 1)
            dve_e.wait_ge(ones, 2)
            dve_e.wait_ge(consts, 16)
            v.tensor_copy(masks[:], masks_in[:]).then_inc(ones, 1)

            def maxima(g):
                for n, (h, qt, c) in enumerate(PIECES):
                    width = min(BLK, P * (qt + 1) - BLK * c)
                    dve_e.wait_ge(s_mm, NP * g + n + 1)
                    v.tensor_reduce(mp[:, c, NQT * h + qt:NQT * h + qt + 1], pS[:, n % 2, 0:width], AX.X,
                                    ALU.max).then_inc(s_red, 1)
                dve_e.wait_ge(s_red, NP * g + len(PIECES) + 2)
                step = Steps(dve_e, dve, g, 2)
                step(v.tensor_tensor(mx[:], mp[:, 0], mp[:, 1], ALU.max))
                step(v.tensor_scalar(mm[:, 0], mx[:], -1.0, None, ALU.mult))
                v.scalar_tensor_tensor(mm[:, 1], mx[:], -1.0, mm[:, 0], ALU.mult,
                                       ALU.subtract).then_inc(mm_ready, 1)
                dve_e.wait_ge(s_mm, NP * g + NP)
                dve_e.wait_ge(m_out, 16 * (g + 1))
                v.tensor_copy(mt[:], pS[0:MROWS * HPG * NQT, len(PIECES) % 2, 0:P // 2].bitcast(BF16)
                              ).then_inc(mt_ready, 1)
                dve_e.wait_ge(mt_ready, g + 1)
                v.sem_inc(s_red, 2)

            for u in range(AHEAD):
                maxima(u)

            def body(g, u, i, last):
                if not last or u + AHEAD < NBUF:
                    maxima(g + AHEAD)
                dve_e.wait_ge(pv_mm, NQT * (g + 1) + 2)
                dve_e.wait_ge(out_stored[u % 2], 16 * (2 * i + u // 2 + 1))
                v.tensor_copy(outg[:, u % 2], pO[:]).then_inc(out_ready, 1)

            groups(dve_e, body)

        @block.scalar
        def _(act):
            a = nc.scalar
            scale = 1.0 / math.sqrt(HD)

            def body(g, u, i, last):
                for kt in range(NQT):
                    act.wait_ge(pv_mm, NQT * g + kt + 1)
                    for h in range(HPG):
                        e = HPG * kt + h
                        act.wait_ge(w_mm, NW * g + e + 1)
                        a.activation(w[:, kt % 2, h, 0:SEQ - P * kt], pW[:, e % 2, 0:SEQ - P * kt], ACT.Exp,
                                     scale=scale).then_inc(exp_done, 1)

            groups(act, body)

        @block.tensor
        def _(pe):
            t = nc.tensor
            pe.wait_ge(ones, 3)

            def score(g, u, n):
                h, qt, c = PIECES[n]
                width = min(BLK, P * (qt + 1) - BLK * c)
                diagonal = c == qt // 4
                pe.wait_ge(s_red, NP * g + n + 1)
                ins = t.matmul(pS[:, n % 2, 0:width], qs[0:SROWS, u, h, P * qt:P * qt + P],
                               ks[0:SROWS, u, h, BLK * c:BLK * c + width], start=True, stop=not diagonal)
                if diagonal:
                    ins = t.matmul(pS[:, n % 2, width - P:width], ident, mask_q, start=False, stop=True)
                ins.then_inc(s_mm, 1)

            def turn_maxima(g):
                n = len(PIECES)
                pe.wait_ge(s_red, NP * g + n + 1)
                pe.wait_ge(mm_ready, g + 1)
                t.transpose(pS[0:MROWS * HPG * NQT, n % 2, 0:P // 2].bitcast(BF16),
                            mm[:].rearrange("p m a -> p (m a)"), ident).then_inc(s_mm, 2)

            def weigh(g, u, kt, h, fill):
                e = HPG * kt + h
                pe.wait_ge(exp_done, NW * g + e + 1)
                at = P * kt
                keys = ks[:, u, h, at:at + P]
                first = min(BLK, SEQ - at)
                t.matmul(pW[:, e % 2, 0:first], keys, qs[:, u, h, at:at + first], start=True, stop=False)
                ins = t.matmul(pW[:, e % 2, 0:P], ident, mask_k, start=False, stop=True)
                if at + first < SEQ:
                    fill(first + P)
                    ins = t.matmul(pW[:, e % 2, BLK:SEQ - at], keys, qs[:, u, h, at + first:SEQ],
                                   start=True, stop=True)
                ins.then_inc(w_mm, 1)
                fill(SEQ - at - first if at + first < SEQ else first + P)

            def values(g, u, kt, fill):
                pe.wait_ge(exp_done, NW * g + HPG * (kt + 1) + 2)
                if kt == 0:
                    pe.wait_ge(out_ready, g + 1)
                at = P * kt
                for lo, hi in ((at, BLK), (max(BLK, at), SEQ)):
                    if lo >= hi:
                        continue
                    for h in range(HPG):
                        ins = t.matmul(pO[VW * h:VW * h + VW, lo:hi], vs[:, u, kt, VW * h:VW * h + VW],
                                       w[:, kt % 2, h, lo - at:hi - at], start=kt == 0,
                                       stop=kt == (3 if hi == BLK else NQT - 1))
                    if hi < SEQ or lo >= hi:
                        fill(HPG * (hi - lo))
                ins.then_inc(pv_mm, 1)
                fill(HPG * (SEQ - max(BLK, at)))

            for u in range(AHEAD):
                pe.wait_ge(loaded[u], 16 * LOADS)
                for n in range(len(PIECES)):
                    score(u, u, n)
                turn_maxima(u)

            def body(g, u, i, last):
                ahead = not last or u + AHEAD < NBUF
                ua = (u + AHEAD) % NBUF
                if ahead:
                    pe.wait_ge(loaded[ua], 16 * LOADS * (i + 1 + (u + AHEAD) // NBUF))
                pe.wait_ge(m_in[u], 16 * (i + 1))
                done = [0, 0]

                def fill(columns):
                    done[1] += columns
                    while ahead and done[0] < min(len(PIECES), SPREAD * len(PIECES) * done[1] / COLUMNS):
                        score(g + AHEAD, ua, done[0])
                        done[0] += 1

                for kt in range(NQT + 1):
                    if kt < NQT:
                        for h in range(HPG):
                            weigh(g, u, kt, h, fill)
                    if kt > 0:
                        values(g, u, kt - 1, fill)
                assert not ahead or done[0] == len(PIECES)
                if ahead:
                    turn_maxima(g + AHEAD)

            groups(pe, body)


def route_phase(nc, T, E, K, pre, send):
    NT = expert_tiles(E, K)
    NCH = TILES * K
    with ExitStack() as ctx:
        sb = lambda n, s, d=F32: ctx.enter_context(nc.sbuf_tensor(f"{pre}rt_" + n, s, d))
        sem = ctx.enter_context(Semaphores(nc, f"{pre}rt_"))
        before = sb("before", [P, P])
        ones = sb("ones", [P, P])
        iota_e = sb("iota_e", [P, E])
        iota_t = sb("iota_t", [P, NT])
        choice = sb("choice", [P, NCH])
        rows = sb("rows", [P, TILES, D]) if send else None
        hot = sb("hot", [P, NCH, E])
        total = sb("total", [P, NCH, E])
        upto = sb("upto", [P, NCH, E])
        rank = sb("rank", [P, NCH, E])
        zeros = sb("zeros", [P, NCH])
        count = sb("count", [P, E])
        counti = sb("counti", [P, E], I32)
        ntile = sb("ntile", [P, E])
        end = sb("end", [P, E])
        base = sb("base", [P, E])
        slot = sb("slot", [P, NCH])
        sloti = sb("sloti", [P, NCH], I32)
        ge = sb("ge", [P, NT, E])
        te = sb("te", [P, NT])
        tei = sb("tei", [P, NT], I32)
        pC = ctx.enter_context(nc.psum_tensor(f"{pre}rt_pC", [P, NCH, E], F32))
        pN = ctx.enter_context(nc.psum_tensor(f"{pre}rt_pN", [P, NCH, E], F32))
        loaded, hot_ready, counted, dve = sem("loaded"), sem("hot"), sem("counted"), sem("dve")
        slots_ready, rows_in, stored = sem("slots"), sem("rows_in"), sem("stored")
        sent = sem("sent") if send else None
        block = ctx.enter_context(nc.Block())

        @block.sync
        def _(sp):
            for dst, src in ((before, "before"), (ones, "ones"), (choice, pre + "choice")):
                sp.dma_start(dst[:], T[src]).then_inc(loaded, 16)
            sp.dma_start(iota_e[:], T["iota"][:, 0:E]).then_inc(loaded, 16)
            sp.dma_start(iota_t[:], T["iota"][:, 0:NT]).then_inc(loaded, 16)
            if send:
                sp.dma_start(rows[:], T[pre + "rows"]).then_inc(rows_in, 16)
            sp.wait_ge(slots_ready, 1)
            sp.dma_start(T[pre + "slots"], sloti[:]).then_inc(stored, 16)
            sp.dma_start(T[pre + "tile_expert"], tei[0:1, :]).then_inc(stored, 16)
            sp.wait_ge(stored, 32)

        @block.tensor
        def _(pe):
            pe.wait_ge(hot_ready, 1)
            flat = lambda a: a.rearrange("p c e -> p (c e)")
            nc.tensor.matmul(flat(pC[:]), before[:], flat(hot[:]), start=True, stop=True)
            nc.tensor.matmul(flat(pN[:]), ones[:], flat(hot[:]), start=True, stop=True).then_inc(counted, 1)

        @block.vector
        def _(dve_e):
            v = nc.vector
            step = Steps(dve_e, dve)
            dve_e.wait_ge(loaded, 16 * 5)
            step(v.memset(zeros[:], 0.0))
            v.tensor_tensor(hot[:], iota_e[:].unsqueeze(1).to_broadcast([P, NCH, E]),
                            choice[:].unsqueeze(2).to_broadcast([P, NCH, E]),
                            ALU.is_equal).then_inc(hot_ready, 1)
            dve_e.wait_ge(counted, 1)
            step(v.tensor_copy(total[:], pN[:]))
            for e in range(E):
                ins = v.tensor_tensor_scan(upto[:, :, e], total[:, :, e], zeros[:], 0.0, ALU.add, ALU.add)
            step(ins)
            step(v.tensor_scalar(count[:], upto[:, NCH - 1, :], float(P - 1), None, ALU.add))
            step(v.tensor_copy(counti[:], count[:]))
            step(v.tensor_scalar(counti[:], counti[:], P.bit_length() - 1, None, ALU.logical_shift_right))
            step(v.tensor_copy(ntile[:], counti[:]))
            step(v.tensor_tensor_scan(end[:], ntile[:], zeros[:, 0:E], 0.0, ALU.add, ALU.add))
            step(v.tensor_tensor(base[:], end[:], ntile[:], ALU.subtract))
            step(v.tensor_scalar(base[:], base[:], float(P), None, ALU.mult))
            step(v.tensor_tensor(rank[:], upto[:], total[:], ALU.subtract))
            step(v.tensor_tensor(rank[:], rank[:], pC[:], ALU.add))
            step(v.tensor_tensor(rank[:], rank[:], base[:].unsqueeze(1).to_broadcast([P, NCH, E]), ALU.add))
            step(v.tensor_tensor(rank[:], rank[:], hot[:], ALU.mult))
            step(v.tensor_reduce(slot[:], rank[:], AX.X, ALU.add))
            step(v.tensor_copy(sloti[:], slot[:]))
            step(v.tensor_tensor(ge[:], iota_t[:].unsqueeze(2).to_broadcast([P, NT, E]),
                                 end[:].unsqueeze(1).to_broadcast([P, NT, E]), ALU.is_ge))
            step(v.tensor_reduce(te[:], ge[:], AX.X, ALU.add))
            step(v.tensor_scalar(te[:], te[:], float(E - 1), None, ALU.min))
            v.tensor_copy(tei[:], te[:]).then_inc(slots_ready, 1)

        if send:
            @block.gpsimd
            def _(pool):
                pool.wait_ge(rows_in, 16)
                pool.wait_ge(slots_ready, 1)
                for t in range(TILES):
                    for k in range(K):
                        c = K * t + k
                        nc.gpsimd.indirect_dma_start(
                            out=T[pre + "sorted"], in_=rows[:, t, :], in_offset=None,
                            out_offset=bass.IndirectOffsetOnAxis(ap=sloti[:, c:c + 1], axis=0)).then_inc(sent, 16)
                pool.wait_ge(sent, 16 * NCH)


class ExpertWeights:

    def __init__(self, nc, ctx, T, E, pre):
        sem = ctx.enter_context(Semaphores(nc, f"{pre}w_"))
        self.T, self.E, self.pre = T, E, pre
        self.w1 = ctx.enter_context(nc.sbuf_tensor(f"{pre}held_w1", [P, E, KC, HID], F32))
        self.w2 = ctx.enter_context(nc.sbuf_tensor(f"{pre}held_w2", [P, E, HC, D], F32))
        self.loaded = sem("loaded")
        self.all_loaded = 16 * 2 * E

    def load(self, sp):
        for e in range(self.E):
            sp.dma_start(self.w1[:, e], self.T[self.pre + "w1"][e]).then_inc(self.loaded, 16)
            sp.dma_start(self.w2[:, e], self.T[self.pre + "w2"][e]).then_inc(self.loaded, 16)


class ExpertTiles:

    def __init__(self, nc, ctx, sem, T, E, K, pre, weights, func):
        sb = lambda n, s, d=F32: ctx.enter_context(nc.sbuf_tensor(f"{pre}ex_" + n, s, d))
        ps = lambda n, s, d=F32: ctx.enter_context(nc.psum_tensor(f"{pre}ex_" + n, s, d))
        self.nc, self.T, self.E, self.pre, self.func, self.weights = nc, T, E, pre, func, weights
        self.NT = expert_tiles(E, K)
        self.ident = sb("ident", [P, P])
        self.wnorm = sb("wnorm", [P, KC])
        self.tile_expert = sb("tile_expert", [1, self.NT], I32)
        self.brow = sb("brow", [E * PARTS, NB], BF16)
        self.pick_in = sb("pick_in", [E * PARTS, E])
        self.pick = sb("pick", [E * PARTS, E, P], BF16)
        self.xs = sb("xs", [P, 2, D])
        self.xsT = sb("xsT", [P, D])
        self.h = sb("h", [P, HID])
        self.hT = sb("hT", [P, HID])
        self.y = sb("y", [P, 2, D])
        self.pX = ps("pX", [P, BLK])
        self.pH = ps("pH", [P, HID])
        self.pT = ps("pT", [P, HID])
        self.pY = ps("pY", [P, 2, BLK])
        self.consts, self.ready = sem("consts"), sem("ready")
        self.x_in = [sem("x_in0"), sem("x_in1")]
        self.y_out = [sem("y_out0"), sem("y_out1")]
        self.xt, self.xt_ev, self.hm, self.gated, self.ht, self.ht_ev, self.ym, self.y_ev = (
            sem(n) for n in ("xt", "xt_ev", "hm", "gated", "ht", "ht_ev", "ym", "y_ev"))
        self.tiles_in = T[pre + "sorted"].rearrange("(n p) d -> n p d", p=P)
        self.tiles_out = T[pre + "y"].rearrange("(n p) d -> n p d", p=P)

    def load_tables(self, sp):
        T, pre = self.T, self.pre
        for dst, src in ((self.ident, T["ident"]), (self.tile_expert, T[pre + "tile_expert"]),
                         (self.wnorm, T[pre + "wnorm"]), (self.pick_in, T[pre + "pick"]),
                         (self.brow, T[pre + "bparts"].rearrange("e s n -> (e s) n"))):
            sp.dma_start(dst[:], src).then_inc(self.consts, 16)
        for u in range(2):
            sp.dma_start(self.xs[:, u], self.tiles_in[u]).then_inc(self.x_in[u], 16)

    def load_rows(self, sp, n, u):
        sp.wait_ge(self.xt, n + 1)
        sp.dma_start(self.xs[:, u], self.tiles_in[n + 2]).then_inc(self.x_in[u], 16)

    def store_result(self, sp, n, u):
        sp.wait_ge(self.y_ev, n + 1 + 2)
        sp.dma_start(self.tiles_out[n], self.y[:, u]).then_inc(self.y_out[u], 16)

    def stored(self, sp):
        for u in range(2):
            sp.wait_ge(self.y_out[u], 16 * (self.NT // 2 + 1))

    def prepare(self, dve_e):
        v = self.nc.vector
        for credit, count in ((self.xt_ev, 1), (self.y_ev, 2), (self.y_out[0], 16), (self.y_out[1], 16),
                              (self.gated, 1), (self.ht_ev, 1), (self.ym, 1), (self.ht, 1)):
            v.sem_inc(credit, count)
        dve_e.wait_ge(self.consts, 16 * 5)
        v.tensor_copy(self.pick[:], self.pick_in[:].unsqueeze(2).to_broadcast(
            [self.E * PARTS, self.E, P])).then_inc(self.ready, 1)

    def scale_weights(self, dve_e):
        w = self.weights
        dve_e.wait_ge(w.loaded, w.all_loaded)
        for e in range(self.E):
            for kc in range(KC):
                ins = self.nc.vector.tensor_scalar(w.w1[:, e, kc], w.w1[:, e, kc],
                                                   self.wnorm[:, kc:kc + 1], None, ALU.mult)
        ins.then_inc(self.ready, 1)

    def rows_turned(self, dve_e, n):
        dve_e.wait_ge(self.xt, n + 1)
        self.nc.vector.tensor_copy(self.xsT[:], self.pX[:, 0:D]).then_inc(self.xt_ev, 1)

    def hidden_turned(self, dve_e, n):
        dve_e.wait_ge(self.ht, n + 2)
        self.nc.vector.tensor_copy(self.hT[:], self.pT[:]).then_inc(self.ht_ev, 1)

    def result(self, dve_e, n, u, pairs):
        dve_e.wait_ge(self.ym, n + 2)
        dve_e.wait_ge(self.y_out[u], 16 * (pairs + 1))
        self.nc.vector.tensor_copy(self.y[:, u], self.pY[:, u, 0:D]).then_inc(self.y_ev, 1)

    def gate(self, act, n):
        act.wait_ge(self.hm, n + 1)
        self.nc.scalar.activation(self.h[:], self.pH[:], self.func).then_inc(self.gated, 1)

    def products(self, pe, scaled):
        t, w = self.nc.tensor, self.weights
        pe.wait_ge(self.consts, 16 * 5)
        pe.wait_ge(w.loaded, w.all_loaded)
        pe.wait_ge(self.ready, 2 if scaled else 1)

        def rows(n, pairs, u):
            pe.wait_ge(self.x_in[u], 16 * (pairs + 1))
            pe.wait_ge(self.xt_ev, n + 1)
            for kc in range(KC):
                ins = t.transpose(self.pX[:, P * kc:P * kc + P], self.xs[:, u, P * kc:P * kc + P], self.ident[:])
            ins.then_inc(self.xt, 1)

        def up(n):
            e = pe.value_load(self.tile_expert[0:1, bass.ds(n, 1)], min_val=0, max_val=self.E - 1)
            pe.wait_ge(self.xt_ev, n + 2)
            pe.wait_ge(self.gated, n + 1)
            for c in range(2):
                out = self.pH[:, BLK * c:BLK * c + BLK]
                t.matmul(out, self.pick[:, e], self.brow[:, BLK * c:BLK * c + BLK], start=True, stop=False)
                for kc in range(KC):
                    ins = t.matmul(out, self.xsT[:, P * kc:P * kc + P], w.w1[:, e, kc, BLK * c:BLK * c + BLK],
                                   start=False, stop=kc == KC - 1)
            ins.then_inc(self.hm, 1)

        def turn_hidden(n):
            pe.wait_ge(self.gated, n + 2)
            pe.wait_ge(self.ht_ev, n + 1)
            for c in range(HC):
                ins = t.transpose(self.pT[:, P * c:P * c + P], self.h[:, P * c:P * c + P], self.ident[:])
            ins.then_inc(self.ht, 1)

        def down(n, u):
            e = pe.value_load(self.tile_expert[0:1, bass.ds(n, 1)], min_val=0, max_val=self.E - 1)
            pe.wait_ge(self.ht_ev, n + 2)
            pe.wait_ge(self.y_ev, n + 1)
            t.matmul(self.pY[:, u, 0:D], self.pick[:, e], self.brow[:, HID:NB], start=True, stop=False)
            for c in range(HC):
                ins = t.matmul(self.pY[:, u, 0:D], self.hT[:, P * c:P * c + P], w.w2[:, e, c], start=False,
                               stop=c == HC - 1)
            ins.then_inc(self.ym, 1)

        def turn(i, last):
            for u in range(2):
                n = 2 * i + u
                turn_hidden(n)
                if not (last and u == 1):
                    up(n + 1)
                if not last:
                    rows(n + 2, i + 1, u)
                down(n, u)

        rows(0, 0, 0)
        up(0)
        rows(1, 0, 1)
        with pe.Fori(0, self.NT // 2 - 1) as i:
            turn(i, False)
        turn(self.NT // 2 - 1, True)


def experts_phase(nc, T, E, K, pre, func, weights):
    with ExitStack() as ctx:
        sem = ctx.enter_context(Semaphores(nc, f"{pre}ex_"))
        tiles = ExpertTiles(nc, ctx, sem, T, E, K, pre, weights, func)
        PAIRS = tiles.NT // 2
        block = ctx.enter_context(nc.Block())

        @block.sync
        def _(sp):
            tiles.load_tables(sp)

            def turn(i, last):
                for u in range(2):
                    if not last:
                        tiles.load_rows(sp, 2 * i + u, u)
                    tiles.store_result(sp, 2 * i + u, u)

            with sp.Fori(0, PAIRS - 1) as i:
                turn(i, False)
            turn(PAIRS - 1, True)
            tiles.stored(sp)

        @block.vector
        def _(dve_e):
            tiles.prepare(dve_e)
            tiles.scale_weights(dve_e)
            for n in range(2):
                tiles.rows_turned(dve_e, n)

            def turn(i, last):
                for u in range(2):
                    n = 2 * i + u
                    tiles.hidden_turned(dve_e, n)
                    if not last:
                        tiles.rows_turned(dve_e, n + 2)
                    tiles.result(dve_e, n, u, i)

            with dve_e.Fori(0, PAIRS - 1) as i:
                turn(i, False)
            turn(PAIRS - 1, True)

        @block.scalar
        def _(act):
            with act.Fori(0, PAIRS) as i:
                for u in range(2):
                    tiles.gate(act, 2 * i + u)

        @block.tensor
        def _(pe):
            tiles.products(pe, True)


def bias_parts_phase(nc, T):
    with ExitStack() as ctx:
        sb = lambda n, s, d=F32: ctx.enter_context(nc.sbuf_tensor("bp_" + n, s, d))
        sem = ctx.enter_context(Semaphores(nc, "bp_"))
        loaded, dve, stored = sem("loaded"), sem("dve"), sem("stored")
        tables = [(pre, sb(pre + "bias", [E, NB]), sb(pre + "parts", [E, PARTS, NB], BF16))
                  for pre, E in (("a_", E0), ("b_", E1))]
        block = ctx.enter_context(nc.Block())

        @block.sync
        def _(sp):
            for pre, bias, parts in tables:
                sp.dma_start(bias[:], T[pre + "bias"]).then_inc(loaded, 16)
            for n, (pre, bias, parts) in enumerate(tables):
                sp.wait_ge(dve, 5 * (n + 1))
                sp.dma_start(T[pre + "bparts"], parts[:]).then_inc(stored, 16)
            sp.wait_ge(stored, 32)

        @block.vector
        def _(dve_e):
            v = nc.vector
            step = Steps(dve_e, dve)
            dve_e.wait_ge(loaded, 32)
            for pre, bias, parts in tables:
                step(v.tensor_copy(parts[:, 0], bias[:]))
                step(v.tensor_tensor(bias[:], bias[:], parts[:, 0], ALU.subtract))
                step(v.tensor_copy(parts[:, 1], bias[:]))
                step(v.tensor_tensor(bias[:], bias[:], parts[:, 1], ALU.subtract))
                step(v.tensor_copy(parts[:, 2], bias[:]))


def denominators_phase(nc, T, weights):
    with ExitStack() as ctx:
        den = ctx.enter_context(nc.sbuf_tensor("dn_den", [P, SEQ], F32))
        sem = ctx.enter_context(Semaphores(nc, "dn_"))
        loaded, ready, stored = sem("in"), sem("ready"), sem("out")
        block = ctx.enter_context(nc.Block())
        sums = T["att"].rearrange("g (j r) t -> (g j) r t", r=VW)

        @block.sync
        def _(sp):
            sp.dma_start(den[:], sums[:, HD, :]).then_inc(loaded, 16)
            weights.load(sp)
            sp.wait_ge(ready, 1)
            sp.dma_start(T["rden"].rearrange("g j t -> (g j) t"), den[:]).then_inc(stored, 16)
            sp.wait_ge(stored, 16)

        @block.vector
        def _(dve_e):
            dve_e.wait_ge(loaded, 16)
            nc.vector.reciprocal(den[:], den[:]).then_inc(ready, 1)


def mix_phase(nc, T, second):
    E, K, pre = (E1, K1, "b_") if second else (E0, K0, "a_")
    NBLK = TOK // BLK
    with ExitStack() as ctx:
        sb = lambda n, s, d=F32: ctx.enter_context(nc.sbuf_tensor(f"{pre}mx_" + n, s, d))
        ps = lambda n, s, d=F32: ctx.enter_context(nc.psum_tensor(f"{pre}mx_" + n, s, d))
        sem = ctx.enter_context(Semaphores(nc, f"{pre}mx_"))
        ident = sb("ident", [P, P])
        gate = sb("gate", [P, KC, 8])
        gnorm = sb("gnorm", [P, KC])
        gbias = sb("gbias", [P, 8])
        if second:
            slots = sb("slots", [P, TILES], I32)
            moe = sb("moe", [P, TILES, D])
            base_in = sb("base_in", [P, SUB, D])
        else:
            wo = sb("wo", [P, 2, HG, D])
            att = sb("att", [P, 2, HG, BLK])
            rden = sb("rden", [P, 2, HG, BLK])
            xn = sb("xn", [P, SUB, D])
            x = sb("x", [P, SUB, D])
            sumx = sb("sumx", [P, SUB, D])
        x2 = sb("x2", [P, SUB, D])
        base = sb("base", [P, SUB, D])
        rows = sb("rows", [P, SUB, D])
        stats = sb("stats", [P, SUB, 6])
        spare = sb("spare", [P, 1])
        mv = sb("mv", [P, SUB, 2])
        rs = sb("rs", [P, 3, SUB])
        rowsT = sb("rowsT", [P, KC, BLK])
        logits = sb("logits", [P, SUB, 8])
        top = sb("top", [P, SUB, 8])
        topi = sb("topi", [P, SUB, 8], U32)
        choice = sb("choice", [P, TILES, K])
        gap = sb("gap", [P, TILES])
        weights = sb("weights", [P, K, TILES])
        pM = ps("pM", [P, 2, BLK])
        pA = ps("pA", [P, 2, BLK])
        pT = ps("pT", [P, KC, BLK])
        pL = ps("pL", [P, SUB, 8])
        consts, dve, dve2, scaled = sem("consts"), sem("dve"), sem("dve2"), sem("scaled")
        in_a, in_x, norm0, norm1, mm = sem("in_a"), sem("in_x"), sem("norm0"), sem("norm1"), sem("mm")
        x2_done, var_ready, root_ready, rows_ready = sem("x2"), sem("var"), sem("root"), sem("rows")
        base_ready, turned, turned_ev, lm, top_ready = (
            sem("base"), sem("turned"), sem("turned_ev"), sem("lm"), sem("top"))
        base_c = sem("base_c")
        summed, stored, rows_st, gathered = sem("summed"), sem("stored"), sem("rows_st"), sem("gathered")
        exp_in, exp_out, final = sem("exp_in"), sem("exp_out"), sem("final")
        block = ctx.enter_context(nc.Block())
        NCONST = 5 if second else 5

        @block.sync
        def _(sp):
            for dst, src in ((ident, "ident"), (gate, pre + "gate"), (gnorm, pre + "gnorm"),
                             (gbias, pre + "gbias"), (slots, "a_slots") if second else (wo, "wo")):
                sp.dma_start(dst[:], T[src]).then_inc(consts, 16)
            with sp.Fori(0, BATCH) as b:
                for h in range(2):
                    n = 2 * b + h
                    tok = slice(SUB * h, SUB * h + SUB)
                    if second:
                        sp.wait_ge(base_ready, n + 1)
                        sp.dma_start(base_in[:], T["base"][:, bass.ds(SUB * n, SUB), :]).then_inc(in_x, 16)
                    else:
                        sp.wait_ge(mm, 4 * n + 4)
                        for at in range(2):
                            for hg in range(HG):
                                g = at * BATCH * HG + b * HG + hg
                                sp.dma_start(att[:, at, hg], T["att"][g, :, BLK * h:BLK * h + BLK]
                                             ).then_inc(in_a, 16)
                                for j in range(HPG):
                                    src = T["rden"][g, j:j + 1, BLK * h:BLK * h + BLK]
                                    sp.dma_start(rden[VW * j:VW * j + VW, at, hg],
                                                 src.to_broadcast([VW, BLK])).then_inc(in_a, 16)
                        sp.wait_ge(base_ready, n + 1)
                        sp.dma_start(xn[:], T["xn"][b, :, tok, :]).then_inc(in_x, 16)
                        sp.dma_start(x[:], T["x"][b, :, tok, :]).then_inc(in_x, 16)
                    sp.wait_ge(base_ready, n + 2)
                    sp.dma_start(T["res" if second else "base"][:, bass.ds(SUB * n, SUB), :], base[:]
                                 ).then_inc(stored, 16)
                    sp.wait_ge(rows_ready, n + 1)
                    sp.dma_start(T[pre + "rows"][:, bass.ds(SUB * n, SUB), :], rows[:]).then_inc(rows_st, 16)
                    if second:
                        sp.wait_ge(turned_ev, 2 * n + 2)
                        sp.dma_start(T["uT"][:, :, bass.ds(BLK * n, BLK)], rowsT[:]).then_inc(rows_st, 16)
            sp.wait_ge(final, 1)
            sp.dma_start(T[pre + "choice"], choice[:].rearrange("p t k -> p (t k)")).then_inc(consts, 16)
            if second:
                sp.dma_start(T["weights"], weights[:]).then_inc(consts, 16)
            sp.wait_ge(consts, 16 * (NCONST + (2 if second else 1)))
            sp.wait_ge(stored, 16 * (NBLK + 1))
            sp.wait_ge(rows_st, (32 if second else 16) * (NBLK + 1))

        @block.gpsimd
        def _(pool):
            g = nc.gpsimd
            pool.wait_ge(consts, 16 * NCONST)
            if second:
                for n in range(NBLK):
                    for j in range(SUB):
                        g.indirect_dma_start(
                            out=moe[:, SUB * n + j, :], out_offset=None, in_=T["a_y"],
                            in_offset=bass.IndirectOffsetOnAxis(ap=slots[:, SUB * n + j:SUB * n + j + 1], axis=0)
                        ).then_inc(gathered, 16)
                    pool.wait_ge(gathered, 16 * SUB * (n + 1))
                    pool.sem_inc(in_a, 1)
            else:
                with pool.Fori(0, NBLK) as n:
                    pool.wait_ge(in_a, 16 * 40 * (n + 1))
                    g.tensor_tensor(att[:, 1], att[:, 1], rden[:, 1], ALU.mult).then_inc(norm1, 1)
                    pool.wait_ge(x2_done, 4 * n + 4)
                    g.tensor_tensor(sumx[:], x[:], x2[:], ALU.add).then_inc(summed, 1)

        @block.vector
        def _(dve_e):
            v = nc.vector
            for credit, count in ((base_ready, 1), (base_c, 2), (mm, 4), (stored, 16),
                                  (rows_st, 32 if second else 16)):
                v.sem_inc(credit, count)
            dve_e.wait_ge(consts, 16 * NCONST)
            for kc in range(KC):
                v.tensor_scalar(gate[:, kc], gate[:, kc], gnorm[:, kc:kc + 1], None, ALU.mult).then_inc(scaled, 1)
            with dve_e.Fori(0, NBLK) as n:
                step = Steps(dve_e, dve, n, 6 if second else 8)
                if second:
                    dve_e.wait_ge(in_x, 16 * (n + 1))
                    dve_e.wait_ge(in_a, n + 1)
                    dve_e.wait_ge(stored, 16 * (n + 1))
                    v.tensor_tensor(base[:], base_in[:], moe[:, bass.ds(SUB * n, SUB), :], ALU.add).then_inc(base_ready, 1)
                    dve_e.wait_ge(base_ready, n + 2)
                    src = base
                else:
                    dve_e.wait_ge(in_a, 16 * 40 * (n + 1))
                    v.tensor_tensor(att[:, 0], att[:, 0], rden[:, 0], ALU.mult).then_inc(norm0, 1)
                    dve_e.wait_ge(in_x, 32 * (n + 1))
                    for j in range(SUB):
                        dve_e.wait_ge(mm, 4 * n + j + 1 + 4)
                        v.tensor_tensor(x2[:, j], pM[:, j % 2, 0:D], xn[:, j], ALU.add).then_inc(x2_done, 1)
                        if j == 0:
                            dve_e.wait_ge(stored, 16 * (n + 1))
                        v.tensor_copy(base[:, j], pM[:, j % 2, D:2 * D]).then_inc(base_c, 1)
                    dve_e.wait_ge(x2_done, 4 * n + 4)
                    src = x2
                for j in range(SUB):
                    ins = v.bn_stats(stats[:, j], src[:, j])
                step(ins)
                v.memset(spare[:], 0.0)
                for j in range(SUB):
                    ins = v.bn_aggr(mv[:, j], stats[:, j])
                step(ins)
                if second:
                    v.tensor_scalar(rs[:, 0], mv[:, :, 1], LN_EPS, None, ALU.add).then_inc(var_ready, 1)
                else:
                    step(v.tensor_tensor(rs[:, 0], mv[:, :, 0], mv[:, :, 0], ALU.mult))
                    step(v.tensor_tensor(rs[:, 0], rs[:, 0], mv[:, :, 1], ALU.add))
                    v.tensor_scalar(rs[:, 0], rs[:, 0], RMS_EPS, None, ALU.add).then_inc(var_ready, 1)
                dve_e.wait_ge(root_ready, n + 1)
                step(v.reciprocal(rs[:, 2], rs[:, 1]))
                dve_e.wait_ge(rows_st, (32 if second else 16) * (n + 1))
                for j in range(SUB):
                    if second:
                        ins = v.tensor_scalar(rows[:, j], src[:, j], mv[:, j, 0:1], rs[:, 2, j:j + 1],
                                              ALU.subtract, ALU.mult)
                    else:
                        ins = v.tensor_scalar(rows[:, j], src[:, j], rs[:, 2, j:j + 1], None, ALU.mult)
                ins.then_inc(rows_ready, 1)
                if not second:
                    dve_e.wait_ge(summed, n + 1)
                    dve_e.wait_ge(base_c, 4 * n + 4 + 2)
                    v.tensor_tensor(base[:], base[:], sumx[:], ALU.add).then_inc(base_ready, 1)
                dve_e.wait_ge(lm, n + 1)
                step(v.tensor_tensor(logits[:], pL[:], gbias[:].unsqueeze(1).to_broadcast([P, SUB, 8]), ALU.add))
                v.memset(spare[:], 0.0)
                for j in range(SUB):
                    ins = v.max(top[:, j], logits[:, j])
                step(ins)
                v.memset(spare[:], 0.0)
                for j in range(SUB):
                    ins = v.max_index(topi[:, j], top[:, j], logits[:, j])
                step(ins)
                ins = v.tensor_copy(choice[:, bass.ds(SUB * n, SUB), :], topi[:, :, 0:K])
                if second:
                    ins = v.tensor_tensor(gap[:, bass.ds(SUB * n, SUB)], top[:, :, 1], top[:, :, 0], ALU.subtract)
                ins.then_inc(top_ready, 1)
                step.end()
            dve_e.wait_ge(top_ready, NBLK)
            if second:
                dve_e.wait_ge(exp_out, 1)
                v.tensor_scalar(gap[:], weights[:, 1], 1.0, None, ALU.add).then_inc(dve2, 1)
                dve_e.wait_ge(dve2, 1)
                v.reciprocal(weights[:, 0], gap[:]).then_inc(dve2, 1)
                dve_e.wait_ge(dve2, 2)
                v.tensor_tensor(weights[:, 1], weights[:, 1], weights[:, 0], ALU.mult).then_inc(final, 1)
            else:
                v.sem_inc(final, 1)

        @block.scalar
        def _(act):
            a = nc.scalar
            with act.Fori(0, NBLK) as n:
                act.wait_ge(var_ready, n + 1)
                a.activation(rs[:, 1], rs[:, 0], ACT.Sqrt).then_inc(root_ready, 1)
                for kc in range(KC):
                    act.wait_ge(turned, 2 * n + kc + 1)
                    if second:
                        act.wait_ge(rows_st, 32 * (n + 1))
                    a.activation(rowsT[:, kc], pT[:, kc], ACT.Copy).then_inc(turned_ev, 1)
            if second:
                act.wait_ge(top_ready, NBLK)
                a.activation(weights[:, 1], gap[:], ACT.Exp).then_inc(exp_out, 1)

        @block.tensor
        def _(pe):
            t = nc.tensor
            pe.wait_ge(consts, 16 * NCONST)
            pe.wait_ge(scaled, 2)
            with pe.Fori(0, NBLK) as n:
                if not second:
                    pe.wait_ge(norm0, n + 1)
                    pe.wait_ge(norm1, n + 1)
                    for j in range(SUB):
                        pe.wait_ge(base_c, 4 * n + j + 1)
                        for at in (1, 0):
                            for hg in range(HG):
                                ins = t.matmul(pM[:, j % 2, D * (1 - at):D * (1 - at) + D],
                                               att[:, at, hg, P * j:P * j + P], wo[:, at, hg],
                                               start=hg == 0, stop=hg == HG - 1)
                        ins.then_inc(mm, 1)
                pe.wait_ge(rows_ready, n + 1)
                for kc in range(KC):
                    for j in range(SUB):
                        ins = t.transpose(pT[:, kc, P * j:P * j + P], rows[:, j, P * kc:P * kc + P], ident[:])
                    ins.then_inc(turned, 1)
                pe.wait_ge(turned_ev, 2 * n + 2)
                for j in range(SUB):
                    for kc in range(KC):
                        ins = t.matmul(pL[:, j], rowsT[:, kc, P * j:P * j + P], gate[:, kc],
                                       start=kc == 0, stop=kc == KC - 1)
                ins.then_inc(lm, 1)


def scan_inputs_phase(nc, T, weights):
    NBLK = TOK // BLK
    CHUNK = 4
    NCHUNK = TILES // CHUNK
    with ExitStack() as ctx:
        sb = lambda n, s, d=F32: ctx.enter_context(nc.sbuf_tensor("si_" + n, s, d))
        ps = lambda n, s, d=F32: ctx.enter_context(nc.psum_tensor("si_" + n, s, d))
        sem = ctx.enter_context(Semaphores(nc, "si_"))
        w_x = sb("w_x", [P, KC, RANK + 2 * NS])
        w_dt = sb("w_dt", [RANK, KC, P])
        b_dt = sb("b_dt", [P, KC])
        d_par = sb("d_par", [P, KC])
        slots = sb("slots", [P, TILES * K1], I32)
        rows = sb("rows", [P, 2, CHUNK, D])
        uT = sb("uT", [P, 2, KC, BLK])
        dtr = sb("dtr", [RANK, 2, BLK])
        bc = sb("bc", [2 * NS, 2, BLK])
        z = sb("z", [P, 2, KC, BLK])
        ez = sb("ez", [P, 2, KC, BLK])
        wz = sb("wz", [P, 2, KC, BLK])
        dt = sb("dt", [P, 2, KC, BLK])
        dtu = sb("dtu", [P, 2, KC, BLK])
        skip = sb("skip", [P, 2, KC, BLK])
        pR = ps("pR", [RANK, 2, BLK])
        pB = ps("pB", [2 * NS, 2, BLK])
        pZ = ps("pZ", [P, 2, KC, BLK])
        consts, dve = sem("consts"), sem("dve")
        u_in = [sem("u_in0"), sem("u_in1")]
        rows_in = [sem("rows_in0"), sem("rows_in1")]
        out = [sem("out0"), sem("out1")]
        rows_mm, dtr_ev, bc_ev, dt_mm, z_done, exp_done, w_done, ln_done, used = (sem(n) for n in (
            "rows_mm", "dtr_ev", "bc_ev", "dt_mm", "z", "exp", "w", "ln", "used"))
        absd = sem("abs")
        sent, chunk_sent = sem("sent"), sem("chunk_sent")
        block = ctx.enter_context(nc.Block())

        @block.sync
        def _(sp):
            for dst, src in ((w_x, "w_x"), (w_dt, "w_dt"), (b_dt, "b_dt"), (d_par, "d_par"),
                             (slots, "b_slots")):
                sp.dma_start(dst[:], T[src]).then_inc(consts, 16)

            def rows_load(n):
                sp.dma_start(rows[:, n % 2], T["b_rows"][:, CHUNK * n:CHUNK * n + CHUNK, :]
                             ).then_inc(rows_in[n % 2], 16)

            for u in range(2):
                sp.dma_start(uT[:, u], T["uT"][:, :, BLK * u:BLK * u + BLK]).then_inc(u_in[u], 16)
                rows_load(u)
            weights.load(sp)

            def turn(i, last):
                for u in range(2):
                    n = 2 * i + u
                    sp.wait_ge(bc_ev, n + 1 + 2)
                    sp.dma_start(T["bc"][n].rearrange("n c t -> c n t"), bc[:, u]).then_inc(out[u], 16)
                    sp.wait_ge(used, n + 1 + 2)
                    sp.dma_start(T["dt"][n], dt[:, u]).then_inc(out[u], 16)
                    sp.dma_start(T["dtu"][n], dtu[:, u]).then_inc(out[u], 16)
                    sp.dma_start(T["skip"][n], skip[:, u]).then_inc(out[u], 16)
                    if not last:
                        sp.dma_start(uT[:, u], T["uT"][:, :, bass.ds(BLK * n + 2 * BLK, BLK)]
                                     ).then_inc(u_in[u], 16)
                        sp.wait_ge(chunk_sent, n + 1)
                        sp.dma_start(rows[:, u], T["b_rows"][:, bass.ds(CHUNK * n + 2 * CHUNK, CHUNK), :]
                                     ).then_inc(rows_in[u], 16)

            with sp.Fori(0, NBLK // 2 - 1) as i:
                turn(i, False)
            turn(NBLK // 2 - 1, True)
            for u in range(2):
                sp.wait_ge(out[u], 64 * (NBLK // 2 + 1))

        @block.gpsimd
        def _(pool):
            pool.wait_ge(consts, 16 * 5)
            for n in range(NCHUNK):
                pool.wait_ge(rows_in[n % 2], 16 * (n // 2 + 1))
                for c in range(CHUNK * K1):
                    at = CHUNK * K1 * n + c
                    nc.gpsimd.indirect_dma_start(
                        out=T["b_sorted"], out_offset=bass.IndirectOffsetOnAxis(ap=slots[:, at:at + 1], axis=0),
                        in_=rows[:, n % 2, c // K1, :], in_offset=None).then_inc(sent, 16)
                pool.wait_ge(sent, 16 * CHUNK * K1 * (n + 1))
                pool.sem_inc(chunk_sent, 1)

        @block.tensor
        def _(pe):
            t = nc.tensor
            pe.wait_ge(consts, 16 * 5)
            with pe.Fori(0, NBLK // 2) as i:
                for u in range(2):
                    n = 2 * i + u
                    pe.wait_ge(u_in[u], 16 * (i + 1))
                    pe.wait_ge(dtr_ev, n + 1)
                    pe.wait_ge(bc_ev, n + 1)
                    for kc in range(KC):
                        t.matmul(pR[:, u], w_x[:, kc, 0:RANK], uT[:, u, kc], start=kc == 0, stop=kc == KC - 1)
                    for kc in range(KC):
                        ins = t.matmul(pB[:, u], w_x[:, kc, RANK:], uT[:, u, kc], start=kc == 0, stop=kc == KC - 1)
                    ins.then_inc(rows_mm, 1)
                    pe.wait_ge(dtr_ev, n + 1 + 2)
                    pe.wait_ge(z_done, n + 1)
                    for kc in range(KC):
                        ins = t.matmul(pZ[:, u, kc], w_dt[:, kc], dtr[:, u], start=True, stop=True)
                    ins.then_inc(dt_mm, 1)

        @block.scalar
        def _(act):
            a = nc.scalar

            def rows_out(n, u, i):
                act.wait_ge(rows_mm, n + 1)
                a.activation(dtr[:, u], pR[:, u], ACT.Copy).then_inc(dtr_ev, 1)
                act.wait_ge(out[u], 64 * (i + 1))
                a.activation(bc[:, u], pB[:, u], ACT.Copy).then_inc(bc_ev, 1)

            def exponential(n, u):
                act.wait_ge(dt_mm, n + 1)
                act.wait_ge(used, n + 1)
                for kc in range(KC):
                    ins = a.activation(z[:, u, kc], pZ[:, u, kc], ACT.Identity, bias=b_dt[:, kc:kc + 1])
                ins.then_inc(z_done, 1)
                act.wait_ge(z_done, n + 1 + 2)
                a.activation(ez[:, u], z[:, u], ACT.Abs).then_inc(absd, 1)
                act.wait_ge(absd, n + 1)
                a.activation(ez[:, u], ez[:, u], ACT.Exp, scale=-1.0).then_inc(exp_done, 1)

            def logarithm(n, u):
                act.wait_ge(w_done, n + 1)
                a.activation(dt[:, u], wz[:, u], ACT.Ln).then_inc(ln_done, 1)

            act.wait_ge(consts, 16 * 5)
            rows_out(0, 0, 0)
            exponential(0, 0)
            with act.Fori(0, NBLK // 2 - 1) as i:
                for u in range(2):
                    n = 2 * i + u
                    rows_out(n + 1, 1 - u, i + u)
                    logarithm(n, u)
                    exponential(n + 1, 1 - u)
            rows_out(NBLK - 1, 1, NBLK // 2 - 1)
            logarithm(NBLK - 2, 0)
            exponential(NBLK - 1, 1)
            logarithm(NBLK - 1, 1)

        @block.vector
        def _(dve_e):
            v = nc.vector
            for credit, count in ((out[0], 64), (out[1], 64), (dtr_ev, 2), (bc_ev, 2), (z_done, 2), (used, 2)):
                v.sem_inc(credit, count)
            dve_e.wait_ge(consts, 16 * 5)
            with dve_e.Fori(0, NBLK // 2) as i:
                step = Steps(dve_e, dve, i, 2 * 4)
                for u in range(2):
                    n = 2 * i + u
                    dve_e.wait_ge(exp_done, n + 1)
                    dve_e.wait_ge(out[u], 64 * (i + 1))
                    step(v.tensor_scalar(wz[:, u], ez[:, u], 1.0, None, ALU.add))
                    v.sem_inc(w_done, 1)
                    for kc in range(KC):
                        v.tensor_scalar(skip[:, u, kc], uT[:, u, kc], d_par[:, kc:kc + 1], None, ALU.mult)
                    v.tensor_scalar(z[:, u], z[:, u], 0.0, None, ALU.max)
                    step(v.scalar_tensor_tensor(ez[:, u], wz[:, u], -1.0, ez[:, u], ALU.add, ALU.subtract))
                    step(v.tensor_tensor(z[:, u], z[:, u], ez[:, u], ALU.subtract))
                    dve_e.wait_ge(ln_done, n + 1)
                    step(v.tensor_tensor(dt[:, u], dt[:, u], z[:, u], ALU.add))
                    v.tensor_tensor(dtu[:, u], dt[:, u], uT[:, u], ALU.mult).then_inc(used, 1)
                step.end()


def experts_and_scan_phase(nc, T, weights):
    NBUF = 4
    HALVES = SEQ // BLK
    with ExitStack() as ctx:
        sb = lambda n, s, d=F32: ctx.enter_context(nc.sbuf_tensor("es_" + n, s, d))
        sem = ctx.enter_context(Semaphores(nc, "es_"))
        tiles = ExpertTiles(nc, ctx, sem, T, E1, K1, "b_", weights, ACT.Gelu)
        TPT = tiles.NT // BATCH
        SPT = HALVES * NS
        assert TPT * BATCH == tiles.NT and TPT % 2 == 0
        a_log = sb("a_log", [P, KC, NS])
        a_neg = sb("a_neg", [P, KC, NS])
        dt = sb("dt", [P, KC, BLK])
        dtu = sb("dtu", [P, HALVES, KC, BLK])
        bc = sb("bc", [P, NBUF, 2, BLK])
        decay = sb("decay", [P, 2, KC, BLK])
        state = sb("state", [P, 4, KC, BLK])
        carry = sb("carry", [P, NS, KC])
        y = sb("y", [P, HALVES, KC, BLK])
        a_in, a_exp, a_ready, zeroed = sem("a_in"), sem("a_exp"), sem("a_ready"), sem("zeroed")
        bc_in = [sem(f"bc_in{q}") for q in range(NBUF)]
        dt_in = sem("dt_in")
        dtu_in = [sem(f"dtu_in{q}") for q in range(HALVES)]
        y_in = [sem(f"y_in{q}") for q in range(HALVES)]
        y_st = [sem(f"y_st{q}") for q in range(HALVES)]
        dbu_done, decayed, scanned, carried, weighed, summed = (sem(n) for n in (
            "dbu", "decayed", "scanned", "carried", "weighed", "summed"))
        block = ctx.enter_context(nc.Block())

        def spread(count, slots):
            return lambda k: range(count * k // slots, count * (k + 1) // slots)

        @block.sync
        def _(sp):
            sp.dma_start(a_log[:], T["a_log"]).then_inc(a_in, 16)
            tiles.load_tables(sp)
            rows = T["bc"].rearrange("b n c t -> (b n) c t")

            def load_bc(step, q):
                sp.dma_start(bc[:, q], rows[step].unsqueeze(0).to_broadcast([P, 2, BLK])).then_inc(bc_in[q], 16)

            sp.dma_start(dt[:], T["dt"][0]).then_inc(dt_in, 16)
            for h in range(HALVES):
                sp.dma_start(dtu[:, h], T["dtu"][h]).then_inc(dtu_in[h], 16)
                sp.dma_start(y[:, h], T["skip"][h]).then_inc(y_in[h], 16)
            for q in range(NBUF):
                load_bc(q, q)
            tiles.load_rows(sp, 0, 0)
            after = spread(TPT, SPT)

            def turn(b, last):
                for s in range(SPT):
                    for j in after(s):
                        if not (last and j + 3 >= TPT):
                            tiles.load_rows(sp, TPT * b + j + 1, (j + 1) % 2)
                    if not (last and s + NBUF >= SPT):
                        sp.wait_ge(weighed, SPT * b + s + 1)
                        load_bc(SPT * b + s + NBUF, s % NBUF)
                    if s % NS == NS - 3 and not (last and s > NS):
                        sp.wait_ge(decayed, SPT * b + s + 3)
                        sp.dma_start(dt[:], T["dt"][HALVES * b + s // NS + 1]).then_inc(dt_in, 16)
                    if s == NS + 3:
                        finish(b, 0, last)
                    for j in after(s):
                        if j > 0:
                            tiles.store_result(sp, TPT * b + j - 1, (j - 1) % 2)
                tiles.store_result(sp, TPT * b + TPT - 1, 1)
                finish(b, 1, last)

            def finish(b, h, last):
                sp.wait_ge(summed, SPT * b + NS * (h + 1) + 4)
                sp.dma_start(T["y_t"][HALVES * b + h], y[:, h]).then_inc(y_st[h], 16)
                if not last:
                    sp.dma_start(dtu[:, h], T["dtu"][HALVES * b + h + HALVES]).then_inc(dtu_in[h], 16)
                    sp.wait_ge(y_st[h], 16 * (b + 1))
                    sp.dma_start(y[:, h], T["skip"][HALVES * b + h + HALVES]).then_inc(y_in[h], 16)

            with sp.Fori(0, BATCH - 1) as b:
                turn(b, False)
            turn(BATCH - 1, True)
            for h in range(HALVES):
                sp.wait_ge(y_st[h], 16 * BATCH)
            tiles.stored(sp)

        @block.vector
        def _(dve_e):
            v = nc.vector
            v.sem_inc(summed, 4)
            v.sem_inc(scanned, 2)
            dve_e.wait_ge(a_exp, 1)
            v.tensor_scalar(a_neg[:], a_neg[:], -1.0, None, ALU.mult).then_inc(a_ready, 1)
            tiles.prepare(dve_e)

            def inputs(S, s, b):
                h = s // NS
                if s % NS == 0:
                    dve_e.wait_ge(dtu_in[h], 16 * (b + 1))
                dve_e.wait_ge(bc_in[s % NBUF], 16 * (SPT // NBUF * b + s // NBUF + 1))
                dve_e.wait_ge(summed, S + 1)
                v.tensor_tensor(state[:, s % 4], dtu[:, h],
                                bc[:, s % NBUF, 0].unsqueeze(1).to_broadcast([P, KC, BLK]),
                                ALU.mult).then_inc(dbu_done, 1)

            def scan(b, s):
                S = SPT * b + s
                dve_e.wait_ge(dbu_done, S + 1)
                dve_e.wait_ge(decayed, S + 1)
                if s % NS == 0:
                    dve_e.wait_ge(zeroed, HALVES * b + s // NS + 1)
                for kc in range(KC):
                    ins = v.tensor_tensor_scan(state[:, s % 4, kc], decay[:, s % 2, kc], state[:, s % 4, kc],
                                               carry[:, s % NS, kc:kc + 1], ALU.mult, ALU.add)
                ins.then_inc(scanned, 1)

            def weigh(b, s):
                S = SPT * b + s
                dve_e.wait_ge(scanned, S + 1 + 2)
                if s < NS:
                    ins = v.tensor_copy(carry[:, s], state[:, s % 4, :, BLK - 1])
                    ins.then_inc(carried, 1)
                    dve_e.wait_ge(carried, NS * b + s + 1)
                v.tensor_tensor(state[:, s % 4], state[:, s % 4],
                                bc[:, s % NBUF, 1].unsqueeze(1).to_broadcast([P, KC, BLK]),
                                ALU.mult).then_inc(weighed, 1)

            after = spread(3 * TPT, 3 * SPT)

            def copies(b, part, last):
                for c in after(part):
                    j, which = c // 3, c % 3
                    if which == 0:
                        tiles.hidden_turned(dve_e, TPT * b + j)
                    elif which == 1 and not (last and j + 2 >= TPT):
                        tiles.rows_turned(dve_e, TPT * b + j + 2)
                    elif which == 2:
                        tiles.result(dve_e, TPT * b + j, j % 2, TPT // 2 * b + j // 2)

            def turn(b, last):
                for s in range(SPT):
                    scan(b, s)
                    copies(b, 3 * s, last)
                    if not (last and s == SPT - 1):
                        inputs(SPT * b + s + 1, (s + 1) % SPT, b + (s + 1) // SPT)
                    copies(b, 3 * s + 1, last)
                    weigh(b, s)
                    if s == NS - 1:
                        v.sem_inc(zeroed, 1)
                    if s == SPT - 1:
                        v.memset(carry[:], 0.0).then_inc(zeroed, 1)
                    copies(b, 3 * s + 2, last)

            v.memset(carry[:], 0.0).then_inc(zeroed, 1)
            inputs(0, 0, 0)
            for n in range(2):
                tiles.rows_turned(dve_e, n)
            with dve_e.Fori(0, BATCH - 1) as b:
                turn(b, False)
            turn(BATCH - 1, True)

        @block.scalar
        def _(act):
            a = nc.scalar
            act.wait_ge(a_in, 16)
            a.activation(a_neg[:], a_log[:], ACT.Exp).then_inc(a_exp, 1)
            act.wait_ge(a_ready, 1)
            after = spread(TPT, SPT)

            with act.Fori(0, BATCH) as b:
                for s in range(SPT):
                    h = s // NS
                    if s % NS == 0:
                        act.wait_ge(dt_in, 16 * (HALVES * b + h + 1))
                    act.wait_ge(scanned, SPT * b + s + 1)
                    for kc in range(KC):
                        ins = a.activation(decay[:, s % 2, kc], dt[:, kc], ACT.Exp,
                                           scale=a_neg[:, kc, s % NS:s % NS + 1])
                    ins.then_inc(decayed, 1)
                    for j in after(s):
                        tiles.gate(act, TPT * b + j)

        @block.gpsimd
        def _(pool):
            with pool.Fori(0, BATCH) as b:
                for s in range(SPT):
                    h = s // NS
                    if s % NS == 0:
                        pool.wait_ge(y_in[h], 16 * (b + 1))
                    pool.wait_ge(weighed, SPT * b + s + 1)
                    pool.wait_ge(summed, SPT * b + s + 4)
                    nc.gpsimd.tensor_tensor(y[:, h], y[:, h], state[:, s % 4], ALU.add).then_inc(summed, 1)

        @block.tensor
        def _(pe):
            tiles.products(pe, False)


def final_phase(nc, T):
    with ExitStack() as ctx:
        sb = lambda n, s, d=F32: ctx.enter_context(nc.sbuf_tensor("fi_" + n, s, d))
        sem = ctx.enter_context(Semaphores(nc, "fi_"))
        ident = sb("ident", [P, P])
        slots = sb("slots", [P, TILES * K1], I32)
        weights = sb("weights", [P, K1, TILES])
        res = sb("res", [P, 2, SUB, D])
        yT = sb("yT", [P, 2, KC, BLK])
        ex = sb("ex", [P, 4, SUB, K1, D])
        out = sb("out", [P, 2, SUB, D])
        pY = ctx.enter_context(nc.psum_tensor("fi_pY", [P, 2, SUB, D], F32))
        consts, dve, done = sem("consts"), sem("dve"), sem("done")
        gathered = [sem("gathered0"), sem("gathered1")]
        r_in = [sem("r_in0"), sem("r_in1")]
        stored = [sem("stored0"), sem("stored1")]
        g_done, turned, read = sem("g_done"), sem("turned"), sem("read")
        NBLK = TOK // BLK
        block = ctx.enter_context(nc.Block())

        @block.sync
        def _(sp):
            sp.dma_start(slots[:], T["b_slots"]).then_inc(consts, 16)
            sp.dma_start(weights[:], T["weights"]).then_inc(consts, 16)
            sp.dma_start(ident[:], T["ident"]).then_inc(consts, 16)
            for n in range(NBLK):
                u = n % 2
                if n >= 2:
                    sp.wait_ge(done, n - 1)
                sp.dma_start(res[:, u], T["res"][:, SUB * n:SUB * n + SUB, :]).then_inc(r_in[u], 16)
                sp.dma_start(yT[:, u], T["y_t"][n]).then_inc(r_in[u], 16)
                if n >= 1:
                    sp.wait_ge(done, n)
                    sp.dma_start(T["out"][:, SUB * (n - 1):SUB * n, :], out[:, 1 - u]).then_inc(stored[1 - u], 16)
            sp.wait_ge(done, NBLK)
            sp.dma_start(T["out"][:, SUB * (NBLK - 1):, :], out[:, 1]).then_inc(stored[1], 16)
            for u in range(2):
                sp.wait_ge(stored[u], 16 * NBLK // 2)

        @block.gpsimd
        def _(pool):
            def all_gathered(n):
                pool.wait_ge(gathered[n % 2], 16 * SUB * K1 * (n // 2 + 1))
                pool.sem_inc(g_done, 1)

            pool.wait_ge(consts, 48)
            for n in range(NBLK):
                if n >= 4:
                    pool.wait_ge(done, n - 3)
                for j in range(SUB):
                    for k in range(K1):
                        c = K1 * (SUB * n + j) + k
                        nc.gpsimd.indirect_dma_start(
                            out=ex[:, n % 4, j, k, :], out_offset=None, in_=T["b_y"],
                            in_offset=bass.IndirectOffsetOnAxis(ap=slots[:, c:c + 1], axis=0)
                        ).then_inc(gathered[n % 2], 16)
                if n >= 1:
                    all_gathered(n - 1)
            all_gathered(NBLK - 1)

        @block.tensor
        def _(pe):
            pe.wait_ge(consts, 48)
            for n in range(NBLK):
                u = n % 2
                pe.wait_ge(r_in[u], 32 * (n // 2 + 1))
                if n >= 2:
                    pe.wait_ge(read, n - 1)
                for j in range(SUB):
                    for kc in range(KC):
                        ins = nc.tensor.transpose(pY[:, u, j, P * kc:P * kc + P], yT[:, u, kc, P * j:P * j + P],
                                                  ident[:])
                ins.then_inc(turned, 1)

        @block.vector
        def _(dve_e):
            v = nc.vector
            step = Steps(dve_e, dve)
            dve_e.wait_ge(consts, 48)
            for n in range(NBLK):
                u = n % 2
                dve_e.wait_ge(r_in[u], 32 * (n // 2 + 1))
                dve_e.wait_ge(turned, n + 1)
                if n >= 2:
                    dve_e.wait_ge(stored[u], 16 * (n // 2))
                step(v.tensor_tensor(out[:, u], res[:, u], pY[:, u], ALU.add))
                v.sem_inc(read, 1)
                dve_e.wait_ge(g_done, n + 1)
                for k in range(K1):
                    for j in range(SUB):
                        ins = v.scalar_tensor_tensor(out[:, u, j], ex[:, n % 4, j, k], weights[:, k, SUB * n + j:
                                                     SUB * n + j + 1], out[:, u, j], ALU.mult, ALU.add)
                    if k < K1 - 1:
                        step(ins)
                ins.then_inc(done, 1)


def shape_constants():
    half = HD // 2
    freq = (np.float32(1.0) / np.float32(10000.0) ** (np.arange(half, dtype=np.float32) / np.float32(half)))
    angle = np.arange(SEQ, dtype=np.float32)[None, :] * freq.astype(np.float32)[:, None]
    row = np.arange(P) % HD
    cos = np.cos(angle)[row % half]
    sin = np.sin(angle)[row % half] * np.where(row < half, -1, 1)[:, None]
    later = np.where(np.arange(P)[None, :] > np.arange(P)[:, None], np.float32(MASKED), np.float32(0))
    count = np.arange(P, dtype=np.float32)
    pick = lambda e: np.repeat(np.eye(e, dtype=np.float32), PARTS, 0)
    return {"a_pick": pick(E0), "b_pick": pick(E1), "before": (count[:, None] < count[None, :]).astype(np.float32), "ones": np.ones((P, P), np.float32),
            "iota": np.tile(count, (P, 1)), "masks": np.ascontiguousarray(np.stack([np.eye(P, dtype=np.float32), later, later.T], 1)),
            "ident": np.eye(P, dtype=np.float32), "cos": cos.astype(np.float32), "sin": sin.astype(np.float32)}


def turned_rows(w):
    w = w.reshape(-1, 2, HD // 2, w.shape[-1])
    return w[:, ::-1].reshape(-1, w.shape[-1])


def lhs_pair(w):
    w = np.asarray(w)
    both = np.stack([w, turned_rows(w)])
    k = w.shape[1]
    both = both.reshape(2, -1, P, k // P, P)
    return np.ascontiguousarray(both.transpose(4, 3, 1, 0, 2))


def k_major(w):
    w = np.asarray(w)
    return np.ascontiguousarray(w.T.reshape(-1, P, w.shape[0]).transpose(1, 0, 2))


def layouts(a):
    a = {k: np.asarray(v) for k, v in a.items()}
    out = dict(shape_constants())
    out["x"] = np.ascontiguousarray(a["L0_attn_x"].reshape(BATCH, NQT, P, D).transpose(0, 2, 1, 3))
    wqkv = a["L0_attn_w_qkv"]
    out["w_qk"] = lhs_pair(wqkv[:2 * D])
    out["w_v"] = k_major(wqkv[2 * D:])
    out["m_q"] = lhs_pair(a["L0_ffn_Wq"])
    out["m_dkv"] = k_major(a["L0_ffn_Wdkv"])
    out["m_k"] = np.ascontiguousarray(lhs_pair(a["L0_ffn_Wuk"])[:, 0])
    out["m_v"] = np.ascontiguousarray(a["L0_ffn_Wuv"].T)
    out["norm1"] = np.ascontiguousarray(a["L0_ffn_norm1_w"].reshape(KC, P).T)
    out["lng"] = np.ascontiguousarray(np.stack([a["L0_ffn_ln_g"], a["L0_ffn_ln_b"]], 1))
    out["a_w1"] = experts_in(a["L0_ffn_W1"].transpose(0, 2, 1))
    out["a_w2"] = experts_in(a["L0_ffn_W2"].transpose(0, 2, 1))
    out["a_bias"] = np.concatenate([a["L0_ffn_b1"], a["L0_ffn_b2"]], 1)
    out["a_wnorm"] = np.ascontiguousarray(a["L0_ffn_norm2_w"].reshape(KC, P).T)
    out["b_w1"] = experts_in(a["L1_ffn_w1"])
    out["b_w2"] = experts_in(a["L1_ffn_w2"])
    out["b_bias"] = np.concatenate([a["L1_ffn_b1"], a["L1_ffn_b2"]], 1)
    out["b_wnorm"] = np.ones((P, KC), np.float32)
    heads = lambda w: np.asarray(w).T.reshape(HG, HPG, HD, D)
    wo = np.zeros((HPG, VW, 2, HG, D), np.float32)
    wo[:, :HD, 0] = heads(a["L0_attn_w_out"]).transpose(1, 2, 0, 3)
    wo[:, :HD, 1] = heads(a["L0_ffn_Wo"]).transpose(1, 2, 0, 3)
    out["wo"] = wo.reshape(P, 2, HG, D)
    for pre, gw, gb in (("a_", "L0_ffn_gate_w", "L0_ffn_gate_b"), ("b_", "L1_ffn_gate_w", "L1_ffn_gate_b")):
        e = a[gw].shape[0]
        gate = np.zeros((P, KC, 8), np.float32)
        gate[:, :, :e] = k_major(a[gw])
        bias = np.full((P, 8), -3.0e38, np.float32)
        bias[:, :e] = a[gb][None]
        out[pre + "gate"], out[pre + "gbias"] = gate, bias
    out["a_gnorm"], out["b_gnorm"] = out["a_wnorm"], out["b_wnorm"]
    out["w_x"] = k_major(a["L1_attn_W_x"])
    out["w_dt"] = np.ascontiguousarray(a["L1_attn_W_dt"].T.reshape(-1, KC, P))
    out["b_dt"] = np.ascontiguousarray(a["L1_attn_b_dt"].reshape(KC, P).T)
    out["d_par"] = np.ascontiguousarray(a["L1_attn_D_param"].reshape(KC, P).T)
    out["a_log"] = np.ascontiguousarray(a["L1_attn_A_log"].reshape(KC, P, -1).transpose(1, 0, 2))
    return out


def experts_in(w):
    e, k, n = w.shape
    return np.ascontiguousarray(w.reshape(e, k // P, P, n).transpose(0, 2, 1, 3))


def expert_scratch(pre, experts, per_token):
    rows = P * expert_tiles(experts, per_token)
    return {
        pre + "choice": ((P, TILES * per_token), F32),
        pre + "rows": ((P, TILES, D), F32),
        pre + "sorted": ((rows, D), F32),
        pre + "y": ((rows, D), F32),
        pre + "slots": ((P, TILES * per_token), I32),
        pre + "tile_expert": ((1, rows // P), I32),
        pre + "bparts": ((experts, PARTS, 5 * D), BF16),
    }


SCRATCH = {
    "rden": ((GROUPS, HPG, SEQ), F32),
    "base": ((P, TILES, D), F32),
    "res": ((P, TILES, D), F32),
    "uT": ((P, KC, TOK), F32),
    "bc": ((TOK // BLK, NS, 2, BLK), F32),
    "dt": ((TOK // BLK, P, KC, BLK), F32),
    "dtu": ((TOK // BLK, P, KC, BLK), F32),
    "skip": ((TOK // BLK, P, KC, BLK), F32),
    "y_t": ((TOK // BLK, P, KC, BLK), F32),
    "weights": ((P, K1, TILES), F32),
    **expert_scratch("a_", E0, K0),
    **expert_scratch("b_", E1, K1),
    "xn": ((BATCH, P, NQT, D), F32),
    "qk_parts": ((2 * BATCH, HG, 2, PARTS, HPG * HD, SEQ), BF16),
    "m_rows": ((GROUPS, MROWS, HPG * SEQ), BF16),
    "att": ((GROUPS, P, SEQ), F32),
    "v_pad": ((2 * BATCH, HG, SEQ, HPG * VW), F32),
}


INPUTS = ("x", "ident", "cos", "sin", "w_qk", "w_v", "m_q", "m_dkv", "m_k", "m_v", "norm1", "lng", "masks", "before", "ones", "iota", "a_w1", "a_w2", "a_bias", "a_wnorm", "b_w1", "b_w2",
          "b_bias", "b_wnorm", "wo", "a_gate", "a_gbias", "a_gnorm", "b_gate", "b_gbias", "b_gnorm", "w_x",
          "w_dt", "b_dt", "d_par", "a_log", "a_pick", "b_pick")


def build_program(nc, T):
    bias_parts_phase(nc, T)
    project_phase(nc, T)
    attention_phase(nc, T)
    with ExitStack() as held:
        weights = ExpertWeights(nc, held, T, E0, "a_")
        denominators_phase(nc, T, weights)
        mix_phase(nc, T, False)
        route_phase(nc, T, E0, K0, "a_", True)
        experts_phase(nc, T, E0, K0, "a_", ACT.Relu, weights)
    mix_phase(nc, T, True)
    route_phase(nc, T, E1, K1, "b_", False)
    with ExitStack() as held:
        weights = ExpertWeights(nc, held, T, E1, "b_")
        scan_inputs_phase(nc, T, weights)
        experts_and_scan_phase(nc, T, weights)
    final_phase(nc, T)


def kernel(**inputs):
    import concourse.bacc as bacc
    from concourse.bass_utils import run_bass_kernel_spmd

    nc = bacc.Bacc("TRN2", target_bir_lowering=False, num_devices=1)
    laid = layouts(inputs)
    arrays, T = {}, {}
    for name in INPUTS:
        a = np.ascontiguousarray(laid[name])
        arrays["in_" + name] = a
        T[name] = nc.dram_tensor("in_" + name, a.shape, mybir.dt.from_np(a.dtype), kind="ExternalInput").ap()
    for name, (shape, dtype) in SCRATCH.items():
        T[name] = nc.dram_tensor("scratch_" + name, shape, dtype).ap()
    T["out"] = nc.dram_tensor("out", (P, TILES, D), F32, kind="ExternalOutput").ap()
    build_program(nc, T)
    r = run_bass_kernel_spmd(nc, [arrays], core_ids=[0])
    out = r.results[0]["out"]
    return np.ascontiguousarray(out.transpose(1, 0, 2)).reshape(BATCH, SEQ, D)
```

```python
import math
from contextlib import ExitStack

import numpy as np

import concourse.bass as bass
from concourse import mybir

F32 = mybir.dt.float32
BF16 = mybir.dt.bfloat16
I32 = mybir.dt.int32
U32 = mybir.dt.uint32
ALU = mybir.AluOpType
ACT = mybir.ActivationFunctionType
AX = mybir.AxisListType

P = 128
BATCH, SEQ, D = 4, 1024, 256
TOK = BATCH * SEQ
H, HD = 16, 16
KC = D // P
BLK = 512
SUB = BLK // P
HPG = 4
HG = H // HPG
GROUPS = 2 * BATCH * HG
NQT = SEQ // P
TILES = TOK // P
E0, K0 = 4, 1
E1, K1 = 8, 2
PARTS = 3
SPLIT = [(0, 0), (0, 1), (1, 0), (1, 1), (0, 2), (2, 0)]
SROWS = len(SPLIT) * HD
MROWS = 2
VW = 2 * HD
MASKED = -1.0e30
LN_EPS, RMS_EPS = 1e-5, 1e-6
HID = 4 * D
HC = HID // P
NB = HID + D
NS, RANK = 16, 64


def expert_tiles(experts, per_token):
    most = TILES * per_token + experts - 1
    return most + most % 2


class Semaphores:

    GPSIMD_DMAS = ("sent", "gathered")

    def __init__(self, nc, prefix):
        self.nc, self.prefix, self.held = nc, prefix, []

    def __call__(self, name):
        s = self.nc.alloc_semaphore(self.prefix + name)
        if not name.startswith(self.GPSIMD_DMAS):
            self.held.append(s)
        return s

    def __enter__(self):
        return self

    def __exit__(self, *_):
        self.nc.clear_and_free_semaphores(self.held)
        self.nc.all_engine_barrier()


class Steps:

    def __init__(self, eng, sem, turn=0, per_turn=0):
        self.eng, self.sem, self.turn, self.per_turn, self.n = eng, sem, turn, per_turn, 0

    def __call__(self, ins):
        ins.then_inc(self.sem, 1)
        self.n += 1
        self.eng.wait_ge(self.sem, self.turn * self.per_turn + self.n)

    def end(self):
        assert self.n == self.per_turn, (self.n, self.per_turn)


def project_phase(nc, T):
    with ExitStack() as ctx:
        sb = lambda n, s, d=F32: ctx.enter_context(nc.sbuf_tensor("pj_" + n, s, d))
        ps = lambda n, s, d=F32: ctx.enter_context(nc.psum_tensor("pj_" + n, s, d))
        sem = ctx.enter_context(Semaphores(nc, "pj_"))
        ident = sb("ident", [P, P])
        cos = sb("cos", [P, SEQ])
        sin = sb("sin", [P, SEQ])
        w_qk = sb("w_qk", [P, KC, 4, P])
        w_v = sb("w_v", [P, KC, D])
        m_q = sb("m_q", [P, KC, 2, P])
        m_dkv = sb("m_dkv", [P, KC, P])
        m_k = sb("m_k", [P, 2, P])
        m_v = sb("m_v", [P, D])
        norm1 = sb("norm1", [P, KC])
        lng = sb("lng", [P, 2])
        x = sb("x", [P, 2, SUB, D])
        xn = sb("xn", [P, 2, SUB, D])
        xr = sb("xr", [P, 2, SUB, D])
        stats = sb("stats", [P, SUB, 6])
        spare = sb("spare", [P, 1])
        mv = sb("mv", [P, SUB, 2])
        rs = sb("rs", [P, 4, SUB])
        xnT = sb("xnT", [P, 2, KC, BLK])
        xrT = sb("xrT", [P, 2, KC, BLK])
        lat = sb("lat", [P, SUB, P])
        latn = sb("latn", [P, SUB, P])
        lstats = sb("lstats", [P, SUB, 6])
        lmv = sb("lmv", [P, SUB, 2])
        lrs = sb("lrs", [P, 2, SUB])
        latT = sb("latT", [P, BLK])
        tc = sb("tc", [P, 2, BLK])
        ts = sb("ts", [P, 2, BLK])
        swapped = sb("swapped", [P, 2, BLK])
        rot = sb("rot", [P, 2, BLK])
        rest = sb("rest", [P, 2, BLK])
        parts = sb("parts", [P, 2, PARTS, BLK], BF16)
        val = sb("val", [P, 2, SUB, H * VW])
        pT = ps("pT", [P, 2, BLK])
        pQ = ps("pQ", [P, 4, BLK])
        pV = ps("pV", [P, 2, BLK])

        consts = sem("consts")
        x_in, xn_stored = [sem("x_in0"), sem("x_in1")], [sem("xn_stored0"), sem("xn_stored1")]
        front, swap_done = sem("front"), sem("swap_done")
        scaled, dve, normed, tps, tev = sem("scaled"), sem("dve"), sem("normed"), sem("tps"), sem("tev")
        pair_mm, pair_rot, rotd = sem("pair_mm"), sem("pair_rot"), sem("rotd")
        hi_done, rest_done, mid_done, lo_done = sem("hi"), sem("rest"), sem("mid"), sem("lo")
        stored = [sem("stored0"), sem("stored1")]
        dkv_mm, lat_ev, latn_ready, latT_ready = sem("dkv"), sem("lat_ev"), sem("latn"), sem("latT")
        v_mm, v_ev, ones = sem("v_mm"), sem("v_ev"), sem("ones")
        v_stored = [sem("v_stored0"), sem("v_stored1")]
        var_ready, root_ready, lvar_ready, lroot_ready = sem("var"), sem("root"), sem("lvar"), sem("lroot")
        block = ctx.enter_context(nc.Block())
        NCONST = 11
        PAIRS = 8

        @block.sync
        def _(sp):
            for dst, src in ((ident, "ident"), (cos, "cos"), (sin, "sin"), (w_qk, "w_qk"), (w_v, "w_v"),
                             (m_q, "m_q"), (m_dkv, "m_dkv"), (m_k, "m_k"), (m_v, "m_v"), (norm1, "norm1"),
                             (lng, "lng")):
                sp.dma_start(dst[:], T[src]).then_inc(consts, 16)
            for h in range(2):
                sp.dma_start(x[:, h], T["x"][0, :, SUB * h:SUB * h + SUB, :]).then_inc(x_in[h], 16)

            def turn(b, last):
                for h in range(2):
                    n = 2 * b + h
                    sp.wait_ge(normed, n + 1)
                    if not last:
                        sp.dma_start(x[:, h], T["x"][b + 1, :, SUB * h:SUB * h + SUB, :]).then_inc(x_in[h], 16)
                    sp.dma_start(T["xn"][b, :, SUB * h:SUB * h + SUB, :], xn[:, h]).then_inc(xn_stored[h], 16)
                    for s in range(PAIRS):
                        k, p = PAIRS * n + s, s % 2
                        at, qk, c = s // 4, s // 2 % 2, s % 2
                        sp.wait_ge(lo_done, k + 1)
                        for g2 in range(2):
                            sp.dma_start(
                                T["qk_parts"][at * BATCH + b, 2 * c + g2, qk].rearrange("a r t -> r a t")[
                                    :, :, BLK * h:BLK * h + BLK],
                                parts[64 * g2:64 * g2 + 64, p]).then_inc(stored[p], 16)
                        if s not in (3, 6):
                            continue
                        at = s // 6
                        sp.wait_ge(v_ev, 4 * n + 2 * at + 3)
                        for hg in range(HG):
                            sp.dma_start(
                                T["v_pad"][at * BATCH + b, hg, BLK * h:BLK * h + BLK, :].rearrange(
                                    "(j p) w -> p j w", p=P),
                                val[:, at, :, P * hg:P * hg + P]).then_inc(v_stored[at], 16)

            with sp.Fori(0, BATCH - 1) as b:
                turn(b, False)
            turn(BATCH - 1, True)
            for h in range(2):
                sp.wait_ge(xn_stored[h], 16 * (BATCH + 1))
            for at in range(2):
                sp.wait_ge(v_stored[at], 64 * (2 * BATCH + 1))
            for p in range(2):
                sp.wait_ge(stored[p], 32 * (4 * 2 * BATCH + 1))

        @block.vector
        def _(dve_e):
            v = nc.vector
            for credit, count in ((xn_stored[0], 16), (xn_stored[1], 16), (dkv_mm, 2), (latn_ready, 1),
                                  (latT_ready, 1), (v_ev, 1), (pair_rot, 4), (rotd, 2), (stored[0], 32), (stored[1], 32),
                                  (v_stored[0], 64), (v_stored[1], 64)):
                v.sem_inc(credit, count)

            def statistics(n, h, b):
                step = Steps(dve_e, front, n, 3)
                dve_e.wait_ge(x_in[h], 16 * (b + 1))
                for j in range(SUB):
                    ins = v.bn_stats(stats[:, j], x[:, h, j])
                step(ins)
                v.memset(spare[:], 0.0)
                for j in range(SUB):
                    ins = v.bn_aggr(mv[:, j], stats[:, j])
                step(ins)
                v.tensor_scalar(rs[:, 0], mv[:, :, 1], LN_EPS, None, ALU.add)
                v.tensor_scalar(rs[:, 1], mv[:, :, 1], 1.0 + RMS_EPS, LN_EPS * RMS_EPS, ALU.mult,
                                ALU.add).then_inc(var_ready, 1)
                return step

            def normalised(n, h, b, step):
                dve_e.wait_ge(root_ready, n + 1)
                step(v.reciprocal(rs[:, 0:2], rs[:, 2:4]))
                step.end()
                dve_e.wait_ge(xn_stored[h], 16 * (b + 1))
                dve_e.wait_ge(dkv_mm, n + 1)
                for j in range(SUB):
                    v.tensor_scalar(xn[:, h, j], x[:, h, j], mv[:, j, 0:1], rs[:, 0, j:j + 1],
                                    ALU.subtract, ALU.mult)
                for j in range(SUB):
                    ins = v.tensor_scalar(xr[:, h, j], x[:, h, j], mv[:, j, 0:1], rs[:, 1, j:j + 1],
                                          ALU.subtract, ALU.mult)
                ins.then_inc(normed, 1)

            def pair(n, h, s):
                k, p = PAIRS * n + s, s % 2
                at = BLK * h
                dve_e.wait_ge(pair_mm, k + 1)
                dve_e.wait_ge(rotd, k + 1)
                v.tensor_tensor(tc[:, p], pQ[:, s % 4], cos[:, at:at + BLK], ALU.mult)
                v.stream_shuffle(swapped[:, p], pQ[:, s % 4], [row ^ (HD // 2) for row in range(32)]
                                 ).then_inc(swap_done, 1)
                dve_e.wait_ge(swap_done, k + 1)
                v.tensor_tensor(ts[:, p], swapped[:, p], sin[:, at:at + BLK], ALU.mult).then_inc(pair_rot, 1)

            def latent_norm(n):
                step = Steps(dve_e, dve, n, 3)
                dve_e.wait_ge(lat_ev, n + 1)
                for j in range(SUB):
                    ins = v.bn_stats(lstats[:, j], lat[:, j])
                step(ins)
                v.memset(spare[:], 0.0)
                for j in range(SUB):
                    ins = v.bn_aggr(lmv[:, j], lstats[:, j])
                step(ins)
                v.tensor_scalar(lrs[:, 0], lmv[:, :, 1], LN_EPS, None, ALU.add).then_inc(lvar_ready, 1)
                dve_e.wait_ge(lroot_ready, n + 1)
                step(v.reciprocal(lrs[:, 0], lrs[:, 1]))
                step.end()
                for j in range(SUB):
                    ins = v.tensor_scalar(latn[:, j], lat[:, j], lmv[:, j, 0:1], lrs[:, 0, j:j + 1],
                                          ALU.subtract, ALU.mult)
                ins.then_inc(latn_ready, 1)

            def turn(b, last):
                for h in range(2):
                    n = 2 * b + h
                    more = not (last and h == 1)
                    pair(n, h, 0)
                    latent_norm(n)
                    pair(n, h, 1)
                    if more:
                        step = statistics(n + 1, 1 - h, b + h)
                    pair(n, h, 2)
                    if more:
                        normalised(n + 1, 1 - h, b + h, step)
                    for s in range(3, PAIRS):
                        pair(n, h, s)

            step = statistics(0, 0, 0)
            v.memset(val[:], 1.0).then_inc(ones, 1)
            normalised(0, 0, 0, step)
            dve_e.wait_ge(consts, 16 * NCONST)
            for kc in range(KC):
                v.tensor_scalar(m_q[:, kc], m_q[:, kc], norm1[:, kc:kc + 1], None, ALU.mult).then_inc(scaled, 1)
                v.tensor_scalar(m_dkv[:, kc], m_dkv[:, kc], norm1[:, kc:kc + 1], None,
                                ALU.mult).then_inc(scaled, 1)
            with dve_e.Fori(0, BATCH - 1) as b:
                turn(b, False)
            turn(BATCH - 1, True)

        @block.scalar
        def _(act):
            a = nc.scalar

            def root(n):
                act.wait_ge(var_ready, n + 1)
                a.activation(rs[:, 2:4], rs[:, 0:2], ACT.Sqrt).then_inc(root_ready, 1)

            def turned_rows_out(n, h, which):
                for q in which:
                    act.wait_ge(tps, 5 * n + q + 1)
                    a.activation((xnT, xrT)[q // 2][:, h, q % 2], pT[:, q % 2], ACT.Copy).then_inc(tev, 1)

            def latent(n):
                act.wait_ge(dkv_mm, n + 3)
                act.wait_ge(latn_ready, n + 1)
                a.activation(lat[:], pV[:, 0].rearrange("p (j l) -> p j l", j=SUB),
                             ACT.Copy).then_inc(lat_ev, 1)

            def split(n, s):
                k, p = PAIRS * n + s, s % 2
                act.wait_ge(rotd, k + 3)
                act.wait_ge(stored[p], 32 * (4 * n + s // 2 + 1))
                a.activation(parts[:, p, 0], rot[:, p], ACT.Copy).then_inc(hi_done, 1)
                act.wait_ge(rest_done, k + 1)
                a.activation(parts[:, p, 1], rest[:, p], ACT.Copy).then_inc(mid_done, 1)

            def values(n, at, half):
                act.wait_ge(v_mm, 4 * n + 2 * at + half + 1)
                if half == 0:
                    act.wait_ge(v_stored[at], 64 * (n + 1))
                for j in range(2):
                    ins = a.activation(
                        val[:, at, 2 * half + j].rearrange("p (h w) -> p h w", w=VW)[:, :, 0:HD],
                        pV[:, half, D * j:D * j + D].rearrange("p (h w) -> p h w", w=HD), ACT.Copy)
                ins.then_inc(v_ev, 1)

            def turn(b, last):
                for h in range(2):
                    n = 2 * b + h
                    more = not (last and h == 1)
                    latent(n)
                    act.wait_ge(lvar_ready, n + 1)
                    a.activation(lrs[:, 1], lrs[:, 0], ACT.Sqrt).then_inc(lroot_ready, 1)
                    split(n, 0)
                    values(n, 0, 0)
                    split(n, 1)
                    act.wait_ge(tps, 5 * n + 5)
                    a.activation(latT[:], pT[:, 0], ACT.Identity, bias=lng[:, 1:2],
                                 scale=lng[:, 0:1]).then_inc(latT_ready, 1)
                    if more:
                        root(n + 1)
                    split(n, 2)
                    values(n, 0, 1)
                    split(n, 3)
                    if more:
                        turned_rows_out(n + 1, 1 - h, (0, 1))
                    split(n, 4)
                    values(n, 1, 0)
                    if more:
                        turned_rows_out(n + 1, 1 - h, (2, 3))
                    split(n, 5)
                    values(n, 1, 1)
                    split(n, 6)
                    split(n, 7)

            root(0)
            turned_rows_out(0, 0, range(4))
            act.wait_ge(ones, 1)
            act.wait_ge(consts, 16 * NCONST)
            with act.Fori(0, BATCH - 1) as b:
                turn(b, False)
            turn(BATCH - 1, True)

        @block.gpsimd
        def _(pool):
            g = nc.gpsimd

            def turned(k, p):
                pool.wait_ge(pair_rot, k + 5)
                g.tensor_tensor(rot[:, p], tc[:, p], ts[:, p], ALU.add).then_inc(rotd, 1)

            def turn(b, last):
                for m in range(2 * PAIRS):
                    k, p = 2 * PAIRS * b + m, m % 2
                    pool.wait_ge(hi_done, k + 1)
                    g.tensor_tensor(rest[:, p], rot[:, p], parts[:, p, 0], ALU.subtract).then_inc(rest_done, 1)
                    if not (last and m == 2 * PAIRS - 1):
                        turned(k + 1, 1 - p)
                    pool.wait_ge(mid_done, k + 1)
                    g.tensor_tensor(parts[:, p, 2], rest[:, p], parts[:, p, 1],
                                    ALU.subtract).then_inc(lo_done, 1)

            turned(0, 0)
            with pool.Fori(0, BATCH - 1) as b:
                turn(b, False)
            turn(BATCH - 1, True)

        @block.tensor
        def _(pe):
            t = nc.tensor

            def turn_rows(n, h, which):
                pe.wait_ge(normed, n + 1)
                for q in which:
                    if q < 2:
                        pe.wait_ge(latT_ready, n + 1)
                    else:
                        pe.wait_ge(tev, 4 * n + q - 1)
                    src = xn if q < 2 else xr
                    for j in range(SUB):
                        ins = t.transpose(pT[:, q % 2, P * j:P * j + P],
                                          src[:, h, j, P * (q % 2):P * (q % 2) + P], ident[:])
                    ins.then_inc(tps, 1)

            def latent(n, h):
                pe.wait_ge(tev, 4 * n + 4)
                pe.wait_ge(v_ev, 4 * n + 1)
                for j in range(SUB):
                    for kc in range(KC):
                        ins = t.matmul(pV[:, 0, P * j:P * j + P], xrT[:, h, kc, P * j:P * j + P],
                                       m_dkv[:, kc], start=kc == 0, stop=kc == KC - 1)
                ins.then_inc(dkv_mm, 1)

            def pair(n, h, s):
                k, c = PAIRS * n + s, s % 4
                pe.wait_ge(pair_rot, k + 1)
                if s < 4:
                    ops = [(w_qk[:, kc, c], xnT[:, h, kc]) for kc in range(KC)]
                elif s < 6:
                    ops = [(m_q[:, kc, c], xrT[:, h, kc]) for kc in range(KC)]
                else:
                    ops = [(m_k[:, c - 2], latT[:])]
                for m, (w, r) in enumerate(ops):
                    ins = t.matmul(pQ[:, s % 4], w, r, start=m == 0, stop=m == len(ops) - 1)
                ins.then_inc(pair_mm, 1)

            def values(n, h, at, half):
                if half == 0 and at == 0:
                    pe.wait_ge(lat_ev, n + 1)
                else:
                    pe.wait_ge(v_ev, 4 * n + 2 * at + half)
                for j in range(2):
                    jj = 2 * half + j
                    if at == 0:
                        for kc in range(KC):
                            ins = t.matmul(pV[:, half, D * j:D * j + D],
                                           xnT[:, h, kc, P * jj:P * jj + P], w_v[:, kc],
                                           start=kc == 0, stop=kc == KC - 1)
                    else:
                        ins = t.matmul(pV[:, half, D * j:D * j + D], latT[:, P * jj:P * jj + P],
                                       m_v[:], start=True, stop=True)
                ins.then_inc(v_mm, 1)

            def turn(b, last):
                for h in range(2):
                    n = 2 * b + h
                    more = not (last and h == 1)
                    pair(n, h, 0)
                    pair(n, h, 1)
                    values(n, h, 0, 0)
                    pair(n, h, 2)
                    pe.wait_ge(latn_ready, n + 2)
                    for j in range(SUB):
                        ins = t.transpose(pT[:, 0, P * j:P * j + P], latn[:, j], ident[:])
                    ins.then_inc(tps, 1)
                    values(n, h, 0, 1)
                    pair(n, h, 3)
                    pair(n, h, 4)
                    if more:
                        turn_rows(n + 1, 1 - h, (0, 1))
                    pe.wait_ge(latT_ready, n + 2)
                    values(n, h, 1, 0)
                    pair(n, h, 5)
                    if more:
                        turn_rows(n + 1, 1 - h, (2, 3))
                    values(n, h, 1, 1)
                    pair(n, h, 6)
                    pair(n, h, 7)
                    if more:
                        latent(n + 1, 1 - h)

            pe.wait_ge(consts, 16 * NCONST)
            turn_rows(0, 0, range(4))
            pe.wait_ge(scaled, 2 * KC)
            latent(0, 0)
            with pe.Fori(0, BATCH - 1) as b:
                turn(b, False)
            turn(BATCH - 1, True)


def attention_phase(nc, T, experts):
    with ExitStack() as ctx:
        sb = lambda n, s, d=F32: ctx.enter_context(nc.sbuf_tensor("at_" + n, s, d))
        ps = lambda n, s, d=F32: ctx.enter_context(nc.psum_tensor("at_" + n, s, d))
        sem = ctx.enter_context(Semaphores(nc, "at_"))
        NBUF = 4
        AHEAD = 2
        masks_in = sb("masks_in", [P, 3, P])
        masks = sb("masks", [P, 3, P], BF16)
        ident, mask_q, mask_k = masks[:, 0], masks[:, 1], masks[:, 2]
        qs = sb("qs", [SROWS + MROWS, NBUF, HPG, SEQ], BF16)
        ks = sb("ks", [SROWS + MROWS, NBUF, HPG, SEQ], BF16)
        vs = sb("vs", [P, NBUF, NQT, HPG * VW])
        mp = sb("mp", [P, 2, HPG * NQT])
        mx = sb("mx", [P, HPG * NQT])
        mm = sb("mm", [P, MROWS, HPG * NQT], BF16)
        mt = sb("mt", [MROWS * HPG * NQT, P], BF16)
        w = sb("w", [P, 2, HPG, SEQ])
        zero = sb("zero", [P, SUB * D])
        outg = sb("outg", [P, 2, SEQ])
        pS = ps("pS", [P, 2, BLK])
        pW = ps("pW", [P, 4, BLK])
        pO = ps("pO", [P, SEQ])

        consts, ones = sem("consts"), sem("ones")
        loaded = [sem(f"loaded{u}") for u in range(NBUF)]
        m_in = [sem(f"m_in{u}") for u in range(NBUF)]
        s_mm, s_red, mm_ready, mt_ready, m_out = (sem(n) for n in (
            "s_mm", "s_red", "mm_ready", "mt_ready", "m_out"))
        w_mm, exp_done, pv_mm, dve, out_ready = (sem(n) for n in ("w_mm", "exp", "pv_mm", "dve", "out_ready"))
        zeroed, cleared = sem("zeroed"), sem("cleared")
        out_stored = [sem("out_stored0"), sem("out_stored1")]
        block = ctx.enter_context(nc.Block())

        key_width = lambda qt, c: min(BLK, P * (qt + 1) - BLK * c)
        PIECES = [(range(h, h + BLK // key_width(qt, c)), qt, c) for qt in range(NQT)
                  for c in range((qt + 4) // 4) for h in range(0, HPG, BLK // key_width(qt, c))]
        SPREAD = 1.1
        FIXED = 128
        SPENT = [0]
        for heads, qt, c in PIECES:
            SPENT.append(SPENT[-1] + len(heads) * key_width(qt, c) + FIXED)
        COLUMNS = HPG * (2 * P * NQT * (NQT + 1) // 2 + P * NQT)
        NP = len(PIECES) + 2
        NW = NQT * HPG
        LOADS = 2 * len(SPLIT) + 1
        STORES = 2 * HPG
        TURNS = GROUPS // NBUF

        def banks(kt, h):
            e = HPG * kt + h
            if kt < NQT // 2:
                return 2 * (e % 2), 2, (3 if e == 0 else 2)
            return e % 4, 1, min(4, 2 + (e - NW // 2 + 1) // 2)

        def groups(eng, body):
            with eng.Fori(0, TURNS - 1) as i:
                for u in range(NBUF):
                    body(NBUF * i + u, u, i, False)
            for u in range(NBUF):
                body(NBUF * (TURNS - 1) + u, u, TURNS - 1, True)

        @block.sync
        def _(sp):
            sp.dma_start(masks_in[:], T["masks"]).then_inc(consts, 16)
            parts = T["qk_parts"].rearrange("a g q p r t -> (a g) q p r t")
            vals = T["v_pad"].rearrange("a g t w -> (a g) t w")
            att = T["att"].rearrange("s c (x j d) t -> (s c x) j d t", j=HPG, d=HD)

            def load(g, u):
                for n, which in enumerate(SPLIT):
                    for side, dst in enumerate((qs, ks)):
                        sp.dma_start(dst[HD * n:HD * n + HD, u],
                                     parts[g, side, which[side]].rearrange("(h d) t -> d h t", d=HD)
                                     ).then_inc(loaded[u], 16)
                sp.dma_start(vs[:, u], vals[g].rearrange("(k p) w -> p k w", p=P)).then_inc(loaded[u], 16)

            def send_maxima(g, u):
                sp.wait_ge(mt_ready, g + 1)
                sp.dma_start(T["m_rows"][g].rearrange("m (a t) -> (m a) t", t=P), mt[:]).then_inc(m_out, 16)
                sp.wait_ge(m_out, 16 * (g + 2))
                sp.dma_start(qs[SROWS:SROWS + MROWS, u], T["m_rows"][g].rearrange("m (h t) -> m h t", h=HPG)
                             ).then_inc(m_in[u], 16)

            def send_out(g, u):
                sp.wait_ge(out_ready, g + 2)
                for j in range(HPG):
                    sp.dma_start(att[g, j], outg[VW * j:VW * j + HD, u % 2]).then_inc(out_stored[u % 2], 16)
                    sp.dma_start(T["sums"][g, j:j + 1], outg[VW * j + HD:VW * j + HD + 1, u % 2]
                                 ).then_inc(out_stored[u % 2], 16)

            for u in range(NBUF - 1):
                load(u, u)
            sp.wait_ge(zeroed, 1)
            clears = 0
            for table in (T["a_sorted"], T["b_sorted"]):
                rows = table.rearrange("(n p j) d -> n p (j d)", p=P, j=SUB)
                for n in range(rows.shape[0]):
                    sp.dma_start(rows[n], zero[:]).then_inc(cleared, 16)
                    clears += 1
            for u in range(AHEAD):
                send_maxima(u, u)

            def body(g, u, i, last):
                if not last or u + NBUF - 1 < NBUF:
                    sp.wait_ge(pv_mm, NQT * g + 2)
                    load(g + NBUF - 1, (u + NBUF - 1) % NBUF)
                if not last or u + AHEAD < NBUF:
                    send_maxima(g + AHEAD, (u + AHEAD) % NBUF)
                send_out(g, u)

            groups(sp, body)
            for p in range(2):
                sp.wait_ge(out_stored[p], 16 * STORES * (GROUPS // 2 + 1))
            sp.wait_ge(cleared, 16 * clears)

        @block.vector
        def _(dve_e):
            v = nc.vector
            for credit, count in ((exp_done, 4), (pv_mm, 2), (out_stored[0], 16 * STORES),
                                  (out_stored[1], 16 * STORES), (s_red, 2), (out_ready, 1), (m_out, 16)):
                v.sem_inc(credit, count)
            v.memset(zero[:], 0.0).then_inc(zeroed, 1)
            v.memset(ks[SROWS:SROWS + MROWS], 1.0).then_inc(ones, 1)
            v.memset(mp[:], -3.0e38).then_inc(ones, 1)
            dve_e.wait_ge(ones, 2)
            dve_e.wait_ge(consts, 16)
            v.tensor_copy(masks[:], masks_in[:]).then_inc(ones, 1)

            def maxima(g):
                for n, (heads, qt, c) in enumerate(PIECES):
                    width = key_width(qt, c)
                    dve_e.wait_ge(s_mm, NP * g + n + 1)
                    v.tensor_reduce(mp[:, c, :].rearrange("p (h q) -> p h q", q=NQT)[:, heads[0]:heads[-1] + 1, qt],
                                    pS[:, n % 2, 0:len(heads) * width].rearrange("p (h t) -> p h t", t=width),
                                    AX.X, ALU.max).then_inc(s_red, 1)
                dve_e.wait_ge(s_red, NP * g + len(PIECES) + 2)
                step = Steps(dve_e, dve, g, 2)
                step(v.tensor_tensor(mx[:], mp[:, 0], mp[:, 1], ALU.max))
                step(v.tensor_scalar(mm[:, 0], mx[:], -1.0, None, ALU.mult))
                v.scalar_tensor_tensor(mm[:, 1], mx[:], -1.0, mm[:, 0], ALU.mult,
                                       ALU.subtract).then_inc(mm_ready, 1)
                dve_e.wait_ge(s_mm, NP * g + NP)
                dve_e.wait_ge(m_out, 16 * (g + 1))
                v.tensor_copy(mt[:], pS[0:MROWS * HPG * NQT, len(PIECES) % 2, 0:P // 2].bitcast(BF16)
                              ).then_inc(mt_ready, 1)
                dve_e.wait_ge(mt_ready, g + 1)
                v.sem_inc(s_red, 2)

            for u in range(AHEAD):
                maxima(u)

            def body(g, u, i, last):
                if not last or u + AHEAD < NBUF:
                    maxima(g + AHEAD)
                dve_e.wait_ge(pv_mm, NQT * (g + 1) + 2)
                dve_e.wait_ge(out_stored[u % 2], 16 * STORES * (2 * i + u // 2 + 1))
                v.tensor_copy(outg[:, u % 2], pO[:]).then_inc(out_ready, 1)

            groups(dve_e, body)

        @block.scalar
        def _(act):
            a = nc.scalar
            scale = 1.0 / math.sqrt(HD)
            act.wait_ge(loaded[0], 16 * LOADS)
            experts.load(act)

            def body(g, u, i, last):
                for kt in range(NQT):
                    act.wait_ge(pv_mm, NQT * g + kt + 1)
                    for h in range(HPG):
                        e = HPG * kt + h
                        act.wait_ge(w_mm, NW * g + e + 1)
                        first, count, _ = banks(kt, h)
                        a.activation(w[:, kt % 2, h, 0:SEQ - P * kt],
                                     pW[:, first:first + count].rearrange("p b t -> p (b t)")[:, 0:SEQ - P * kt],
                                     ACT.Exp, scale=scale).then_inc(exp_done, 1)

            groups(act, body)

        @block.tensor
        def _(pe):
            t = nc.tensor
            pe.wait_ge(ones, 3)

            def score(g, u, n):
                heads, qt, c = PIECES[n]
                width = key_width(qt, c)
                diagonal = c == qt // 4
                pe.wait_ge(s_red, NP * g + n + 1)
                for m, h in enumerate(heads):
                    ins = t.matmul(pS[:, n % 2, width * m:width * m + width],
                                   qs[0:SROWS, u, h, P * qt:P * qt + P],
                                   ks[0:SROWS, u, h, BLK * c:BLK * c + width], start=True, stop=not diagonal)
                    if diagonal:
                        ins = t.matmul(pS[:, n % 2, width * m + width - P:width * m + width], ident, mask_q,
                                       start=False, stop=True)
                ins.then_inc(s_mm, 1)

            def turn_maxima(g):
                n = len(PIECES)
                pe.wait_ge(s_red, NP * g + n + 1)
                pe.wait_ge(mm_ready, g + 1)
                t.transpose(pS[0:MROWS * HPG * NQT, n % 2, 0:P // 2].bitcast(BF16),
                            mm[:].rearrange("p m a -> p (m a)"), ident).then_inc(s_mm, 2)

            def weigh(g, u, kt, h, fill):
                e = HPG * kt + h
                bank, _, back = banks(kt, h)
                pe.wait_ge(exp_done, NW * g + e + 1 + 4 - back)
                at = P * kt
                keys = ks[:, u, h, at:at + P]
                first = min(BLK, SEQ - at)
                t.matmul(pW[:, bank, 0:first], keys, qs[:, u, h, at:at + first], start=True, stop=False)
                ins = t.matmul(pW[:, bank, 0:P], ident, mask_k, start=False, stop=True)
                if at + first < SEQ:
                    fill(first + P)
                    ins = t.matmul(pW[:, bank + 1, 0:SEQ - at - first], keys, qs[:, u, h, at + first:SEQ],
                                   start=True, stop=True)
                ins.then_inc(w_mm, 1)
                fill(SEQ - at - first if at + first < SEQ else first + P)

            def values(g, u, kt, fill):
                pe.wait_ge(exp_done, NW * g + HPG * (kt + 1) + 4)
                if kt == 0:
                    pe.wait_ge(out_ready, g + 1)
                at = P * kt
                for lo, hi in ((at, BLK), (max(BLK, at), SEQ)):
                    if lo >= hi:
                        continue
                    for h in range(HPG):
                        ins = t.matmul(pO[VW * h:VW * h + VW, lo:hi], vs[:, u, kt, VW * h:VW * h + VW],
                                       w[:, kt % 2, h, lo - at:hi - at], start=kt == 0,
                                       stop=kt == (3 if hi == BLK else NQT - 1))
                    if hi == SEQ:
                        ins.then_inc(pv_mm, 1)
                    fill(HPG * (hi - lo))

            for u in range(AHEAD):
                pe.wait_ge(loaded[u], 16 * LOADS)
                for n in range(len(PIECES)):
                    score(u, u, n)
                turn_maxima(u)

            def body(g, u, i, last):
                ahead = not last or u + AHEAD < NBUF
                ua = (u + AHEAD) % NBUF
                if ahead:
                    pe.wait_ge(loaded[ua], 16 * LOADS * (i + 1 + (u + AHEAD) // NBUF))
                pe.wait_ge(m_in[u], 16 * (i + 1))
                done = [0, 0]

                def fill(columns):
                    done[1] += columns
                    while ahead and done[0] < len(PIECES) and (
                            SPENT[done[0]] < SPREAD * SPENT[-1] * done[1] / COLUMNS):
                        score(g + AHEAD, ua, done[0])
                        done[0] += 1

                for kt in range(NQT + 1):
                    if kt < NQT:
                        for h in range(HPG):
                            weigh(g, u, kt, h, fill)
                    if kt > 0:
                        values(g, u, kt - 1, fill)
                assert not ahead or done[0] == len(PIECES)
                if ahead:
                    turn_maxima(g + AHEAD)

            groups(pe, body)


def route_phase(nc, T, E, K, pre, send):
    NT = expert_tiles(E, K)
    NCH = TILES * K
    with ExitStack() as ctx:
        sb = lambda n, s, d=F32: ctx.enter_context(nc.sbuf_tensor(f"{pre}rt_" + n, s, d))
        sem = ctx.enter_context(Semaphores(nc, f"{pre}rt_"))
        before = sb("before", [P, P])
        ones = sb("ones", [P, P])
        iota_e = sb("iota_e", [P, E])
        iota_t = sb("iota_t", [P, NT])
        choice = sb("choice", [P, NCH])
        rows = sb("rows", [P, TILES, D]) if send else None
        hot = sb("hot", [P, NCH, E])
        total = sb("total", [P, NCH, E])
        upto = sb("upto", [P, NCH, E])
        rank = sb("rank", [P, NCH, E])
        zeros = sb("zeros", [P, NCH])
        count = sb("count", [P, E])
        counti = sb("counti", [P, E], I32)
        ntile = sb("ntile", [P, E])
        end = sb("end", [P, E])
        base = sb("base", [P, E])
        slot = sb("slot", [P, NCH])
        sloti = sb("sloti", [P, NCH], I32)
        ge = sb("ge", [P, NT, E])
        te = sb("te", [P, NT])
        tei = sb("tei", [P, NT], I32)
        pC = ctx.enter_context(nc.psum_tensor(f"{pre}rt_pC", [P, NCH, E], F32))
        pN = ctx.enter_context(nc.psum_tensor(f"{pre}rt_pN", [P, NCH, E], F32))
        loaded, hot_ready, counted, dve = sem("loaded"), sem("hot"), sem("counted"), sem("dve")
        slots_ready, rows_in, stored = sem("slots"), sem("rows_in"), sem("stored")
        sent = sem("sent") if send else None
        block = ctx.enter_context(nc.Block())

        @block.sync
        def _(sp):
            for dst, src in ((before, "before"), (ones, "ones"), (choice, pre + "choice")):
                sp.dma_start(dst[:], T[src]).then_inc(loaded, 16)
            sp.dma_start(iota_e[:], T["iota"][:, 0:E]).then_inc(loaded, 16)
            sp.dma_start(iota_t[:], T["iota"][:, 0:NT]).then_inc(loaded, 16)
            if send:
                sp.dma_start(rows[:], T[pre + "rows"]).then_inc(rows_in, 16)
            sp.wait_ge(slots_ready, 1)
            sp.dma_start(T[pre + "slots"], sloti[:]).then_inc(stored, 16)
            sp.dma_start(T[pre + "tile_expert"], tei[0:1, :]).then_inc(stored, 16)
            sp.wait_ge(stored, 32)

        @block.tensor
        def _(pe):
            pe.wait_ge(hot_ready, 1)
            flat = lambda a: a.rearrange("p c e -> p (c e)")
            nc.tensor.matmul(flat(pC[:]), before[:], flat(hot[:]), start=True, stop=True)
            nc.tensor.matmul(flat(pN[:]), ones[:], flat(hot[:]), start=True, stop=True).then_inc(counted, 1)

        @block.vector
        def _(dve_e):
            v = nc.vector
            step = Steps(dve_e, dve)
            dve_e.wait_ge(loaded, 16 * 5)
            step(v.memset(zeros[:], 0.0))
            v.tensor_tensor(hot[:], iota_e[:].unsqueeze(1).to_broadcast([P, NCH, E]),
                            choice[:].unsqueeze(2).to_broadcast([P, NCH, E]),
                            ALU.is_equal).then_inc(hot_ready, 1)
            dve_e.wait_ge(counted, 1)
            step(v.tensor_copy(total[:], pN[:]))
            for e in range(E):
                ins = v.tensor_tensor_scan(upto[:, :, e], total[:, :, e], zeros[:], 0.0, ALU.add, ALU.add)
            step(ins)
            step(v.tensor_scalar(count[:], upto[:, NCH - 1, :], float(P - 1), None, ALU.add))
            step(v.tensor_copy(counti[:], count[:]))
            step(v.tensor_scalar(counti[:], counti[:], P.bit_length() - 1, None, ALU.logical_shift_right))
            step(v.tensor_copy(ntile[:], counti[:]))
            step(v.tensor_tensor_scan(end[:], ntile[:], zeros[:, 0:E], 0.0, ALU.add, ALU.add))
            step(v.tensor_tensor(base[:], end[:], ntile[:], ALU.subtract))
            step(v.tensor_scalar(base[:], base[:], float(P), None, ALU.mult))
            step(v.tensor_tensor(rank[:], upto[:], total[:], ALU.subtract))
            step(v.tensor_tensor(rank[:], rank[:], pC[:], ALU.add))
            step(v.tensor_tensor(rank[:], rank[:], base[:].unsqueeze(1).to_broadcast([P, NCH, E]), ALU.add))
            step(v.tensor_tensor(rank[:], rank[:], hot[:], ALU.mult))
            step(v.tensor_reduce(slot[:], rank[:], AX.X, ALU.add))
            step(v.tensor_copy(sloti[:], slot[:]))
            step(v.tensor_tensor(ge[:], iota_t[:].unsqueeze(2).to_broadcast([P, NT, E]),
                                 end[:].unsqueeze(1).to_broadcast([P, NT, E]), ALU.is_ge))
            step(v.tensor_reduce(te[:], ge[:], AX.X, ALU.add))
            step(v.tensor_scalar(te[:], te[:], float(E - 1), None, ALU.min))
            v.tensor_copy(tei[:], te[:]).then_inc(slots_ready, 1)

        if send:
            @block.gpsimd
            def _(pool):
                pool.wait_ge(rows_in, 16)
                pool.wait_ge(slots_ready, 1)
                for t in range(TILES):
                    for k in range(K):
                        c = K * t + k
                        nc.gpsimd.indirect_dma_start(
                            out=T[pre + "sorted"], in_=rows[:, t, :], in_offset=None,
                            out_offset=bass.IndirectOffsetOnAxis(ap=sloti[:, c:c + 1], axis=0)).then_inc(sent, 16)
                pool.wait_ge(sent, 16 * NCH)


class ExpertWeights:

    def __init__(self, nc, ctx, T, E, pre):
        sem = ctx.enter_context(Semaphores(nc, f"{pre}w_"))
        self.T, self.E, self.pre = T, E, pre
        self.w1 = ctx.enter_context(nc.sbuf_tensor(f"{pre}held_w1", [P, E, KC, HID], F32))
        self.w2 = ctx.enter_context(nc.sbuf_tensor(f"{pre}held_w2", [P, E, HC, D], F32))
        self.loaded = sem("loaded")
        self.all_loaded = 16 * 2 * E

    def load(self, queue):
        for e in range(self.E):
            queue.dma_start(self.w1[:, e], self.T[self.pre + "w1"][e]).then_inc(self.loaded, 16)
            queue.dma_start(self.w2[:, e], self.T[self.pre + "w2"][e]).then_inc(self.loaded, 16)


class ExpertTiles:

    def __init__(self, nc, ctx, sem, T, E, K, pre, weights, func):
        sb = lambda n, s, d=F32: ctx.enter_context(nc.sbuf_tensor(f"{pre}ex_" + n, s, d))
        ps = lambda n, s, d=F32: ctx.enter_context(nc.psum_tensor(f"{pre}ex_" + n, s, d))
        self.nc, self.T, self.E, self.pre, self.func, self.weights = nc, T, E, pre, func, weights
        self.NT = expert_tiles(E, K)
        self.ident = sb("ident", [P, P])
        self.wnorm = sb("wnorm", [P, KC])
        self.tile_expert = sb("tile_expert", [1, self.NT], I32)
        self.brow = sb("brow", [E * PARTS, NB], BF16)
        self.pick_in = sb("pick_in", [E * PARTS, E])
        self.pick = sb("pick", [E * PARTS, E, P], BF16)
        self.xs = sb("xs", [P, 2, D])
        self.xsT = sb("xsT", [P, D])
        self.h = sb("h", [P, HID])
        self.hT = sb("hT", [P, HID])
        self.y = sb("y", [P, 2, D])
        self.pX = ps("pX", [P, BLK])
        self.pH = ps("pH", [P, HID])
        self.pT = ps("pT", [P, HID])
        self.pY = ps("pY", [P, 2, BLK])
        self.consts, self.ready = sem("consts"), sem("ready")
        self.x_in = [sem("x_in0"), sem("x_in1")]
        self.y_out = [sem("y_out0"), sem("y_out1")]
        self.xt, self.xt_ev, self.hm, self.gated, self.ht, self.ht_ev, self.ym, self.y_ev = (
            sem(n) for n in ("xt", "xt_ev", "hm", "gated", "ht", "ht_ev", "ym", "y_ev"))
        self.tiles_in = T[pre + "sorted"].rearrange("(n p) d -> n p d", p=P)
        self.tiles_out = T[pre + "y"].rearrange("(n p) d -> n p d", p=P)

    def load_tables(self, sp):
        T, pre = self.T, self.pre
        for dst, src in ((self.ident, T["ident"]), (self.tile_expert, T[pre + "tile_expert"]),
                         (self.wnorm, T[pre + "wnorm"]), (self.pick_in, T[pre + "pick"]),
                         (self.brow, T[pre + "bparts"].rearrange("e s n -> (e s) n"))):
            sp.dma_start(dst[:], src).then_inc(self.consts, 16)
        for u in range(2):
            sp.dma_start(self.xs[:, u], self.tiles_in[u]).then_inc(self.x_in[u], 16)

    def load_rows(self, sp, n, u):
        sp.wait_ge(self.xt, n + 1)
        sp.dma_start(self.xs[:, u], self.tiles_in[n + 2]).then_inc(self.x_in[u], 16)

    def store_result(self, sp, n, u):
        sp.wait_ge(self.y_ev, n + 1 + 2)
        sp.dma_start(self.tiles_out[n], self.y[:, u]).then_inc(self.y_out[u], 16)

    def stored(self, sp):
        for u in range(2):
            sp.wait_ge(self.y_out[u], 16 * (self.NT // 2 + 1))

    def prepare(self, dve_e):
        v = self.nc.vector
        for credit, count in ((self.xt_ev, 1), (self.y_ev, 2), (self.y_out[0], 16), (self.y_out[1], 16),
                              (self.gated, 1), (self.ht_ev, 1), (self.ym, 1), (self.ht, 1)):
            v.sem_inc(credit, count)
        dve_e.wait_ge(self.consts, 16 * 5)
        v.tensor_copy(self.pick[:], self.pick_in[:].unsqueeze(2).to_broadcast(
            [self.E * PARTS, self.E, P])).then_inc(self.ready, 1)

    def scale_weights(self, dve_e):
        w = self.weights
        dve_e.wait_ge(w.loaded, w.all_loaded)
        for e in range(self.E):
            for kc in range(KC):
                ins = self.nc.vector.tensor_scalar(w.w1[:, e, kc], w.w1[:, e, kc],
                                                   self.wnorm[:, kc:kc + 1], None, ALU.mult)
        ins.then_inc(self.ready, 1)

    def rows_turned(self, dve_e, n):
        dve_e.wait_ge(self.xt, n + 1)
        self.nc.vector.tensor_copy(self.xsT[:], self.pX[:, 0:D]).then_inc(self.xt_ev, 1)

    def hidden_turned(self, dve_e, n):
        dve_e.wait_ge(self.ht, n + 2)
        self.nc.vector.tensor_copy(self.hT[:], self.pT[:]).then_inc(self.ht_ev, 1)

    def result(self, dve_e, n, u, pairs):
        dve_e.wait_ge(self.ym, n + 2)
        dve_e.wait_ge(self.y_out[u], 16 * (pairs + 1))
        self.nc.vector.tensor_copy(self.y[:, u], self.pY[:, u, 0:D]).then_inc(self.y_ev, 1)

    def gate(self, act, n):
        act.wait_ge(self.hm, n + 1)
        self.nc.scalar.activation(self.h[:], self.pH[:], self.func).then_inc(self.gated, 1)

    def products(self, pe, scaled):
        t, w = self.nc.tensor, self.weights
        pe.wait_ge(self.consts, 16 * 5)
        pe.wait_ge(w.loaded, w.all_loaded)
        pe.wait_ge(self.ready, 2 if scaled else 1)

        def rows(n, pairs, u):
            pe.wait_ge(self.x_in[u], 16 * (pairs + 1))
            pe.wait_ge(self.xt_ev, n + 1)
            for kc in range(KC):
                ins = t.transpose(self.pX[:, P * kc:P * kc + P], self.xs[:, u, P * kc:P * kc + P], self.ident[:])
            ins.then_inc(self.xt, 1)

        def up(n):
            e = pe.value_load(self.tile_expert[0:1, bass.ds(n, 1)], min_val=0, max_val=self.E - 1)
            pe.wait_ge(self.xt_ev, n + 2)
            pe.wait_ge(self.gated, n + 1)
            for c in range(2):
                out = self.pH[:, BLK * c:BLK * c + BLK]
                t.matmul(out, self.pick[:, e], self.brow[:, BLK * c:BLK * c + BLK], start=True, stop=False)
                for kc in range(KC):
                    ins = t.matmul(out, self.xsT[:, P * kc:P * kc + P], w.w1[:, e, kc, BLK * c:BLK * c + BLK],
                                   start=False, stop=kc == KC - 1)
            ins.then_inc(self.hm, 1)

        def turn_hidden(n):
            pe.wait_ge(self.gated, n + 2)
            pe.wait_ge(self.ht_ev, n + 1)
            for c in range(HC):
                ins = t.transpose(self.pT[:, P * c:P * c + P], self.h[:, P * c:P * c + P], self.ident[:])
            ins.then_inc(self.ht, 1)

        def down(n, u):
            e = pe.value_load(self.tile_expert[0:1, bass.ds(n, 1)], min_val=0, max_val=self.E - 1)
            pe.wait_ge(self.ht_ev, n + 2)
            pe.wait_ge(self.y_ev, n + 1)
            t.matmul(self.pY[:, u, 0:D], self.pick[:, e], self.brow[:, HID:NB], start=True, stop=False)
            for c in range(HC):
                ins = t.matmul(self.pY[:, u, 0:D], self.hT[:, P * c:P * c + P], w.w2[:, e, c], start=False,
                               stop=c == HC - 1)
            ins.then_inc(self.ym, 1)

        def turn(i, last):
            for u in range(2):
                n = 2 * i + u
                turn_hidden(n)
                if not (last and u == 1):
                    up(n + 1)
                if not last:
                    rows(n + 2, i + 1, u)
                down(n, u)

        rows(0, 0, 0)
        up(0)
        rows(1, 0, 1)
        with pe.Fori(0, self.NT // 2 - 1) as i:
            turn(i, False)
        turn(self.NT // 2 - 1, True)


def experts_phase(nc, T, E, K, pre, func, weights):
    with ExitStack() as ctx:
        sem = ctx.enter_context(Semaphores(nc, f"{pre}ex_"))
        tiles = ExpertTiles(nc, ctx, sem, T, E, K, pre, weights, func)
        PAIRS = tiles.NT // 2
        block = ctx.enter_context(nc.Block())

        @block.sync
        def _(sp):
            tiles.load_tables(sp)

            def turn(i, last):
                for u in range(2):
                    if not last:
                        tiles.load_rows(sp, 2 * i + u, u)
                    tiles.store_result(sp, 2 * i + u, u)

            with sp.Fori(0, PAIRS - 1) as i:
                turn(i, False)
            turn(PAIRS - 1, True)
            tiles.stored(sp)

        @block.vector
        def _(dve_e):
            tiles.prepare(dve_e)
            tiles.scale_weights(dve_e)
            for n in range(2):
                tiles.rows_turned(dve_e, n)

            def turn(i, last):
                for u in range(2):
                    n = 2 * i + u
                    tiles.hidden_turned(dve_e, n)
                    if not last:
                        tiles.rows_turned(dve_e, n + 2)
                    tiles.result(dve_e, n, u, i)

            with dve_e.Fori(0, PAIRS - 1) as i:
                turn(i, False)
            turn(PAIRS - 1, True)

        @block.scalar
        def _(act):
            with act.Fori(0, PAIRS) as i:
                for u in range(2):
                    tiles.gate(act, 2 * i + u)

        @block.tensor
        def _(pe):
            tiles.products(pe, True)


def bias_parts_phase(nc, T):
    with ExitStack() as ctx:
        sb = lambda n, s, d=F32: ctx.enter_context(nc.sbuf_tensor("bp_" + n, s, d))
        sem = ctx.enter_context(Semaphores(nc, "bp_"))
        loaded, dve, stored = sem("loaded"), sem("dve"), sem("stored")
        tables = [(pre, sb(pre + "bias", [E, NB]), sb(pre + "parts", [E, PARTS, NB], BF16))
                  for pre, E in (("a_", E0), ("b_", E1))]
        block = ctx.enter_context(nc.Block())

        @block.sync
        def _(sp):
            for pre, bias, parts in tables:
                sp.dma_start(bias[:], T[pre + "bias"]).then_inc(loaded, 16)
            for n, (pre, bias, parts) in enumerate(tables):
                sp.wait_ge(dve, 5 * (n + 1))
                sp.dma_start(T[pre + "bparts"], parts[:]).then_inc(stored, 16)
            sp.wait_ge(stored, 32)

        @block.vector
        def _(dve_e):
            v = nc.vector
            step = Steps(dve_e, dve)
            dve_e.wait_ge(loaded, 32)
            for pre, bias, parts in tables:
                step(v.tensor_copy(parts[:, 0], bias[:]))
                step(v.tensor_tensor(bias[:], bias[:], parts[:, 0], ALU.subtract))
                step(v.tensor_copy(parts[:, 1], bias[:]))
                step(v.tensor_tensor(bias[:], bias[:], parts[:, 1], ALU.subtract))
                step(v.tensor_copy(parts[:, 2], bias[:]))


def denominators_phase(nc, T):
    with ExitStack() as ctx:
        den = ctx.enter_context(nc.sbuf_tensor("dn_den", [P, SEQ], F32))
        sem = ctx.enter_context(Semaphores(nc, "dn_"))
        loaded, ready, stored = sem("in"), sem("ready"), sem("out")
        block = ctx.enter_context(nc.Block())

        @block.sync
        def _(sp):
            sp.dma_start(den[:], T["sums"].rearrange("g j t -> (g j) t")).then_inc(loaded, 16)
            sp.wait_ge(ready, 1)
            sp.dma_start(T["rden"].rearrange("g j t -> (g j) t"), den[:]).then_inc(stored, 16)
            sp.wait_ge(stored, 16)

        @block.vector
        def _(dve_e):
            dve_e.wait_ge(loaded, 16)
            nc.vector.reciprocal(den[:], den[:]).then_inc(ready, 1)


def mix_phase(nc, T, second, experts=None):
    E, K, pre = (E1, K1, "b_") if second else (E0, K0, "a_")
    NBLK = TOK // BLK
    with ExitStack() as ctx:
        sb = lambda n, s, d=F32: ctx.enter_context(nc.sbuf_tensor(f"{pre}mx_" + n, s, d))
        ps = lambda n, s, d=F32: ctx.enter_context(nc.psum_tensor(f"{pre}mx_" + n, s, d))
        sem = ctx.enter_context(Semaphores(nc, f"{pre}mx_"))
        ident = sb("ident", [P, P])
        gate = sb("gate", [P, KC, 8])
        gnorm = sb("gnorm", [P, KC])
        gbias = sb("gbias", [P, 8])
        if second:
            slots = sb("slots", [P, TILES], I32)
            moe = sb("moe", [P, TILES, D])
            base_in = sb("base_in", [P, 2, SUB, D])
        else:
            wo = sb("wo", [P, 2, KC, D])
            att = sb("att", [P, 2, 2, KC, BLK])
            rden = sb("rden", [P, 2, 2, KC, BLK])
            xn = sb("xn", [P, 2, SUB, D])
            x = sb("x", [P, 2, SUB, D])
            sumx = sb("sumx", [P, 2, SUB, D])
            x2 = sb("x2", [P, 2, SUB, D])
            pM = ps("pM", [P, 2, 2, BLK])
        base = sb("base", [P, 2, SUB, D])
        rows = sb("rows", [P, 2, SUB, D])
        stats = sb("stats", [P, SUB, 6])
        spare = sb("spare", [P, 1])
        mv = sb("mv", [P, SUB, 2])
        rs = sb("rs", [P, 3, SUB])
        rowsT = sb("rowsT", [P, KC, BLK])
        logits = sb("logits", [P, SUB, 8])
        top = sb("top", [P, SUB, 8])
        topi = sb("topi", [P, SUB, 8], U32)
        choice = sb("choice", [P, TILES, K])
        gap = sb("gap", [P, TILES])
        weights = sb("weights", [P, K, TILES])
        pT = ps("pT", [P, KC, BLK])
        pL = ps("pL", [P, SUB, 8])
        consts, norms, gates, last_steps, scaled = (sem(n) for n in (
            "consts", "norms", "gates", "last_steps", "scaled"))
        in_att, in_x = [sem("in_att0"), sem("in_att1")], [sem("in_x0"), sem("in_x1")]
        in_rden = [sem("in_rden0"), sem("in_rden1")]
        in_moe, norm0, norm1, mm = (sem(n) for n in ("in_moe", "norm0", "norm1", "mm"))
        x2_done, copied, summed, base_ready = sem("x2"), sem("copied"), sem("summed"), sem("base")
        var_ready, root_ready, rows_ready = sem("var"), sem("root"), sem("rows")
        turned, turned_ev, lm, top_ready = sem("turned"), sem("turned_ev"), sem("lm"), sem("top")
        stored, rows_st = [sem("stored0"), sem("stored1")], [sem("rows_st0"), sem("rows_st1")]
        uT_st, exp_out, final = sem("uT_st"), sem("exp_out"), sem("final")
        gathered = [sem("gathered0"), sem("gathered1")] if second else None
        block = ctx.enter_context(nc.Block())
        NCONST = 5

        def blocks(eng, body):
            with eng.Fori(0, NBLK // 2 - 1) as i:
                for u in range(2):
                    body(2 * i + u, u, i, True)
            for u in range(2):
                body(NBLK - 2 + u, u, NBLK // 2 - 1, False)

        @block.sync
        def _(sp):
            for dst, src in ((ident, "ident"), (gate, pre + "gate"), (gnorm, pre + "gnorm"),
                             (gbias, pre + "gbias"), (slots, "a_slots") if second else (wo, "wo")):
                sp.dma_start(dst[:], T[src]).then_inc(consts, 16)
            heads = T["att"].rearrange("(a b) c p t -> b p a c t", a=2)
            sums = T["rden"].rearrange("(a b c x) j t -> b a c (x j) t", a=2, b=BATCH, c=KC)

            def load_att(b, u):
                for a in range(2):
                    sp.dma_start(att[:, u, a], heads[b, :, a, :, BLK * u:BLK * u + BLK]).then_inc(in_att[u], 16)

            def load_rden(b, u):
                for a in range(2):
                    for kc in range(KC):
                        src = sums[b, a, kc, :, BLK * u:BLK * u + BLK].unsqueeze(1)
                        sp.dma_start(rden[:, u, a, kc], src.to_broadcast([H // KC, HD, BLK])
                                     ).then_inc(in_rden[u], 16)

            def load_x(b, u):
                if second:
                    sp.dma_start(base_in[:, u], T["base"][:, bass.ds(2 * SUB * b + SUB * u, SUB), :]
                                 ).then_inc(in_x[u], 16)
                    return
                sp.dma_start(xn[:, u], T["xn"][b, :, SUB * u:SUB * u + SUB, :]).then_inc(in_x[u], 16)
                sp.dma_start(x[:, u], T["x"][b, :, SUB * u:SUB * u + SUB, :]).then_inc(in_x[u], 16)

            for u in range(2):
                if not second:
                    load_att(0, u)
                    load_rden(0, u)
                load_x(0, u)

            def store_base(n, u):
                sp.wait_ge(base_ready, n + 1 + 2)
                sp.dma_start(T["res" if second else "base"][:, bass.ds(SUB * n, SUB), :], base[:, u]
                             ).then_inc(stored[u], 16)

            def store_rows(n, u):
                sp.wait_ge(rows_ready, n + 1)
                sp.dma_start(T[pre + "rows"][:, bass.ds(SUB * n, SUB), :], rows[:, u]).then_inc(rows_st[u], 16)

            def body(n, u, i, more):
                store_base(n, u)
                if more:
                    load_x(i + 1, u)
                store_rows(n, u)
                sp.wait_ge(turned_ev, 2 * n + 2 + 2)
                sp.dma_start(T["uT"][:, :, bass.ds(BLK * n, BLK)], rowsT[:]).then_inc(uT_st, 16)

            def load(n, u, b):
                sp.wait_ge(mm, 4 * (n - 2) + 4)
                load_att(b, u)
                load_rden(b, u)
                sp.wait_ge(summed, n - 2 + 1 + 2)
                load_x(b, u)

            if second:
                blocks(sp, body)
            else:
                load(2, 0, 1)
                store_rows(0, 0)

                def behind(n, u, i):
                    load(n + 3, 1 - u, i + 1 + u)
                    store_base(n, u)
                    store_rows(n + 1, 1 - u)

                with sp.Fori(0, NBLK // 2 - 2) as i:
                    for u in range(2):
                        behind(2 * i + u, u, i)
                behind(NBLK - 4, 0, NBLK // 2 - 2)
                for n in range(NBLK - 3, NBLK):
                    store_base(n, n % 2)
                    if n + 1 < NBLK:
                        store_rows(n + 1, (n + 1) % 2)
            sp.wait_ge(final, 1)
            sp.dma_start(T[pre + "choice"], choice[:].rearrange("p t k -> p (t k)")).then_inc(consts, 16)
            if second:
                sp.dma_start(T["weights"], weights[:]).then_inc(consts, 16)
                sp.wait_ge(uT_st, 16 * (NBLK + 1))
            sp.wait_ge(consts, 16 * (NCONST + (2 if second else 1)))
            for u in range(2):
                sp.wait_ge(stored[u], 16 * (NBLK // 2 + 1))
                sp.wait_ge(rows_st[u], 16 * (NBLK // 2 + 1))

        @block.gpsimd
        def _(pool):
            g = nc.gpsimd
            pool.wait_ge(consts, 16 * NCONST)
            if second:
                def all_gathered(n):
                    pool.wait_ge(gathered[n % 2], 16 * SUB * (n // 2 + 1))
                    pool.sem_inc(in_moe, 1)

                for n in range(NBLK):
                    for j in range(SUB):
                        g.indirect_dma_start(
                            out=moe[:, SUB * n + j, :], out_offset=None, in_=T["a_y"],
                            in_offset=bass.IndirectOffsetOnAxis(ap=slots[:, SUB * n + j:SUB * n + j + 1], axis=0)
                        ).then_inc(gathered[n % 2], 16)
                    if n > 0:
                        all_gathered(n - 1)
                all_gathered(NBLK - 1)
                return

            def normalise(n, u, i):
                pool.wait_ge(in_att[u], 16 * 2 * (i + 1))
                pool.wait_ge(in_rden[u], 16 * 2 * KC * (i + 1))
                g.tensor_tensor(att[:, u, 1], att[:, u, 1], rden[:, u, 1], ALU.mult).then_inc(norm1, 1)

            def sums(n, u, i):
                pool.wait_ge(x2_done, 4 * n + 4 + 2)
                pool.wait_ge(base_ready, n + 1)
                g.tensor_tensor(sumx[:, u], x[:, u], x2[:, u], ALU.add).then_inc(summed, 1)

            def body(n, u, i, more):
                if more:
                    normalise(n + 2, u, i + 1)
                if more or u == 0:
                    sums(n + 1, 1 - u, i + u)

            for u in range(2):
                normalise(u, u, 0)
            sums(0, 0, 0)
            blocks(pool, body)

        @block.vector
        def _(dve_e):
            v = nc.vector
            for credit, count in ((base_ready, 2), (copied, 2), (x2_done, 2), (summed, 2), (turned_ev, 2),
                                  (lm, 1), (top_ready, 1), (uT_st, 16), (stored[0], 16), (stored[1], 16),
                                  (rows_st[0], 16), (rows_st[1], 16)):
                v.sem_inc(credit, count)
            dve_e.wait_ge(consts, 16 * NCONST)
            for kc in range(KC):
                v.tensor_scalar(gate[:, kc], gate[:, kc], gnorm[:, kc:kc + 1], None, ALU.mult).then_inc(scaled, 1)

            def normalise(n, u, i):
                dve_e.wait_ge(in_att[u], 16 * 2 * (i + 1))
                dve_e.wait_ge(in_rden[u], 16 * 2 * KC * (i + 1))
                v.tensor_tensor(att[:, u, 0], att[:, u, 0], rden[:, u, 0], ALU.mult).then_inc(norm0, 1)

            def sums_and_norm(n, u, i):
                if second:
                    dve_e.wait_ge(in_x[u], 16 * (i + 1))
                    dve_e.wait_ge(in_moe, n + 1)
                    dve_e.wait_ge(stored[u], 16 * (i + 1))
                    v.tensor_tensor(base[:, u], base_in[:, u], moe[:, bass.ds(SUB * n, SUB), :],
                                    ALU.add).then_inc(base_ready, 1)
                    dve_e.wait_ge(base_ready, n + 1 + 2)
                    src = base
                else:
                    dve_e.wait_ge(in_x[u], 32 * (i + 1))
                    dve_e.wait_ge(summed, n + 1)
                    for j in range(SUB):
                        dve_e.wait_ge(mm, 4 * n + j + 1)
                        v.tensor_tensor(x2[:, u, j], pM[:, 1, j % 2, 0:D], xn[:, u, j], ALU.add).then_inc(x2_done, 1)
                    dve_e.wait_ge(x2_done, 4 * n + 4 + 2)
                    src = x2
                step = Steps(dve_e, norms, n, 3 if second else 5)
                for j in range(SUB):
                    ins = v.bn_stats(stats[:, j], src[:, u, j])
                step(ins)
                v.memset(spare[:], 0.0)
                for j in range(SUB):
                    ins = v.bn_aggr(mv[:, j], stats[:, j])
                step(ins)
                if second:
                    v.tensor_scalar(rs[:, 0], mv[:, :, 1], LN_EPS, None, ALU.add).then_inc(var_ready, 1)
                else:
                    step(v.tensor_tensor(rs[:, 0], mv[:, :, 0], mv[:, :, 0], ALU.mult))
                    step(v.tensor_tensor(rs[:, 0], rs[:, 0], mv[:, :, 1], ALU.add))
                    v.tensor_scalar(rs[:, 0], rs[:, 0], RMS_EPS, None, ALU.add).then_inc(var_ready, 1)
                dve_e.wait_ge(root_ready, n + 1)
                step(v.reciprocal(rs[:, 2], rs[:, 1]))
                step.end()
                dve_e.wait_ge(rows_st[u], 16 * (i + 1))
                for j in range(SUB):
                    if second:
                        ins = v.tensor_scalar(rows[:, u, j], src[:, u, j], mv[:, j, 0:1], rs[:, 2, j:j + 1],
                                              ALU.subtract, ALU.mult)
                    else:
                        ins = v.tensor_scalar(rows[:, u, j], src[:, u, j], rs[:, 2, j:j + 1], None, ALU.mult)
                ins.then_inc(rows_ready, 1)

            def choose(n, u, i):
                if not second:
                    dve_e.wait_ge(summed, n + 1 + 2)
                    dve_e.wait_ge(copied, 4 * n + 4 + 2)
                    v.tensor_tensor(base[:, u], base[:, u], sumx[:, u], ALU.add).then_inc(base_ready, 1)
                step = Steps(dve_e, gates, n, 3)
                dve_e.wait_ge(lm, n + 1 + 1)
                step(v.tensor_tensor(logits[:], pL[:], gbias[:].unsqueeze(1).to_broadcast([P, SUB, 8]), ALU.add))
                v.memset(spare[:], 0.0)
                for j in range(SUB):
                    ins = v.max(top[:, j], logits[:, j])
                step(ins)
                v.memset(spare[:], 0.0)
                for j in range(SUB):
                    ins = v.max_index(topi[:, j], top[:, j], logits[:, j])
                step(ins)
                step.end()
                ins = v.tensor_copy(choice[:, bass.ds(SUB * n, SUB), :], topi[:, :, 0:K])
                if second:
                    ins = v.tensor_tensor(gap[:, bass.ds(SUB * n, SUB)], top[:, :, 1], top[:, :, 0], ALU.subtract)
                ins.then_inc(top_ready, 1)

            def body(n, u, i, more):
                if more or u == 0:
                    sums_and_norm(n + 1, 1 - u, i + u)
                if more and not second:
                    normalise(n + 2, u, i + 1)
                choose(n, u, i)

            if not second:
                for u in range(2):
                    normalise(u, u, 0)
            sums_and_norm(0, 0, 0)
            blocks(dve_e, body)
            dve_e.wait_ge(top_ready, NBLK + 1)
            if second:
                step = Steps(dve_e, last_steps)
                dve_e.wait_ge(exp_out, 1)
                step(v.tensor_scalar(gap[:], weights[:, 1], 1.0, None, ALU.add))
                step(v.reciprocal(weights[:, 0], gap[:]))
                v.tensor_tensor(weights[:, 1], weights[:, 1], weights[:, 0], ALU.mult).then_inc(final, 1)
            else:
                v.sem_inc(final, 1)

        @block.scalar
        def _(act):
            a = nc.scalar
            if second:
                experts.load(act)

            def copies(n, u, i, tiles):
                if second:
                    return
                act.wait_ge(stored[u], 16 * (i + 1))
                for j in tiles:
                    act.wait_ge(mm, 4 * n + j + 1)
                    a.activation(base[:, u, j], pM[:, 0, j % 2, 0:D], ACT.Copy).then_inc(copied, 1)

            def root(n):
                act.wait_ge(var_ready, n + 1)
                a.activation(rs[:, 1], rs[:, 0], ACT.Sqrt).then_inc(root_ready, 1)

            def turned_out(n):
                act.wait_ge(lm, n + 1)
                if second:
                    act.wait_ge(uT_st, 16 * (n + 1))
                for kc in range(KC):
                    act.wait_ge(turned, 2 * n + kc + 1)
                    a.activation(rowsT[:, kc], pT[:, kc], ACT.Copy).then_inc(turned_ev, 1)

            def body(n, u, i, more):
                if more or u == 0:
                    copies(n + 1, 1 - u, i + u, (0, 1))
                turned_out(n)
                if more or u == 0:
                    copies(n + 1, 1 - u, i + u, (2, 3))
                    root(n + 1)

            copies(0, 0, 0, range(SUB))
            root(0)
            blocks(act, body)
            if second:
                act.wait_ge(top_ready, NBLK + 1)
                a.activation(weights[:, 1], gap[:], ACT.Exp).then_inc(exp_out, 1)

        @block.tensor
        def _(pe):
            t = nc.tensor
            pe.wait_ge(consts, 16 * NCONST)
            pe.wait_ge(scaled, 2)

            def products(n, u, tiles):
                if second:
                    return
                pe.wait_ge(norm0, n + 1)
                pe.wait_ge(norm1, n + 1)
                for j in tiles:
                    pe.wait_ge(x2_done, 4 * n + j + 1)
                    pe.wait_ge(copied, 4 * n + j + 1)
                    for at in (1, 0):
                        for kc in range(KC):
                            ins = t.matmul(pM[:, at, j % 2, 0:D], att[:, u, at, kc, P * j:P * j + P],
                                           wo[:, at, kc], start=kc == 0, stop=kc == KC - 1)
                    ins.then_inc(mm, 1)

            def turn(n, u):
                pe.wait_ge(rows_ready, n + 1)
                for kc in range(KC):
                    pe.wait_ge(turned_ev, 2 * n + kc + 1)
                    for j in range(SUB):
                        ins = t.transpose(pT[:, kc, P * j:P * j + P], rows[:, u, j, P * kc:P * kc + P], ident[:])
                    ins.then_inc(turned, 1)

            def gate_products(n):
                pe.wait_ge(turned_ev, 2 * n + 2 + 2)
                pe.wait_ge(top_ready, n + 1)
                for j in range(SUB):
                    for kc in range(KC):
                        ins = t.matmul(pL[:, j], rowsT[:, kc, P * j:P * j + P], gate[:, kc],
                                       start=kc == 0, stop=kc == KC - 1)
                ins.then_inc(lm, 1)

            def body(n, u, i, more):
                if more or u == 0:
                    products(n + 1, 1 - u, (0, 1))
                turn(n, u)
                if more or u == 0:
                    products(n + 1, 1 - u, (2, 3))
                gate_products(n)

            products(0, 0, range(SUB))
            blocks(pe, body)


def scan_inputs_phase(nc, T):
    NBLK = TOK // BLK
    CHUNK = 4
    NCHUNK = TILES // CHUNK
    with ExitStack() as ctx:
        sb = lambda n, s, d=F32: ctx.enter_context(nc.sbuf_tensor("si_" + n, s, d))
        ps = lambda n, s, d=F32: ctx.enter_context(nc.psum_tensor("si_" + n, s, d))
        sem = ctx.enter_context(Semaphores(nc, "si_"))
        w_x = sb("w_x", [P, KC, RANK + 2 * NS])
        w_dt = sb("w_dt", [RANK, KC, P])
        b_dt = sb("b_dt", [P, KC])
        slots = sb("slots", [P, TILES * K1], I32)
        rows = sb("rows", [P, 2, CHUNK, D])
        uT = sb("uT", [P, 2, KC, BLK])
        dtr = sb("dtr", [RANK, 2, BLK])
        bc = sb("bc", [2 * NS, 2, BLK])
        z = sb("z", [P, 2, KC, BLK])
        ez = sb("ez", [P, 2, KC, BLK])
        wz = sb("wz", [P, 2, KC, BLK])
        dt = sb("dt", [P, 2, KC, BLK])
        dtu = sb("dtu", [P, 2, KC, BLK])
        pR = ps("pR", [RANK, 2, BLK])
        pB = ps("pB", [2 * NS, 2, BLK])
        pZ = ps("pZ", [P, 2, KC, BLK])
        consts, dve = sem("consts"), sem("dve")
        u_in = [sem("u_in0"), sem("u_in1")]
        rows_in = [sem("rows_in0"), sem("rows_in1")]
        out = [sem("out0"), sem("out1")]
        rows_mm, dtr_ev, bc_ev, dt_mm, z_done, exp_done, w_done, ln_done, used = (sem(n) for n in (
            "rows_mm", "dtr_ev", "bc_ev", "dt_mm", "z", "exp", "w", "ln", "used"))
        absd = sem("abs")
        sent, chunk_sent = [sem("sent0"), sem("sent1")], sem("chunk_sent")
        block = ctx.enter_context(nc.Block())

        @block.sync
        def _(sp):
            for dst, src in ((w_x, "w_x"), (w_dt, "w_dt"), (b_dt, "b_dt"), (slots, "b_slots")):
                sp.dma_start(dst[:], T[src]).then_inc(consts, 16)

            def rows_load(n):
                sp.dma_start(rows[:, n % 2], T["b_rows"][:, CHUNK * n:CHUNK * n + CHUNK, :]
                             ).then_inc(rows_in[n % 2], 16)

            for u in range(2):
                sp.dma_start(uT[:, u], T["uT"][:, :, BLK * u:BLK * u + BLK]).then_inc(u_in[u], 16)
                rows_load(u)

            def turn(i, last):
                for u in range(2):
                    n = 2 * i + u
                    sp.wait_ge(bc_ev, n + 1 + 2)
                    sp.dma_start(T["bc"][n].rearrange("n c t -> c n t"), bc[:, u]).then_inc(out[u], 16)
                    sp.wait_ge(used, n + 1 + 2)
                    sp.dma_start(T["dt"][n], dt[:, u]).then_inc(out[u], 16)
                    sp.dma_start(T["dtu"][n], dtu[:, u]).then_inc(out[u], 16)
                    if not last:
                        sp.dma_start(uT[:, u], T["uT"][:, :, bass.ds(BLK * n + 2 * BLK, BLK)]
                                     ).then_inc(u_in[u], 16)
                        sp.wait_ge(chunk_sent, n + 1)
                        sp.dma_start(rows[:, u], T["b_rows"][:, bass.ds(CHUNK * n + 2 * CHUNK, CHUNK), :]
                                     ).then_inc(rows_in[u], 16)

            with sp.Fori(0, NBLK // 2 - 1) as i:
                turn(i, False)
            turn(NBLK // 2 - 1, True)
            for u in range(2):
                sp.wait_ge(out[u], 48 * (NBLK // 2 + 1))

        @block.gpsimd
        def _(pool):
            def all_sent(n):
                pool.wait_ge(sent[n % 2], 16 * CHUNK * K1 * (n // 2 + 1))
                pool.sem_inc(chunk_sent, 1)

            pool.wait_ge(consts, 16 * 4)
            for n in range(NCHUNK):
                pool.wait_ge(rows_in[n % 2], 16 * (n // 2 + 1))
                for c in range(CHUNK * K1):
                    at = CHUNK * K1 * n + c
                    nc.gpsimd.indirect_dma_start(
                        out=T["b_sorted"], out_offset=bass.IndirectOffsetOnAxis(ap=slots[:, at:at + 1], axis=0),
                        in_=rows[:, n % 2, c // K1, :], in_offset=None).then_inc(sent[n % 2], 16)
                if n > 0:
                    all_sent(n - 1)
            all_sent(NCHUNK - 1)

        @block.tensor
        def _(pe):
            t = nc.tensor
            pe.wait_ge(consts, 16 * 4)
            with pe.Fori(0, NBLK // 2) as i:
                for u in range(2):
                    n = 2 * i + u
                    pe.wait_ge(u_in[u], 16 * (i + 1))
                    pe.wait_ge(dtr_ev, n + 1)
                    pe.wait_ge(bc_ev, n + 1)
                    for kc in range(KC):
                        t.matmul(pR[:, u], w_x[:, kc, 0:RANK], uT[:, u, kc], start=kc == 0, stop=kc == KC - 1)
                    for kc in range(KC):
                        ins = t.matmul(pB[:, u], w_x[:, kc, RANK:], uT[:, u, kc], start=kc == 0, stop=kc == KC - 1)
                    ins.then_inc(rows_mm, 1)
                    pe.wait_ge(dtr_ev, n + 1 + 2)
                    pe.wait_ge(z_done, n + 1)
                    for kc in range(KC):
                        ins = t.matmul(pZ[:, u, kc], w_dt[:, kc], dtr[:, u], start=True, stop=True)
                    ins.then_inc(dt_mm, 1)

        @block.scalar
        def _(act):
            a = nc.scalar

            def rows_out(n, u, i):
                act.wait_ge(rows_mm, n + 1)
                a.activation(dtr[:, u], pR[:, u], ACT.Copy).then_inc(dtr_ev, 1)
                act.wait_ge(out[u], 48 * (i + 1))
                a.activation(bc[:, u], pB[:, u], ACT.Copy).then_inc(bc_ev, 1)

            def exponential(n, u):
                act.wait_ge(dt_mm, n + 1)
                act.wait_ge(used, n + 1)
                for kc in range(KC):
                    ins = a.activation(z[:, u, kc], pZ[:, u, kc], ACT.Identity, bias=b_dt[:, kc:kc + 1])
                ins.then_inc(z_done, 1)
                act.wait_ge(z_done, n + 1 + 2)
                a.activation(ez[:, u], z[:, u], ACT.Abs).then_inc(absd, 1)
                act.wait_ge(absd, n + 1)
                a.activation(ez[:, u], ez[:, u], ACT.Exp, scale=-1.0).then_inc(exp_done, 1)

            def logarithm(n, u):
                act.wait_ge(w_done, n + 1)
                a.activation(dt[:, u], wz[:, u], ACT.Ln).then_inc(ln_done, 1)

            act.wait_ge(consts, 16 * 4)
            rows_out(0, 0, 0)
            exponential(0, 0)
            with act.Fori(0, NBLK // 2 - 1) as i:
                for u in range(2):
                    n = 2 * i + u
                    rows_out(n + 1, 1 - u, i + u)
                    logarithm(n, u)
                    exponential(n + 1, 1 - u)
            rows_out(NBLK - 1, 1, NBLK // 2 - 1)
            logarithm(NBLK - 2, 0)
            exponential(NBLK - 1, 1)
            logarithm(NBLK - 1, 1)

        @block.vector
        def _(dve_e):
            v = nc.vector
            for credit, count in ((out[0], 48), (out[1], 48), (dtr_ev, 2), (bc_ev, 2), (z_done, 2), (used, 2)):
                v.sem_inc(credit, count)
            dve_e.wait_ge(consts, 16 * 4)
            with dve_e.Fori(0, NBLK // 2) as i:
                step = Steps(dve_e, dve, i, 2 * 4)
                for u in range(2):
                    n = 2 * i + u
                    dve_e.wait_ge(exp_done, n + 1)
                    dve_e.wait_ge(out[u], 48 * (i + 1))
                    step(v.tensor_scalar(wz[:, u], ez[:, u], 1.0, None, ALU.add))
                    v.sem_inc(w_done, 1)
                    v.tensor_scalar(z[:, u], z[:, u], 0.0, None, ALU.max)
                    step(v.scalar_tensor_tensor(ez[:, u], wz[:, u], -1.0, ez[:, u], ALU.add, ALU.subtract))
                    step(v.tensor_tensor(z[:, u], z[:, u], ez[:, u], ALU.subtract))
                    dve_e.wait_ge(ln_done, n + 1)
                    step(v.tensor_tensor(dt[:, u], dt[:, u], z[:, u], ALU.add))
                    v.tensor_tensor(dtu[:, u], dt[:, u], uT[:, u], ALU.mult).then_inc(used, 1)
                step.end()


def experts_and_scan_phase(nc, T, weights):
    NBUF = 4
    HALVES = SEQ // BLK
    with ExitStack() as ctx:
        sb = lambda n, s, d=F32: ctx.enter_context(nc.sbuf_tensor("es_" + n, s, d))
        sem = ctx.enter_context(Semaphores(nc, "es_"))
        tiles = ExpertTiles(nc, ctx, sem, T, E1, K1, "b_", weights, ACT.Gelu)
        TPT = tiles.NT // BATCH
        SPT = HALVES * NS
        assert TPT * BATCH == tiles.NT and TPT % 2 == 0
        a_log = sb("a_log", [P, KC, NS])
        a_neg = sb("a_neg", [P, KC, NS])
        dt = sb("dt", [P, KC, BLK])
        dtu = sb("dtu", [P, HALVES, KC, BLK])
        bc = sb("bc", [P, NBUF, 2, BLK])
        decay = sb("decay", [P, 2, KC, BLK])
        state = sb("state", [P, 4, KC, BLK])
        carry = sb("carry", [P, NS, KC])
        y = sb("y", [P, HALVES, KC, BLK])
        d_par = sb("d_par", [P, KC])
        d_in, skipped = sem("d_in"), sem("skipped")
        a_in, a_exp, a_ready, zeroed = sem("a_in"), sem("a_exp"), sem("a_ready"), sem("zeroed")
        bc_in = [sem(f"bc_in{q}") for q in range(NBUF)]
        dt_in = sem("dt_in")
        dtu_in = [sem(f"dtu_in{q}") for q in range(HALVES)]
        y_in = [sem(f"y_in{q}") for q in range(HALVES)]
        y_st = [sem(f"y_st{q}") for q in range(HALVES)]
        dbu_done, decayed, scanned, carried, weighed, summed = (sem(n) for n in (
            "dbu", "decayed", "scanned", "carried", "weighed", "summed"))
        block = ctx.enter_context(nc.Block())

        def spread(count, slots):
            return lambda k: range(count * k // slots, count * (k + 1) // slots)

        @block.sync
        def _(sp):
            sp.dma_start(a_log[:], T["a_log"]).then_inc(a_in, 16)
            sp.dma_start(d_par[:], T["d_par"]).then_inc(d_in, 16)
            tiles.load_tables(sp)
            rows = T["bc"].rearrange("b n c t -> (b n) c t")
            inputs = T["uT"].rearrange("p k (n t) -> n p k t", t=BLK)

            def load_bc(step, q):
                sp.dma_start(bc[:, q], rows[step].unsqueeze(0).to_broadcast([P, 2, BLK])).then_inc(bc_in[q], 16)

            sp.dma_start(dt[:], T["dt"][0]).then_inc(dt_in, 16)
            for h in range(HALVES):
                sp.dma_start(dtu[:, h], T["dtu"][h]).then_inc(dtu_in[h], 16)
                sp.dma_start(y[:, h], inputs[h]).then_inc(y_in[h], 16)
            for q in range(NBUF):
                load_bc(q, q)
            tiles.load_rows(sp, 0, 0)
            after = spread(TPT, SPT)

            def turn(b, last):
                for s in range(SPT):
                    for j in after(s):
                        if not (last and j + 3 >= TPT):
                            tiles.load_rows(sp, TPT * b + j + 1, (j + 1) % 2)
                        if j > 0:
                            tiles.store_result(sp, TPT * b + j - 1, (j - 1) % 2)
                    if not (last and s + NBUF >= SPT):
                        sp.wait_ge(weighed, SPT * b + s + 1)
                        load_bc(SPT * b + s + NBUF, s % NBUF)
                    if s % NS == NS - 3 and not (last and s > NS):
                        sp.wait_ge(decayed, SPT * b + s + 3)
                        sp.dma_start(dt[:], T["dt"][HALVES * b + s // NS + 1]).then_inc(dt_in, 16)
                    if s == NS + 3:
                        finish(b, 0, last)
                tiles.store_result(sp, TPT * b + TPT - 1, 1)
                finish(b, 1, last)

            def finish(b, h, last):
                sp.wait_ge(summed, SPT * b + NS * (h + 1) + 4)
                sp.dma_start(T["y_t"][HALVES * b + h], y[:, h]).then_inc(y_st[h], 16)
                if not last:
                    sp.dma_start(dtu[:, h], T["dtu"][HALVES * b + h + HALVES]).then_inc(dtu_in[h], 16)
                    sp.wait_ge(y_st[h], 16 * (b + 1))
                    sp.dma_start(y[:, h], inputs[HALVES * b + h + HALVES]).then_inc(y_in[h], 16)

            with sp.Fori(0, BATCH - 1) as b:
                turn(b, False)
            turn(BATCH - 1, True)
            for h in range(HALVES):
                sp.wait_ge(y_st[h], 16 * BATCH)
            tiles.stored(sp)

        @block.vector
        def _(dve_e):
            v = nc.vector
            v.sem_inc(summed, 4)
            v.sem_inc(scanned, 2)
            dve_e.wait_ge(a_exp, 1)
            v.tensor_scalar(a_neg[:], a_neg[:], -1.0, None, ALU.mult).then_inc(a_ready, 1)
            tiles.prepare(dve_e)

            def inputs(S, s, b):
                h = s // NS
                if s % NS == 0:
                    dve_e.wait_ge(dtu_in[h], 16 * (b + 1))
                dve_e.wait_ge(bc_in[s % NBUF], 16 * (SPT // NBUF * b + s // NBUF + 1))
                dve_e.wait_ge(summed, S + 1)
                v.tensor_tensor(state[:, s % 4], dtu[:, h],
                                bc[:, s % NBUF, 0].unsqueeze(1).to_broadcast([P, KC, BLK]),
                                ALU.mult).then_inc(dbu_done, 1)

            def scan(b, s):
                S = SPT * b + s
                dve_e.wait_ge(dbu_done, S + 1)
                dve_e.wait_ge(decayed, S + 1)
                if s % NS == 0:
                    dve_e.wait_ge(zeroed, HALVES * b + s // NS + 1)
                for kc in range(KC):
                    ins = v.tensor_tensor_scan(state[:, s % 4, kc], decay[:, s % 2, kc], state[:, s % 4, kc],
                                               carry[:, s % NS, kc:kc + 1], ALU.mult, ALU.add)
                ins.then_inc(scanned, 1)

            def weigh(b, s):
                S = SPT * b + s
                dve_e.wait_ge(scanned, S + 1 + 2)
                if s < NS:
                    ins = v.tensor_copy(carry[:, s], state[:, s % 4, :, BLK - 1])
                    ins.then_inc(carried, 1)
                    dve_e.wait_ge(carried, NS * b + s + 1)
                v.tensor_tensor(state[:, s % 4], state[:, s % 4],
                                bc[:, s % NBUF, 1].unsqueeze(1).to_broadcast([P, KC, BLK]),
                                ALU.mult).then_inc(weighed, 1)

            after = spread(3 * TPT, 3 * SPT)

            def copies(b, part, last):
                for c in after(part):
                    j, which = c // 3, c % 3
                    if which == 0:
                        tiles.hidden_turned(dve_e, TPT * b + j)
                    elif which == 1 and not (last and j + 2 >= TPT):
                        tiles.rows_turned(dve_e, TPT * b + j + 2)
                    elif which == 2:
                        tiles.result(dve_e, TPT * b + j, j % 2, TPT // 2 * b + j // 2)

            def turn(b, last):
                for s in range(SPT):
                    scan(b, s)
                    copies(b, 3 * s, last)
                    if not (last and s == SPT - 1):
                        inputs(SPT * b + s + 1, (s + 1) % SPT, b + (s + 1) // SPT)
                    copies(b, 3 * s + 1, last)
                    weigh(b, s)
                    if s == NS - 1:
                        v.sem_inc(zeroed, 1)
                    if s == SPT - 1:
                        v.memset(carry[:], 0.0).then_inc(zeroed, 1)
                    copies(b, 3 * s + 2, last)

            v.memset(carry[:], 0.0).then_inc(zeroed, 1)
            inputs(0, 0, 0)
            for n in range(2):
                tiles.rows_turned(dve_e, n)
            with dve_e.Fori(0, BATCH - 1) as b:
                turn(b, False)
            turn(BATCH - 1, True)

        @block.scalar
        def _(act):
            a = nc.scalar
            act.wait_ge(a_in, 16)
            a.activation(a_neg[:], a_log[:], ACT.Exp).then_inc(a_exp, 1)
            act.wait_ge(a_ready, 1)
            after = spread(TPT, SPT)

            with act.Fori(0, BATCH) as b:
                for s in range(SPT):
                    h = s // NS
                    if s % NS == 0:
                        act.wait_ge(dt_in, 16 * (HALVES * b + h + 1))
                    act.wait_ge(scanned, SPT * b + s + 1)
                    for j in after(s):
                        tiles.gate(act, TPT * b + j)
                    for kc in range(KC):
                        ins = a.activation(decay[:, s % 2, kc], dt[:, kc], ACT.Exp,
                                           scale=a_neg[:, kc, s % NS:s % NS + 1])
                    ins.then_inc(decayed, 1)

        @block.gpsimd
        def _(pool):
            pool.wait_ge(d_in, 16)
            with pool.Fori(0, BATCH) as b:
                for s in range(SPT):
                    h = s // NS
                    if s % NS == 0:
                        pool.wait_ge(y_in[h], 16 * (b + 1))
                        nc.gpsimd.tensor_tensor(y[:, h], y[:, h], d_par[:].unsqueeze(2).to_broadcast(
                            [P, KC, BLK]), ALU.mult).then_inc(skipped, 1)
                        pool.wait_ge(skipped, HALVES * b + h + 1)
                    pool.wait_ge(weighed, SPT * b + s + 1)
                    pool.wait_ge(summed, SPT * b + s + 4)
                    nc.gpsimd.tensor_tensor(y[:, h], y[:, h], state[:, s % 4], ALU.add).then_inc(summed, 1)

        @block.tensor
        def _(pe):
            tiles.products(pe, False)


def final_phase(nc, T):
    with ExitStack() as ctx:
        sb = lambda n, s, d=F32: ctx.enter_context(nc.sbuf_tensor("fi_" + n, s, d))
        sem = ctx.enter_context(Semaphores(nc, "fi_"))
        ident = sb("ident", [P, P])
        slots = sb("slots", [P, TILES * K1], I32)
        weights = sb("weights", [P, K1, TILES])
        res = sb("res", [P, 2, SUB, D])
        yT = sb("yT", [P, 2, KC, BLK])
        ex = sb("ex", [P, 4, SUB, K1, D])
        out = sb("out", [P, 2, SUB, D])
        pY = ctx.enter_context(nc.psum_tensor("fi_pY", [P, 2, SUB, D], F32))
        consts, dve, done = sem("consts"), sem("dve"), sem("done")
        gathered = [sem("gathered0"), sem("gathered1")]
        r_in = [sem("r_in0"), sem("r_in1")]
        stored = [sem("stored0"), sem("stored1")]
        g_done, turned, read = sem("g_done"), sem("turned"), sem("read")
        NBLK = TOK // BLK
        block = ctx.enter_context(nc.Block())

        @block.sync
        def _(sp):
            sp.dma_start(slots[:], T["b_slots"]).then_inc(consts, 16)
            sp.dma_start(weights[:], T["weights"]).then_inc(consts, 16)
            sp.dma_start(ident[:], T["ident"]).then_inc(consts, 16)
            for n in range(NBLK):
                u = n % 2
                if n >= 2:
                    sp.wait_ge(done, n - 1)
                sp.dma_start(res[:, u], T["res"][:, SUB * n:SUB * n + SUB, :]).then_inc(r_in[u], 16)
                sp.dma_start(yT[:, u], T["y_t"][n]).then_inc(r_in[u], 16)
                if n >= 1:
                    sp.wait_ge(done, n)
                    sp.dma_start(T["out"][:, SUB * (n - 1):SUB * n, :], out[:, 1 - u]).then_inc(stored[1 - u], 16)
            sp.wait_ge(done, NBLK)
            sp.dma_start(T["out"][:, SUB * (NBLK - 1):, :], out[:, 1]).then_inc(stored[1], 16)
            for u in range(2):
                sp.wait_ge(stored[u], 16 * NBLK // 2)

        @block.gpsimd
        def _(pool):
            def all_gathered(n):
                pool.wait_ge(gathered[n % 2], 16 * SUB * K1 * (n // 2 + 1))
                pool.sem_inc(g_done, 1)

            pool.wait_ge(consts, 48)
            for n in range(NBLK):
                if n >= 4:
                    pool.wait_ge(done, n - 3)
                for j in range(SUB):
                    for k in range(K1):
                        c = K1 * (SUB * n + j) + k
                        nc.gpsimd.indirect_dma_start(
                            out=ex[:, n % 4, j, k, :], out_offset=None, in_=T["b_y"],
                            in_offset=bass.IndirectOffsetOnAxis(ap=slots[:, c:c + 1], axis=0)
                        ).then_inc(gathered[n % 2], 16)
                if n >= 1:
                    all_gathered(n - 1)
            all_gathered(NBLK - 1)

        @block.tensor
        def _(pe):
            pe.wait_ge(consts, 48)
            for n in range(NBLK):
                u = n % 2
                pe.wait_ge(r_in[u], 32 * (n // 2 + 1))
                if n >= 2:
                    pe.wait_ge(read, n - 1)
                for j in range(SUB):
                    for kc in range(KC):
                        ins = nc.tensor.transpose(pY[:, u, j, P * kc:P * kc + P], yT[:, u, kc, P * j:P * j + P],
                                                  ident[:])
                ins.then_inc(turned, 1)

        @block.vector
        def _(dve_e):
            v = nc.vector
            step = Steps(dve_e, dve)
            dve_e.wait_ge(consts, 48)
            for n in range(NBLK):
                u = n % 2
                dve_e.wait_ge(r_in[u], 32 * (n // 2 + 1))
                dve_e.wait_ge(turned, n + 1)
                if n >= 2:
                    dve_e.wait_ge(stored[u], 16 * (n // 2))
                step(v.tensor_tensor(out[:, u], res[:, u], pY[:, u], ALU.add))
                v.sem_inc(read, 1)
                dve_e.wait_ge(g_done, n + 1)
                for k in range(K1):
                    for j in range(SUB):
                        ins = v.scalar_tensor_tensor(out[:, u, j], ex[:, n % 4, j, k], weights[:, k, SUB * n + j:
                                                     SUB * n + j + 1], out[:, u, j], ALU.mult, ALU.add)
                    if k < K1 - 1:
                        step(ins)
                ins.then_inc(done, 1)


def shape_constants():
    half = HD // 2
    freq = (np.float32(1.0) / np.float32(10000.0) ** (np.arange(half, dtype=np.float32) / np.float32(half)))
    angle = np.arange(SEQ, dtype=np.float32)[None, :] * freq.astype(np.float32)[:, None]
    row = np.arange(P) % HD
    cos = np.cos(angle)[row % half]
    sin = np.sin(angle)[row % half] * np.where(row < half, -1, 1)[:, None]
    later = np.where(np.arange(P)[None, :] > np.arange(P)[:, None], np.float32(MASKED), np.float32(0))
    count = np.arange(P, dtype=np.float32)
    pick = lambda e: np.repeat(np.eye(e, dtype=np.float32), PARTS, 0)
    return {"a_pick": pick(E0), "b_pick": pick(E1),
            "before": (count[:, None] < count[None, :]).astype(np.float32),
            "ones": np.ones((P, P), np.float32), "iota": np.tile(count, (P, 1)),
            "masks": np.ascontiguousarray(np.stack([np.eye(P, dtype=np.float32), later, later.T], 1)),
            "ident": np.eye(P, dtype=np.float32), "cos": cos.astype(np.float32), "sin": sin.astype(np.float32)}


def k_major(w):
    w = np.asarray(w)
    return np.ascontiguousarray(w.T.reshape(-1, P, w.shape[0]).transpose(1, 0, 2))


def layouts(a):
    a = {k: np.asarray(v) for k, v in a.items()}
    out = dict(shape_constants())
    out["x"] = np.ascontiguousarray(a["L0_attn_x"].reshape(BATCH, NQT, P, D).transpose(0, 2, 1, 3))
    wqkv = a["L0_attn_w_qkv"]
    out["w_qk"] = k_major(wqkv[:2 * D]).reshape(P, KC, 4, P)
    out["w_v"] = k_major(wqkv[2 * D:])
    out["m_q"] = k_major(a["L0_ffn_Wq"]).reshape(P, KC, 2, P)
    out["m_dkv"] = k_major(a["L0_ffn_Wdkv"])
    out["m_k"] = k_major(a["L0_ffn_Wuk"]).reshape(P, 2, P)
    out["m_v"] = np.ascontiguousarray(a["L0_ffn_Wuv"].T)
    out["norm1"] = np.ascontiguousarray(a["L0_ffn_norm1_w"].reshape(KC, P).T)
    out["lng"] = np.ascontiguousarray(np.stack([a["L0_ffn_ln_g"], a["L0_ffn_ln_b"]], 1))
    out["a_w1"] = experts_in(a["L0_ffn_W1"].transpose(0, 2, 1))
    out["a_w2"] = experts_in(a["L0_ffn_W2"].transpose(0, 2, 1))
    out["a_bias"] = np.concatenate([a["L0_ffn_b1"], a["L0_ffn_b2"]], 1)
    out["a_wnorm"] = np.ascontiguousarray(a["L0_ffn_norm2_w"].reshape(KC, P).T)
    out["b_w1"] = experts_in(a["L1_ffn_w1"])
    out["b_w2"] = experts_in(a["L1_ffn_w2"])
    out["b_bias"] = np.concatenate([a["L1_ffn_b1"], a["L1_ffn_b2"]], 1)
    out["b_wnorm"] = np.ones((P, KC), np.float32)
    out["wo"] = np.ascontiguousarray(np.stack([k_major(a["L0_attn_w_out"]), k_major(a["L0_ffn_Wo"])], 1))
    for pre, gw, gb in (("a_", "L0_ffn_gate_w", "L0_ffn_gate_b"), ("b_", "L1_ffn_gate_w", "L1_ffn_gate_b")):
        e = a[gw].shape[0]
        gate = np.zeros((P, KC, 8), np.float32)
        gate[:, :, :e] = k_major(a[gw])
        bias = np.full((P, 8), -3.0e38, np.float32)
        bias[:, :e] = a[gb][None]
        out[pre + "gate"], out[pre + "gbias"] = gate, bias
    out["a_gnorm"], out["b_gnorm"] = out["a_wnorm"], out["b_wnorm"]
    out["w_x"] = k_major(a["L1_attn_W_x"])
    out["w_dt"] = np.ascontiguousarray(a["L1_attn_W_dt"].T.reshape(-1, KC, P))
    out["b_dt"] = np.ascontiguousarray(a["L1_attn_b_dt"].reshape(KC, P).T)
    out["d_par"] = np.ascontiguousarray(a["L1_attn_D_param"].reshape(KC, P).T)
    out["a_log"] = np.ascontiguousarray(a["L1_attn_A_log"].reshape(KC, P, -1).transpose(1, 0, 2))
    return out


def experts_in(w):
    e, k, n = w.shape
    return np.ascontiguousarray(w.reshape(e, k // P, P, n).transpose(0, 2, 1, 3))


def expert_scratch(pre, experts, per_token):
    rows = P * expert_tiles(experts, per_token)
    return {
        pre + "choice": ((P, TILES * per_token), F32),
        pre + "rows": ((P, TILES, D), F32),
        pre + "sorted": ((rows, D), F32),
        pre + "y": ((rows, D), F32),
        pre + "slots": ((P, TILES * per_token), I32),
        pre + "tile_expert": ((1, rows // P), I32),
        pre + "bparts": ((experts, PARTS, 5 * D), BF16),
    }


SCRATCH = {
    "rden": ((GROUPS, HPG, SEQ), F32),
    "base": ((P, TILES, D), F32),
    "res": ((P, TILES, D), F32),
    "uT": ((P, KC, TOK), F32),
    "bc": ((TOK // BLK, NS, 2, BLK), F32),
    "dt": ((TOK // BLK, P, KC, BLK), F32),
    "dtu": ((TOK // BLK, P, KC, BLK), F32),
    "y_t": ((TOK // BLK, P, KC, BLK), F32),
    "weights": ((P, K1, TILES), F32),
    **expert_scratch("a_", E0, K0),
    **expert_scratch("b_", E1, K1),
    "xn": ((BATCH, P, NQT, D), F32),
    "qk_parts": ((2 * BATCH, HG, 2, PARTS, HPG * HD, SEQ), BF16),
    "m_rows": ((GROUPS, MROWS, HPG * SEQ), BF16),
    "att": ((2 * BATCH, KC, P, SEQ), F32),
    "sums": ((GROUPS, HPG, SEQ), F32),
    "v_pad": ((2 * BATCH, HG, SEQ, HPG * VW), F32),
}


INPUTS = ("x", "ident", "cos", "sin", "w_qk", "w_v", "m_q", "m_dkv", "m_k", "m_v", "norm1", "lng", "masks",
          "before", "ones", "iota", "a_w1", "a_w2", "a_bias", "a_wnorm", "b_w1", "b_w2",
          "b_bias", "b_wnorm", "wo", "a_gate", "a_gbias", "a_gnorm", "b_gate", "b_gbias", "b_gnorm", "w_x",
          "w_dt", "b_dt", "d_par", "a_log", "a_pick", "b_pick")


def build_program(nc, T):
    bias_parts_phase(nc, T)
    project_phase(nc, T)
    with ExitStack() as held:
        weights = ExpertWeights(nc, held, T, E0, "a_")
        attention_phase(nc, T, weights)
        denominators_phase(nc, T)
        mix_phase(nc, T, False)
        route_phase(nc, T, E0, K0, "a_", True)
        experts_phase(nc, T, E0, K0, "a_", ACT.Relu, weights)
    with ExitStack() as held:
        weights = ExpertWeights(nc, held, T, E1, "b_")
        mix_phase(nc, T, True, weights)
        route_phase(nc, T, E1, K1, "b_", False)
        scan_inputs_phase(nc, T)
        experts_and_scan_phase(nc, T, weights)
    final_phase(nc, T)


def kernel(**inputs):
    import concourse.bacc as bacc
    from concourse.bass_utils import run_bass_kernel_spmd

    nc = bacc.Bacc("TRN2", target_bir_lowering=False, num_devices=1)
    laid = layouts(inputs)
    arrays, T = {}, {}
    for name in INPUTS:
        a = np.ascontiguousarray(laid[name])
        arrays["in_" + name] = a
        T[name] = nc.dram_tensor("in_" + name, a.shape, mybir.dt.from_np(a.dtype), kind="ExternalInput").ap()
    for name, (shape, dtype) in SCRATCH.items():
        T[name] = nc.dram_tensor("scratch_" + name, shape, dtype).ap()
    T["out"] = nc.dram_tensor("out", (P, TILES, D), F32, kind="ExternalOutput").ap()
    build_program(nc, T)
    r = run_bass_kernel_spmd(nc, [arrays], core_ids=[0])
    out = r.results[0]["out"]
    return np.ascontiguousarray(out.transpose(1, 0, 2)).reshape(BATCH, SEQ, D)
```
